# Optimizing a Trainium2 kernel written in Bass

```python
import numpy as np
import jax
import jax.numpy as jnp

def _softmax(x, axis=-1):
    return jax.nn.softmax(x, axis=axis)

def _gelu(x):
    return jax.nn.gelu(x, approximate=True)

def _silu(x):
    return jax.nn.silu(x)

def _sigmoid(x):
    return jax.nn.sigmoid(x)

def _layernorm(x, axis=-1, eps=1e-05):
    m = jnp.mean(x, axis=axis, keepdims=True)
    v = jnp.var(x, axis=axis, keepdims=True)
    return (x - m) / jnp.sqrt(v + eps)

def _scatter_add(tgt, idx, src, axis=0):
    return tgt.at[idx].add(src)

def _segment_sum(src, seg, n):
    return jax.ops.segment_sum(src, seg, n)
kernel_name = 'mk_gps_d1_gnn_r8_d0a8af'

def setup_inputs(seed: int=0):
    np.random.seed(seed)
    _w = jnp.asarray

    def _rec_inputs():
        import jax
        import jax.numpy as jnp
        _gk = jax.random.key(seed)
        x = -0.0003713 + 1 * jax.random.normal(jax.random.fold_in(_gk, 1), (6250, 256), jnp.float32)
        src = jax.random.randint(jax.random.fold_in(_gk, 2), (100000,), 0, 6250, jnp.int32)
        dst = jax.random.randint(jax.random.fold_in(_gk, 3), (100000,), 0, 6250, jnp.int32)
        _o = jnp.argsort(dst, stable=True)
        src = src[_o]
        dst = dst[_o]
        edge_attr_18 = 0.00023367 + 0.999922 * jax.random.normal(jax.random.fold_in(_gk, 11), (100000, 18), jnp.float32)
        return (x, src, dst, edge_attr_18)
    x, src, dst, edge_attr_18 = _rec_inputs()

    def _L0_gnn_setup():
        import jax, jax.numpy as jnp
        import numpy as np
        N, E = (6250, 100000)
        DIM, H, D = (256, 16, 8)
        DH = D * H
        IN_RPE = 18
        SCALE = D ** (-0.5)
        EPS = 1e-16

        def _segment_softmax(compat, s, num_nodes):
            m = jax.ops.segment_max(compat, s, num_segments=num_nodes)
            ex = jnp.exp(compat - m[s])
            den = jax.ops.segment_sum(ex, s, num_segments=num_nodes)
            return ex / (den[s] + EPS)
        key = jax.random.key(seed)
        ks = jax.random.split(key, 10)
        x = jax.random.normal(ks[0], (N, DIM), dtype=jnp.float32)
        edge_index = jax.random.randint(ks[1], (2, E), 0, N, dtype=jnp.int64)
        edge_attr = jax.random.normal(ks[2], (E, IN_RPE), dtype=jnp.float32)
        Wqkv = jax.random.normal(ks[3], (DIM, 2 * DH + DIM), dtype=jnp.float32) * DIM ** (-0.5)
        bqkv = jnp.zeros((2 * DH + DIM,), dtype=jnp.float32)
        Wk_rpe = jax.random.normal(ks[4], (IN_RPE, DH), dtype=jnp.float32) * IN_RPE ** (-0.5)
        bk_rpe = jnp.zeros((DH,), dtype=jnp.float32)
        Wq_rpe = jax.random.normal(ks[5], (IN_RPE, DH), dtype=jnp.float32) * IN_RPE ** (-0.5)
        bq_rpe = jnp.zeros((DH,), dtype=jnp.float32)
        return {'x': x, 'edge_index': edge_index, 'edge_attr': edge_attr, 'Wqkv': Wqkv, 'bqkv': bqkv, 'Wk_rpe': Wk_rpe, 'bk_rpe': bk_rpe, 'Wq_rpe': Wq_rpe, 'bq_rpe': bq_rpe}
    _L0_gnn_all = _L0_gnn_setup()
    _L0_gnn_in = {k: v for k, v in _L0_gnn_all.items() if k in ('Wqkv', 'bqkv', 'Wk_rpe', 'bk_rpe', 'Wq_rpe', 'bq_rpe')}
    del _L0_gnn_all

    def _L0_mix_setup():
        import jax, jax.numpy as jnp
        import numpy as np
        A, Bc, Cc = (0.5, 1.0, 1.0)
        H = 8
        EPS = 1e-12

        def _normalize(t):
            n = jnp.linalg.norm(t, axis=-1, keepdims=True)
            return t / jnp.maximum(n, EPS)
        key = jax.random.key(seed)
        ks = jax.random.split(key, 5)
        B, N, C = (8, 256, 256)
        D = C // H
        x = jax.random.normal(ks[0], (B, N, C), dtype=jnp.float32)
        Wqkv = jax.random.normal(ks[1], (3 * H * D, C), dtype=jnp.float32) * 0.02
        bqkv = jnp.zeros((3 * H * D,), dtype=jnp.float32)
        Wproj = jax.random.normal(ks[2], (C, H * D), dtype=jnp.float32) * 0.02
        bproj = jnp.zeros((C,), dtype=jnp.float32)
        temperature = jnp.ones((1, H, 1, 1), dtype=jnp.float32)
        return {'x': x, 'Wqkv': Wqkv, 'bqkv': bqkv, 'Wproj': Wproj, 'bproj': bproj, 'temperature': temperature}
    _L0_mix_all = _L0_mix_setup()
    _L0_mix_in = {k: v for k, v in _L0_mix_all.items() if k in ('Wqkv', 'bqkv', 'Wproj', 'bproj', 'temperature')}
    del _L0_mix_all

    def _L0_ffn_setup():
        import jax, jax.numpy as jnp
        import numpy as np
        BN_EPS = 0.001

        def _bn(h, g, b, m, v):
            return g * (h - m) * jax.lax.rsqrt(v + BN_EPS) + b
        key = jax.random.key(seed)
        ks = jax.random.split(key, 8)
        B, F, Df = (256, 64, 256)
        E, H, D = (8, 256, 256)
        s1 = 1.0 / np.sqrt(Df)
        s2 = 1.0 / np.sqrt(H)
        return {'x': jax.random.normal(ks[0], (B, F, Df), jnp.float32), 'Wr': jax.random.normal(ks[1], (Df, E), jnp.float32) * s1, 'br': jnp.zeros((E,), jnp.float32), 'W1': jax.random.normal(ks[2], (E, Df, H), jnp.float32) * s1, 'b1': jnp.zeros((E, H), jnp.float32), 'g1': jnp.ones((E, H), jnp.float32), 'be1': jnp.zeros((E, H), jnp.float32), 'm1': jnp.zeros((E, H), jnp.float32), 'v1': jnp.ones((E, H), jnp.float32), 'W2': jax.random.normal(ks[3], (E, H, H), jnp.float32) * s2, 'b2': jnp.zeros((E, H), jnp.float32), 'g2': jnp.ones((E, H), jnp.float32), 'be2': jnp.zeros((E, H), jnp.float32), 'm2': jnp.zeros((E, H), jnp.float32), 'v2': jnp.ones((E, H), jnp.float32), 'Wo': jax.random.normal(ks[4], (E, H, D), jnp.float32) * s2, 'bo': jnp.zeros((E, D), jnp.float32)}
    _L0_ffn_all = _L0_ffn_setup()
    _L0_ffn_in = {k: v for k, v in _L0_ffn_all.items() if k in ('Wr', 'br', 'W1', 'b1', 'g1', 'be1', 'm1', 'v1', 'W2', 'b2', 'g2', 'be2', 'm2', 'v2', 'Wo', 'bo')}
    del _L0_ffn_all
    return {'x': x, 'src': src, 'dst': dst, 'edge_attr_18': edge_attr_18, 'L0_gnn_Wqkv': _L0_gnn_in['Wqkv'], 'L0_gnn_bqkv': _L0_gnn_in['bqkv'], 'L0_gnn_Wk_rpe': _L0_gnn_in['Wk_rpe'], 'L0_gnn_bk_rpe': _L0_gnn_in['bk_rpe'], 'L0_gnn_Wq_rpe': _L0_gnn_in['Wq_rpe'], 'L0_gnn_bq_rpe': _L0_gnn_in['bq_rpe'], 'L0_mix_Wqkv': _L0_mix_in['Wqkv'], 'L0_mix_bqkv': _L0_mix_in['bqkv'], 'L0_mix_Wproj': _L0_mix_in['Wproj'], 'L0_mix_bproj': _L0_mix_in['bproj'], 'L0_mix_temperature': _L0_mix_in['temperature'], 'L0_ffn_Wr': _L0_ffn_in['Wr'], 'L0_ffn_br': _L0_ffn_in['br'], 'L0_ffn_W1': _L0_ffn_in['W1'], 'L0_ffn_b1': _L0_ffn_in['b1'], 'L0_ffn_g1': _L0_ffn_in['g1'], 'L0_ffn_be1': _L0_ffn_in['be1'], 'L0_ffn_m1': _L0_ffn_in['m1'], 'L0_ffn_v1': _L0_ffn_in['v1'], 'L0_ffn_W2': _L0_ffn_in['W2'], 'L0_ffn_b2': _L0_ffn_in['b2'], 'L0_ffn_g2': _L0_ffn_in['g2'], 'L0_ffn_be2': _L0_ffn_in['be2'], 'L0_ffn_m2': _L0_ffn_in['m2'], 'L0_ffn_v2': _L0_ffn_in['v2'], 'L0_ffn_Wo': _L0_ffn_in['Wo'], 'L0_ffn_bo': _L0_ffn_in['bo']}

def reference(x, src, dst, edge_attr_18, L0_gnn_Wqkv, L0_gnn_bqkv, L0_gnn_Wk_rpe, L0_gnn_bk_rpe, L0_gnn_Wq_rpe, L0_gnn_bq_rpe, L0_mix_Wqkv, L0_mix_bqkv, L0_mix_Wproj, L0_mix_bproj, L0_mix_temperature, L0_ffn_Wr, L0_ffn_br, L0_ffn_W1, L0_ffn_b1, L0_ffn_g1, L0_ffn_be1, L0_ffn_m1, L0_ffn_v1, L0_ffn_W2, L0_ffn_b2, L0_ffn_g2, L0_ffn_be2, L0_ffn_m2, L0_ffn_v2, L0_ffn_Wo, L0_ffn_bo):
    import jax
    import jax.numpy as jnp

    def _L0_gnn_ref(x, edge_index, edge_attr, Wqkv, bqkv, Wk_rpe, bk_rpe, Wq_rpe, bq_rpe):
        import jax, jax.numpy as jnp
        import numpy as np
        N, E = (6250, 100000)
        DIM, H, D = (256, 16, 8)
        DH = D * H
        IN_RPE = 18
        SCALE = D ** (-0.5)
        EPS = 1e-16

        def _segment_softmax(compat, s, num_nodes):
            m = jax.ops.segment_max(compat, s, num_segments=num_nodes)
            ex = jnp.exp(compat - m[s])
            den = jax.ops.segment_sum(ex, s, num_segments=num_nodes)
            return ex / (den[s] + EPS)
        n = x.shape[0]
        e = edge_index.shape[1]
        qkv = x @ Wqkv + bqkv
        q = qkv[:, :DH].reshape(n, H, D)
        k = qkv[:, DH:2 * DH].reshape(n, H, D)
        v = qkv[:, 2 * DH:].reshape(n, H, DIM // H)
        s, t = (edge_index[0], edge_index[1])
        qe = q[s] * SCALE
        ke = k[t]
        ke = ke + (edge_attr @ Wk_rpe + bk_rpe).reshape(e, H, D)
        qe = qe + (edge_attr @ Wq_rpe + bq_rpe).reshape(e, H, D)
        compat = jnp.einsum('ehd,ehd->eh', qe, ke)
        attn = _segment_softmax(compat, s, n)
        msg = (v[t] * attn[..., None]).reshape(e, DIM)
        out = jax.ops.segment_sum(msg, s, num_segments=n)
        return out

    def _L0_mix_ref(x, Wqkv, bqkv, Wproj, bproj, temperature):
        import jax, jax.numpy as jnp
        import numpy as np
        A, Bc, Cc = (0.5, 1.0, 1.0)
        H = 8
        EPS = 1e-12

        def _normalize(t):
            n = jnp.linalg.norm(t, axis=-1, keepdims=True)
            return t / jnp.maximum(n, EPS)
        B, N, C = x.shape
        D = C // H
        scale = float(D) ** 0.25
        qkv = (x @ Wqkv.T + bqkv).reshape(B, N, 3, H, D)
        qkv = jnp.transpose(qkv, (2, 0, 3, 1, 4))
        q, k, v = (qkv[0], qkv[1], qkv[2])
        q = q * scale
        v1 = jnp.concatenate([jnp.ones((B, H, N, 1), dtype=v.dtype), v], axis=-1)
        qn = _normalize(q) * (scale * temperature)
        kn = _normalize(k) * scale
        vN = v1 / N
        kv_mod = jnp.einsum('bhni,bhnj,bhne->bhije', kn, kn, vN)
        kv = jnp.einsum('bhnd,bhne->bhde', kn, vN)
        vsum = jnp.sum(vN, axis=-2)[:, :, None, :]
        y = A * jnp.einsum('bhni,bhnj,bhije->bhne', qn, qn, kv_mod) + scale ** 2 * Bc * jnp.einsum('bhnd,bhde->bhne', qn, kv) + scale ** 4 * Cc * vsum
        y_norm, y = (y[..., :1], y[..., 1:])
        y = y / y_norm
        out = jnp.transpose(y, (0, 2, 1, 3)).reshape(B, N, H * D)
        return out @ Wproj.T + bproj

    def _L0_ffn_ref(x, Wr, br, W1, b1, g1, be1, m1, v1, W2, b2, g2, be2, m2, v2, Wo, bo):
        import jax, jax.numpy as jnp
        import numpy as np
        BN_EPS = 0.001

        def _bn(h, g, b, m, v):
            return g * (h - m) * jax.lax.rsqrt(v + BN_EPS) + b
        feat = jnp.mean(x, axis=0)
        w = jax.nn.softmax(feat @ Wr + br, axis=-1)
        h = jnp.einsum('bfd,edh->bfeh', x, W1) + b1
        h = jax.nn.relu(_bn(h, g1, be1, m1, v1))
        h = jnp.einsum('bfeh,ehk->bfek', h, W2) + b2
        h = jax.nn.relu(_bn(h, g2, be2, m2, v2))
        y = jnp.einsum('bfeh,ehd->bfed', h, Wo) + bo
        return jnp.einsum('bfed,fe->bfd', y, w)
    edge_index = jnp.stack([src, dst])
    xn = _layernorm(x, axis=-1)
    x = x + _L0_gnn_ref(xn, edge_index, edge_attr_18, L0_gnn_Wqkv, L0_gnn_bqkv, L0_gnn_Wk_rpe, L0_gnn_bk_rpe, L0_gnn_Wq_rpe, L0_gnn_bq_rpe) + _L0_mix_ref(xn[None], L0_mix_Wqkv, L0_mix_bqkv, L0_mix_Wproj, L0_mix_bproj, L0_mix_temperature)[0]
    x = x + _L0_ffn_ref(_layernorm(x, axis=-1)[None], L0_ffn_Wr, L0_ffn_br, L0_ffn_W1, L0_ffn_b1, L0_ffn_g1, L0_ffn_be1, L0_ffn_m1, L0_ffn_v1, L0_ffn_W2, L0_ffn_b2, L0_ffn_g2, L0_ffn_be2, L0_ffn_m2, L0_ffn_v2, L0_ffn_Wo, L0_ffn_bo)[0]
    return x

_drawn_inputs = setup_inputs


def setup_inputs(seed=0):
    import zlib

    import numpy as np

    out = dict(_drawn_inputs(seed))
    spreads = {'L0_gnn_bqkv': (0.0, 0.1),
     'L0_gnn_bk_rpe': (0.0, 0.1),
     'L0_gnn_bq_rpe': (0.0, 0.1),
     'L0_mix_bqkv': (0.0, 0.344),
     'L0_mix_bproj': (0.0, 0.1),
     'L0_mix_temperature': (1.0, 0.6),
     'L0_ffn_br': (0.0, 0.304),
     'L0_ffn_b1': (0.0, 0.403),
     'L0_ffn_g1': (1.0, 0.2),
     'L0_ffn_be1': (0.0, 0.416),
     'L0_ffn_m1': (0.0, 0.404),
     'L0_ffn_v1': (1.0, 0.6),
     'L0_ffn_b2': (0.0, 0.289),
     'L0_ffn_g2': (1.0, 0.2),
     'L0_ffn_be2': (0.0, 0.303),
     'L0_ffn_m2': (0.0, 0.299),
     'L0_ffn_v2': (1.0, 0.6),
     'L0_ffn_bo': (0.0, 0.1)}
    factors = {'L0_mix_Wqkv': 37.023}
    for name, (base, spread) in spreads.items():
        noise = np.random.default_rng([zlib.crc32(name.encode()), seed]).standard_normal(out[name].shape)
        drawn = base * np.exp(spread * noise) if base else spread * noise
        out[name] = jnp.asarray(drawn.astype(out[name].dtype))
    for name, factor in factors.items():
        out[name] = (out[name] * factor).astype(out[name].dtype)
    return out
```

```python
from contextlib import ExitStack

import numpy as np

import concourse.bass as bass
from concourse import mybir

F32 = mybir.dt.float32
BF16 = mybir.dt.bfloat16
I32 = mybir.dt.int32
ALU = mybir.AluOpType
ACT = mybir.ActivationFunctionType
AX = mybir.AxisListType.X
ENG = mybir.EngineType

P = 128
N, D = 6250, 256
NB = 50
NP = NB * P
HB = 49
E = 100000
ET = 784
EP = ET * P
FAKE = HB * P - 1
CH = 8
STEPS = 104
SLOTS = CH * STEPS * P
REC = 32
R_ONE, R_T, R_S, R_LO = 18, 19, 20, 21
GH, GD = 16, 8
MH, MD = 8, 32
ND = 17
PAIRS = ND * MD + MD + 1
NE = 8
CB = 5
NEG = -1.0e38
MSCALE = float(MD) ** 0.25

C_ID, C_IOTA, C_BEFORE, C_AFTER = 0, 128, 256, 384
C_SEL = 512
C_P = C_SEL + 7 * 128
C_MASK = C_P + 1
C_TILE = C_MASK + NB
C_END = C_TILE + CH * STEPS


def constants():
    c = np.zeros((P, C_END), np.float32)
    r = np.arange(P)
    c[:, C_ID:C_ID + P] = np.eye(P)
    c[:, C_IOTA:C_IOTA + P] = r[None, :]
    c[:, C_BEFORE:C_BEFORE + P] = r[None, :] < r[:, None]
    c[:, C_AFTER:C_AFTER + P] = r[:, None] < r[None, :]
    sel = c[:, C_SEL:C_SEL + 7 * P].reshape(P, 7, P)
    i = np.arange(MD)
    for part in range(3):
        for dd in range(4):
            sel[part * MD + i, 0, dd * MD + i] = 1
            for j in range(4):
                sel[part * MD + (i + 4 * j + dd) % MD, 1 + j, dd * MD + i] = 1
        sel[part * MD + i, 5, i] = 1
        sel[part * MD + (i + 16) % MD, 6, i] = 1
        sel[part * MD + i, 6, MD + i] = 1
    sel[96, 5, MD:2 * MD + 1] = 1
    sel[96, 6, 2 * MD] = 1
    c[:, C_P] = r
    node = np.arange(NP).reshape(NB, P).T
    c[:, C_MASK:C_MASK + NB] = (node < N) / np.float32(N)
    tile = np.arange(CH)[None, :] * STEPS + np.arange(STEPS)[:, None]
    c[:, C_TILE:C_END] = tile.reshape(-1)[None, :]
    return c


class Space:

    def __init__(self, arena, at, end):
        self.arena, self.at, self.end = arena, at, end

    def f32(self, *shape, dt=None):
        n = int(np.prod(shape))
        assert self.at + n <= self.end, (self.at, n, self.end)
        ap = self.arena[:, self.at:self.at + n]
        self.at += n
        if dt is not None:
            ap = ap.bitcast(dt)
        return split(ap, shape)

    def bf16(self, *shape):
        n = int(np.prod(shape))
        assert n % 2 == 0 and self.at + n // 2 <= self.end, (self.at, n, self.end)
        ap = self.arena[:, self.at:self.at + n // 2].bitcast(BF16)
        self.at += n // 2
        return split(ap, shape)


def split(ap, shape):
    if len(shape) == 1:
        return ap
    names = "abcd"[:len(shape)]
    return ap.rearrange(f"p ({' '.join(names)}) -> p {' '.join(names)}",
                        **{k: v for k, v in zip(names[1:], shape[1:])})


def over(ap, *dims):
    return bass.AP(tensor=ap.tensor, offset=ap.offset, ap=[list(ap.ap[0]), *[list(d) for d in dims]])


class Shared:
    pass


def rounds(eng, n):
    yield 0
    with eng.Fori(1, n) as i:
        yield i


def need(eng, sem, value):
    if isinstance(value, int) and value <= 0:
        return
    eng.wait_ge(sem, value)


def sems(nc, k, phase, names):
    s = {n: nc.alloc_semaphore(f"{phase}_{n}") for n in names.split()}
    k.sems += s.values()
    return s


def phase_setup(nc, k):
    w = Space(k.arena, k.WORK0, k.COLS0)
    lin, scol_i, tcol_i, half = (w.f32(ET, dt=I32) for _ in range(4))
    slin = w.f32(ET)
    llin = w.bf16(ET)
    blank = w.f32(64, REC)
    with ExitStack() as ctx:
        s = sems(nc, k, "setup", "loaded low_row ints blanked stored consts")
        block = ctx.enter_context(nc.Block())

        @block.sync
        def _(sp):
            sp.dma_start(k.cst, k.consts).then_inc(s["consts"], 16)
            sp.dma_start(lin, k.src_lin).then_inc(s["loaded"], 16)
            sp.dma_start(scol_i, k.src_col).then_inc(s["loaded"], 16)
            sp.dma_start(tcol_i, k.dst_col).then_inc(s["loaded"], 16)
            sp.wait_ge(s["low_row"], 2)
            sp.dma_start(k.row_s.rearrange("(p c) -> p c", p=P), slin).then_inc(s["stored"], 16)
            sp.dma_start(k.row_lo.rearrange("(p c) -> p c", p=P), llin).then_inc(s["stored"], 16)
            sp.wait_ge(s["blanked"], 2)
            for n in range(SLOTS // (64 * P)):
                sp.dma_start(k.records[n * 64 * P:(n + 1) * 64 * P, :].rearrange("(p r) f -> p r f", p=P),
                             blank).then_inc(s["stored"], 16)
            sp.wait_ge(s["stored"], 16 * (2 + SLOTS // (64 * P)))

        @block.scalar
        def _(act):
            act.wait_ge(s["consts"], 16)
            act.copy(k.ident_b, k.cst[:, C_ID:C_ID + P])
            act.copy(k.iota_b, k.cst[:, C_IOTA:C_IOTA + P])
            act.copy(k.sel_b, split(k.cst[:, C_SEL:C_SEL + 7 * P], (7, P)))

        @block.vector
        def _(dve):
            dve.memset(blank, 0.0).then_inc(s["blanked"], 1)
            dve.wait_ge(s["blanked"], 1)
            dve.memset(blank[:, :, R_S:R_S + 2], 300.0).then_inc(s["blanked"], 1)
            dve.wait_ge(s["loaded"], 48)
            dve.tensor_copy(slin, lin).then_inc(s["low_row"], 1)
            dve.tensor_scalar(half, lin, 127, None, ALU.bitwise_and).then_inc(s["ints"], 1)
            dve.wait_ge(s["ints"], 1)
            dve.tensor_copy(llin, half).then_inc(s["low_row"], 1)
            dve.tensor_copy(k.cols[:, 0], tcol_i)
            dve.tensor_copy(k.cols[:, 1], scol_i)
            dve.wait_ge(s["low_row"], 2)
            dve.tensor_scalar(half, scol_i, 127, None, ALU.bitwise_and).then_inc(s["ints"], 1)
            dve.wait_ge(s["ints"], 2)
            dve.tensor_copy(k.cols[:, 2], half).then_inc(s["ints"], 1)
            dve.wait_ge(s["ints"], 3)
            dve.tensor_scalar(half, scol_i, 7, None, ALU.arith_shift_right).then_inc(s["ints"], 1)
            dve.wait_ge(s["ints"], 4)
            dve.tensor_copy(k.cols[:, 3], half)


def phase_nodes(nc, k):
    w = Space(k.arena, k.WORK0, k.COLS0)
    wg, wm = w.f32(2, 512), w.f32(2, 768)
    bias, ones, factor = w.f32(512 + 768), w.f32(P), w.f32(16)
    xb, xn, xT = w.f32(2, D), w.f32(2, D), w.f32(2, 2, P)
    stat, gnn = w.f32(2, 16), w.f32(2, 512)
    qs, rest = w.f32(2, P), w.f32(2, P)
    mix, sq = w.f32(2, 24, MD), w.f32(2, 16, MD)
    nrm = w.f32(2, 5, 16)
    kext, v1, qn, qrest = w.f32(2, MH, 48), w.f32(2, MH, 33), w.f32(2, MH, MD), w.f32(2, MH, MD)
    parts, qTs = w.bf16(2, MH, 98), w.bf16(2, MH, P)
    ps = k.ps
    with ExitStack() as ctx:
        s = sems(nc, k, "nodes", "passed weights set x_in0 x_in1 stats mean var root_v inv xn xT_ps xT proj gnn mixed "
                 "squared qpart v1 norm2 root_n clip recip factor normed split qT_ps qT "
                 "k_out0 k_out1 v_out0 v_out1 e_out0 e_out1 w_out0 w_out1 q_out0 q_out1")
        x_in, k_out, v_out, e_out, w_out, q_out = (
            (a, b) for a, b in ((s["x_in0"], s["x_in1"]), (s["k_out0"], s["k_out1"]), (s["v_out0"], s["v_out1"]),
                                (s["e_out0"], s["e_out1"]), (s["w_out0"], s["w_out1"]), (s["q_out0"], s["q_out1"])))
        block = ctx.enter_context(nc.Block())

        @block.sync
        def _(sp):
            sp.dma_start(wg, k.gnn_w).then_inc(s["weights"], 16)
            sp.dma_start(wm, k.mix_w).then_inc(s["weights"], 16)
            sp.dma_start(bias[0:1, :], k.node_bias).then_inc(s["weights"], 16)
            sp.dma_start(factor[:, 0:MH], k.temperature.to_broadcast([P, MH])).then_inc(s["weights"], 16)
            for i in rounds(sp, NB // 2):
                for u in (0, 1):
                    b = 2 * i + u
                    need(sp, s["xn"], b - 1)
                    sp.dma_start(xb[:, u, :], k.x[bass.ds(b * P, P), :]).then_inc(x_in[u], 16)

        @block.gpsimd
        def _(pool):
            for i in rounds(pool, NB // 2):
                for u in (0, 1):
                    b = 2 * i + u
                    pool.wait_ge(s["gnn"], b + 1)
                    pool.dma_start(k.k_rows[bass.ds(b * P, P), :], gnn[:, u, P:2 * P]).then_inc(k_out[u], 16)
                    pool.dma_start(k.v_rows[bass.ds(b * P, P), :], gnn[:, u, 2 * P:]).then_inc(v_out[u], 16)
                    pool.wait_ge(s["v1"], 2 * b + 2)
                    pool.dma_start(k.v1_rows[bass.ds(b * P, P), :],
                                   v1[:, u].rearrange("p h i -> p (h i)")).then_inc(w_out[u], 16)
                    pool.wait_ge(s["normed"], 3 * b + 3)
                    pool.dma_start(k.kext_rows[bass.ds(b * P, P), :],
                                   kext[:, u].rearrange("p h i -> p (h i)")).then_inc(e_out[u], 16)
                    pool.wait_ge(s["qT"], b + 1)
                    pool.dma_start(k.qT_rows[bass.ds(b * 97, 97), :],
                                   qTs[0:97, u].rearrange("p h i -> p (h i)")).then_inc(q_out[u], 16)
            for u in (0, 1):
                for sem in (k_out[u], v_out[u], w_out[u], e_out[u], q_out[u]):
                    pool.wait_ge(sem, 16 * (NB // 2))

        @block.tensor
        def _(pe):
            def queries_T(b, u):
                pe.wait_ge(s["split"], 4 * b + 4)
                need(pe, s["qT"], b)
                for h in range(MH):
                    mm = pe.transpose(k.ps_b[0:97, 4, h * P:(h + 1) * P], parts[:, u, h, 0:97], k.ident_b)
                mm.then_inc(s["qT_ps"], 1)

            pe.wait_ge(s["weights"], 64)
            pe.wait_ge(s["set"], 1)
            for i in rounds(pe, NB // 2):
                for u in (0, 1):
                    b = 2 * i + u
                    pe.wait_ge(s["xn"], b + 1)
                    need(pe, s["xT"], b)
                    for c in range(2):
                        mm = pe.transpose(ps[:, 0, c * P:(c + 1) * P], xn[:, u, c * P:(c + 1) * P], k.ident)
                    mm.then_inc(s["xT_ps"], 1)
                    pe.wait_ge(s["xT"], b + 1)
                    need(pe, s["mixed"], 3 * b)
                    for bank, wt, c0, n, at in ((1, wg, 0, 512, 0), (2, wm, 0, 512, 512), (3, wm, 512, 256, 1024)):
                        for c in range(2):
                            pe.matmul(ps[:, bank, 0:n], xT[:, u, c, :], wt[:, c, c0:c0 + n],
                                      start=(c == 0), stop=False)
                        mm = pe.matmul(ps[:, bank, 0:n], ones[0:1, :], bias[0:1, at:at + n],
                                       start=False, stop=True)
                    mm.then_inc(s["proj"], 1)
                    if not (isinstance(b, int) and b == 0):
                        queries_T(b - 1, 1 - u)
            queries_T(NB - 1, 1)

        @block.scalar
        def _(act):
            def root_of_norms(b, u):
                act.wait_ge(s["norm2"], b + 1)
                act.activation(nrm[:, u, 1], nrm[:, u, 0], ACT.Sqrt).then_inc(s["root_n"], 1)

            def queries_T(b, u):
                act.wait_ge(s["qT_ps"], b + 1)
                need(act, q_out[u], 16 * (b // 2) if isinstance(b, int) else 8 * (b - u))
                act.copy(qTs[0:97, u], split(k.ps_b[0:97, 4, :], (MH, P))).then_inc(s["qT"], 1)

            for i in rounds(act, NB // 2):
                for u in (0, 1):
                    b = 2 * i + u
                    act.wait_ge(s["var"], b + 1)
                    act.activation(stat[:, u, 9:10], stat[:, u, 8:9], ACT.Sqrt).then_inc(s["root_v"], 1)
                    act.wait_ge(s["xT_ps"], b + 1)
                    act.copy(xT[:, u], split(ps[:, 0, 0:2 * P], (2, P))).then_inc(s["xT"], 1)
                    if not (isinstance(b, int) and b == 0):
                        root_of_norms(b - 1, 1 - u)
                    act.wait_ge(s["proj"], b + 1)
                    need(act, k_out[u], 16 * i)
                    need(act, v_out[u], 16 * i)
                    need(act, s["split"], 4 * b - 4)
                    act.copy(gnn[:, u, :], ps[:, 1, :]).then_inc(s["gnn"], 1)
                    act.activation(mix[:, u, 0:8], split(ps[:, 2, 0:D], (8, MD)), ACT.Copy,
                                   scale=MSCALE).then_inc(s["mixed"], 1)
                    act.copy(mix[:, u, 8:16], split(ps[:, 2, D:], (8, MD))).then_inc(s["mixed"], 1)
                    act.copy(mix[:, u, 16:24], split(ps[:, 3, 0:D], (8, MD))).then_inc(s["mixed"], 1)
                    act.wait_ge(s["mixed"], 3 * b + 3)
                    act.activation(sq[:, u], mix[:, u, 0:16], ACT.Square).then_inc(s["squared"], 1)
                    if not (isinstance(b, int) and b == 0):
                        queries_T(b - 1, 1 - u)
            root_of_norms(NB - 1, 1)
            queries_T(NB - 1, 1)

        @block.vector
        def _(dve):
            def layer_norm(b, u, i):
                dve.wait_ge(x_in[u], 16 * (i + 1))
                need(dve, s["xT_ps"], b - 1)
                dve.bn_stats(stat[:, u, 0:6], xb[:, u, :]).then_inc(s["stats"], 1)
                dve.wait_ge(s["stats"], b + 1)
                dve.sem_inc(s["passed"])
                dve.bn_aggr(stat[:, u, 6:8], stat[:, u, 0:6]).then_inc(s["mean"], 1)
                dve.wait_ge(s["mean"], b + 1)
                dve.tensor_scalar(stat[:, u, 8:9], stat[:, u, 7:8], 1e-5, None, ALU.add).then_inc(s["var"], 1)
                dve.wait_ge(s["root_v"], b + 1)
                dve.reciprocal(stat[:, u, 10:11], stat[:, u, 9:10]).then_inc(s["inv"], 1)
                dve.wait_ge(s["inv"], b + 1)
                dve.tensor_scalar(xn[:, u, :], xb[:, u, :], stat[:, u, 6:7], stat[:, u, 10:11],
                                  ALU.subtract, ALU.mult).then_inc(s["xn"], 1)

            def attention_inputs(b, u):
                i = b // 2 if isinstance(b, int) else None
                first = isinstance(b, int) and b < 2
                q = k.qtab[:, bass.ds(b, 1)].rearrange("p o t d -> p (o t) d")
                dve.wait_ge(s["gnn"], b + 1)
                dve.tensor_scalar(qs[:, u, :], gnn[:, u, 0:P], GD ** -0.5, None, ALU.mult).then_inc(s["qpart"], 1)
                dve.wait_ge(s["mixed"], 3 * b + 3)
                if not first:
                    dve.wait_ge(w_out[u], 8 * (b - u))
                mask = k.cst[:, bass.ds(C_MASK + b, 1)]
                dve.tensor_scalar(v1[:, u, :, 1:33], mix[:, u, 16:24], mask, None, ALU.mult).then_inc(s["v1"], 1)
                dve.tensor_scalar(v1[:, u, :, 0:1], split(ones[:, 0:MH], (MH, 1)), mask, None,
                                  ALU.mult).then_inc(s["v1"], 1)
                dve.wait_ge(s["qpart"], 5 * b + 1)
                dve.tensor_copy(q[:, 0], qs[:, u, :]).then_inc(s["qpart"], 1)
                dve.wait_ge(s["squared"], b + 1)
                dve.tensor_reduce(nrm[:, u, 0], sq[:, u], AX, ALU.add).then_inc(s["norm2"], 1)
                dve.wait_ge(s["qpart"], 5 * b + 2)
                dve.tensor_tensor(rest[:, u, :], qs[:, u, :], q[:, 0], ALU.subtract).then_inc(s["qpart"], 1)
                dve.wait_ge(s["root_n"], b + 1)
                dve.tensor_scalar(nrm[:, u, 2], nrm[:, u, 1], 1e-12, None, ALU.max).then_inc(s["clip"], 1)
                dve.wait_ge(s["qpart"], 5 * b + 3)
                dve.tensor_copy(q[:, 1], rest[:, u, :]).then_inc(s["qpart"], 1)
                dve.wait_ge(s["clip"], b + 1)
                dve.reciprocal(nrm[:, u, 3], nrm[:, u, 2]).then_inc(s["recip"], 1)
                dve.wait_ge(s["qpart"], 5 * b + 4)
                dve.tensor_tensor(q[:, 2], rest[:, u, :], q[:, 1], ALU.subtract).then_inc(s["qpart"], 1)
                dve.wait_ge(s["recip"], b + 1)
                dve.scalar_tensor_tensor(nrm[:, u, 4], nrm[:, u, 3], MSCALE, factor, ALU.mult,
                                         ALU.mult).then_inc(s["factor"], 1)
                dve.wait_ge(s["factor"], b + 1)
                if not first:
                    dve.wait_ge(e_out[u], 8 * (b - u))
                fac = nrm[:, u, 4]
                dve.tensor_tensor(qn[:, u], mix[:, u, 0:8], over(fac, (1, 8), (0, MD)),
                                  ALU.mult).then_inc(s["normed"], 1)
                fk = nrm[:, u, 4, 8:16]
                dve.tensor_tensor(kext[:, u, :, 0:32], mix[:, u, 8:16], over(fk, (1, 8), (0, 32)),
                                  ALU.mult).then_inc(s["normed"], 1)
                dve.tensor_tensor(kext[:, u, :, 32:48], mix[:, u, 8:16, 0:16], over(fk, (1, 8), (0, 16)),
                                  ALU.mult).then_inc(s["normed"], 1)
                dve.wait_ge(s["normed"], 3 * b + 1)
                need(dve, s["qT_ps"], b - 1)
                dve.tensor_copy(parts[:, u, :, 0:32], qn[:, u]).then_inc(s["split"], 1)
                dve.wait_ge(s["split"], 4 * b + 1)
                dve.tensor_tensor(qrest[:, u], qn[:, u], parts[:, u, :, 0:32], ALU.subtract).then_inc(s["split"], 1)
                dve.wait_ge(s["split"], 4 * b + 2)
                dve.tensor_copy(parts[:, u, :, 32:64], qrest[:, u]).then_inc(s["split"], 1)
                dve.wait_ge(s["split"], 4 * b + 3)
                dve.tensor_tensor(parts[:, u, :, 64:96], qrest[:, u], parts[:, u, :, 32:64],
                                  ALU.subtract).then_inc(s["split"], 1)

            dve.memset(factor[:, MH:], 1.0)
            dve.memset(parts[:, :, :, 96:97], 1.0)
            dve.memset(ones, 1.0).then_inc(s["set"], 1)
            dve.wait_ge(s["set"], 1)
            dve.wait_ge(s["weights"], 64)
            for i in rounds(dve, NB // 2):
                for u in (0, 1):
                    b = 2 * i + u
                    layer_norm(b, u, i)
                    if not (isinstance(b, int) and b == 0):
                        attention_inputs(b - 1, 1 - u)
            attention_inputs(NB - 1, 1)


def phase_kv_sums(nc, k):
    w = Space(k.arena, k.WORK0, k.MT0)
    kext, v1 = w.f32(2, MH, 48), w.f32(2, MH, 33)
    kk = w.f32(2, 4, PAIRS)
    zero = w.f32(512)
    sums = w.f32(4, 640)
    ps = k.ps
    with ExitStack() as ctx:
        s = sems(nc, k, "kv", "set in0 in1 pairs lin used summed copied turned")
        arrived = (s["in0"], s["in1"])
        block = ctx.enter_context(nc.Block())

        @block.sync
        def _(sp):
            for i in rounds(sp, NB // 2):
                for u in (0, 1):
                    b = 2 * i + u
                    need(sp, s["used"], 2 * b - 2)
                    sp.dma_start(kext[:, u].rearrange("p h i -> p (h i)"),
                                 k.kext_rows[bass.ds(b * P, P), :]).then_inc(arrived[u], 16)
                    sp.dma_start(v1[:, u].rearrange("p h i -> p (h i)"),
                                 k.v1_rows[bass.ds(b * P, P), :]).then_inc(arrived[u], 16)

        @block.vector
        def _(dve):
            dve.memset(zero, 0.0)
            dve.memset(kk[:, :, :, PAIRS - 1:], 1.0)
            dve.memset(sums, 0.0).then_inc(s["set"], 1)
            for i in rounds(dve, NB // 2):
                for u in (0, 1):
                    b = 2 * i + u
                    dve.wait_ge(arrived[u], 32 * (i + 1))
                    for half in (0, 1):
                        need(dve, s["used"], 2 * b + half - 1)
                        a = kext[:, u, 4 * half:4 * half + 4]
                        dve.tensor_tensor(over(kk[:, half], (PAIRS, 4), (MD, ND), (1, MD)),
                                          over(a, (48, 4), (0, ND), (1, MD)),
                                          over(a, (48, 4), (1, ND), (1, MD)), ALU.mult).then_inc(s["pairs"], 1)

        @block.tensor
        def _(pe):
            pe.wait_ge(s["set"], 1)
            for side in (0, 64):
                for bank in range(5):
                    n = 512 if bank < 4 else 4 * 65
                    pe.matmul(ps[side:side + 33, bank, 0:n], zero[:, 0:33], zero[:, 0:n], start=True, stop=False,
                              skip_group_check=True)
            for i in rounds(pe, NB // 2):
                for u in (0, 1):
                    b = 2 * i + u
                    for half in (0, 1):
                        pe.wait_ge(s["pairs"], 2 * b + half + 1)
                        pe.wait_ge(s["lin"], 2 * b + half + 1)
                        for j in range(4):
                            h = 4 * half + j
                            hp, side = h // 2, 64 * (h % 2)
                            pe.matmul(ps[side:side + 33, hp, :], v1[:, u, h, :], kk[:, half, j, 0:512],
                                      start=False, stop=False, skip_group_check=True)
                            mm = pe.matmul(ps[side:side + 33, 4, 65 * hp:65 * hp + 65], v1[:, u, h, :],
                                           kk[:, half, j, 512:PAIRS], start=False, stop=False,
                                           skip_group_check=True)
                        mm.then_inc(s["used"], 1)
            pe.wait_ge(s["copied"], 1)
            for t in range(20):
                mm = pe.transpose(ps[:, t // 4, (t % 4) * P:(t % 4 + 1) * P],
                                  sums[:, t // 5, (t % 5) * P:(t % 5 + 1) * P], k.ident)
            mm.then_inc(s["turned"], 1)

        @block.scalar
        def _(act):
            for i in rounds(act, NB // 2):
                for u in (0, 1):
                    b = 2 * i + u
                    act.wait_ge(arrived[u], 32 * (i + 1))
                    for half in (0, 1):
                        need(act, s["used"], 2 * b + half - 1)
                        act.copy(over(kk[:, half, 0, 544:], (PAIRS, 4), (1, MD)),
                                 kext[:, u, 4 * half:4 * half + 4, 0:32]).then_inc(s["lin"], 1)
            act.wait_ge(s["used"], 2 * NB)
            for side in (0, 64):
                r = slice(side, side + 33)
                for hp in range(4):
                    act.mul(sums[r, hp, 0:32], ps[r, hp, 0:32], 0.5)
                    act.copy(sums[r, hp, 32:512], ps[r, hp, 32:512])
                    act.mul(sums[r, hp, 512:544], ps[r, 4, 65 * hp:65 * hp + 32], 0.5)
                    act.mul(sums[r, hp, 544:576], ps[r, 4, 65 * hp + 32:65 * hp + 64], MSCALE ** 2)
                    last = act.mul(sums[r, hp, 576:577], ps[r, 4, 65 * hp + 64:65 * hp + 65], MSCALE ** 4)
            last.then_inc(s["copied"], 1)
            act.wait_ge(s["turned"], 1)
            for bank in range(5):
                act.copy(k.mt[:, 4 * bank:4 * bank + 4, :], split(ps[:, bank, :], (4, P)))


def phase_mix_out(nc, k):
    w = Space(k.arena, k.WORK0, k.MT0)
    wp, bias, ones = w.f32(2, D), w.f32(D), w.f32(P)
    qT = w.bf16(2, 4, P)
    a_sb = w.f32(2, 2, 4 * P)
    qq = w.f32(2, 5, 4 * P)
    xb, yo, yT, xo, rn = w.f32(2, D), w.f32(MH, MD), w.f32(2, P), w.f32(2, D), w.f32(MH)
    ps = k.ps
    with ExitStack() as ctx:
        s = sems(nc, k, "mix", "weights set q_in0 q_in1 x_in0 x_in1 a_ps a4_ps b_ps a_sb a4_sb qq y recip yo yT_ps "
                 "yT proj xo out0 out1")
        q_in, x_in, out = (s["q_in0"], s["q_in1"]), (s["x_in0"], s["x_in1"]), (s["out0"], s["out1"])
        block = ctx.enter_context(nc.Block())

        @block.sync
        def _(sp):
            sp.dma_start(wp, k.proj_w).then_inc(s["weights"], 16)
            sp.dma_start(bias[0:1, :], k.proj_bias).then_inc(s["weights"], 16)
            for i in rounds(sp, NB // 2):
                for u in (0, 1):
                    b = 2 * i + u
                    for half in (0, 1):
                        need(sp, s["qq"], 10 * b + 5 * half - 5)
                        sp.dma_start(qT[0:97, half],
                                     k.qT_rows[bass.ds(b * 97, 97), 512 * half:512 * half + 512].rearrange(
                                         "p (h n) -> p h n", h=4)).then_inc(q_in[half], 16)
                    need(sp, s["xo"], b - 1)
                    sp.dma_start(xb[:, u, :], k.x[bass.ds(b * P, P), :]).then_inc(x_in[u], 16)

        @block.gpsimd
        def _(pool):
            for i in rounds(pool, NB // 2):
                for u in (0, 1):
                    b = 2 * i + u
                    pool.wait_ge(s["xo"], b + 1)
                    pool.dma_start(k.xm_rows[bass.ds(b * P, P), :], xo[:, u, :]).then_inc(out[u], 16)
            for u in (0, 1):
                pool.wait_ge(out[u], 16 * (NB // 2))

        @block.tensor
        def _(pe):
            def sum_head(b, half, j):
                n = 2 * b + half
                if j == 0:
                    pe.wait_ge(s["qq"], 5 * n + 5)
                    if half == 0:
                        need(pe, s["yo"], b)
                h = 4 * half + j
                at = 64 * (h % 2)
                for g in range(5):
                    r = slice(0, P) if g < 4 else slice(0, 65)
                    mm = pe.matmul(ps[:, 4, 33 * h:33 * h + 33], qq[r, half, g, j * P:(j + 1) * P],
                                   k.mt[r, 5 * (h // 2) + g, at:at + 33], start=(g == 0), stop=(g == 4))
                if j == 3:
                    mm.then_inc(s["y"], 1)

            def finish(b):
                pe.wait_ge(s["yo"], b + 1)
                need(pe, s["yT"], b)
                for c in range(2):
                    mm = pe.transpose(ps[:, 5, c * P:(c + 1) * P],
                                      yo.rearrange("p h i -> p (h i)")[:, c * P:(c + 1) * P], k.ident)
                mm.then_inc(s["yT_ps"], 1)
                pe.wait_ge(s["yT"], b + 1)
                need(pe, s["xo"], b)
                for c in range(2):
                    pe.matmul(ps[:, 6, 0:D], yT[:, c, :], wp[:, c, :], start=(c == 0), stop=False)
                pe.matmul(ps[:, 6, 0:D], ones[0:1, :], bias[0:1, :], start=False, stop=True).then_inc(s["proj"], 1)

            pe.wait_ge(s["weights"], 32)
            pe.wait_ge(s["set"], 1)
            for b in rounds(pe, NB):
                first = isinstance(b, int)
                for half in (0, 1):
                    n = 2 * b + half
                    q = qT[0:97, half].rearrange("p h n -> p (h n)")
                    pe.wait_ge(q_in[half], 16 * (b + 1))
                    need(pe, s["a_sb"], n)
                    pe.matmul(ps[:, 0, :], k.sel_b[0:97, 0, :], q, start=True, stop=True).then_inc(s["a_ps"], 1)
                    need(pe, s["a4_sb"], n)
                    pe.matmul(ps[0:65, 1, :], k.sel_b[0:97, 5, 0:65], q, start=True, stop=True).then_inc(s["a4_ps"], 1)
                    for g in range(5):
                        m = 5 * half + g
                        need(pe, s["qq"], 10 * b + m - 1)
                        if g < 4:
                            pe.matmul(ps[:, 2 + m % 2, :], k.sel_b[0:97, 1 + g, :], q, start=True,
                                      stop=True).then_inc(s["b_ps"], 1)
                        else:
                            pe.matmul(ps[0:65, 2 + m % 2, :], k.sel_b[0:97, 6, 0:65], q, start=True,
                                      stop=True).then_inc(s["b_ps"], 1)
                        if g >= 1:
                            if half == 1:
                                sum_head(b, 0, g - 1)
                            elif not first:
                                sum_head(b - 1, 1, g - 1)
                    if half == 1 and not first:
                        finish(b - 1)
            for j in range(4):
                sum_head(NB - 1, 1, j)
            finish(NB - 1)

        @block.scalar
        def _(act):
            def turn(b):
                act.wait_ge(s["yT_ps"], b + 1)
                need(act, s["proj"], b)
                act.copy(yT, split(ps[:, 5, 0:2 * P], (2, P))).then_inc(s["yT"], 1)

            for b in rounds(act, NB):
                for half in (0, 1):
                    n = 2 * b + half
                    act.wait_ge(s["a_ps"], n + 1)
                    need(act, s["qq"], 5 * n - 5)
                    act.copy(a_sb[:, half, 0], ps[:, 0, :]).then_inc(s["a_sb"], 1)
                    act.wait_ge(s["a4_ps"], n + 1)
                    act.copy(a_sb[0:65, half, 1], ps[0:65, 1, :]).then_inc(s["a4_sb"], 1)
                if not isinstance(b, int):
                    turn(b - 1)
            turn(NB - 1)

        @block.vector
        def _(dve):
            def divide(b):
                dve.wait_ge(s["y"], 2 * b + 2)
                y = split(ps[:, 4, 0:MH * 33], (MH, 33))
                dve.reciprocal(split(rn, (MH, 1)), y[:, :, 0:1]).then_inc(s["recip"], 1)
                dve.wait_ge(s["recip"], b + 1)
                need(dve, s["yT_ps"], b)
                dve.tensor_tensor(yo, y[:, :, 1:33], over(rn, (1, MH), (0, MD)), ALU.mult).then_inc(s["yo"], 1)

            def add(b, u):
                dve.wait_ge(s["proj"], b + 1)
                dve.wait_ge(x_in[u], 8 * (b - u) + 16)
                if not (isinstance(b, int) and b < 2):
                    dve.wait_ge(out[u], 8 * (b - u))
                dve.tensor_tensor(xo[:, u, :], ps[:, 6, 0:D], xb[:, u, :], ALU.add).then_inc(s["xo"], 1)

            dve.memset(ones, 1.0).then_inc(s["set"], 1)
            for i in rounds(dve, NB // 2):
                for u in (0, 1):
                    b = 2 * i + u
                    start = isinstance(b, int) and b == 0
                    for half in (0, 1):
                        n = 2 * b + half
                        dve.wait_ge(s["a_sb"], n + 1)
                        dve.wait_ge(s["a4_sb"], n + 1)
                        need(dve, s["y"], n - 1)
                        for g in range(5):
                            m = 5 * half + g
                            r = slice(0, P) if g < 4 else slice(0, 65)
                            dve.wait_ge(s["b_ps"], 10 * b + m + 1)
                            dve.tensor_tensor(qq[r, half, g], ps[r, 2 + m % 2, :], a_sb[r, half, int(g == 4)],
                                              ALU.mult).then_inc(s["qq"], 1)
                        if half == 0 and not start:
                            divide(b - 1)
                    if not start:
                        add(b - 1, 1 - u)
            divide(NB - 1)
            add(NB - 1, 1)


def phase_histogram(nc, k):
    w = Space(k.arena, k.WORK0, k.COLS0)
    low, high, zero = w.bf16(2, 8, P), w.bf16(2, 8, NB), w.bf16(P)
    with ExitStack() as ctx:
        s = sems(nc, k, "hist", "set hot used")
        block = ctx.enter_context(nc.Block())

        @block.vector
        def _(dve):
            dve.memset(zero, 0.0).then_inc(s["set"], 1)
            for i in rounds(dve, ET // 16):
                for u in (0, 1):
                    g = 2 * i + u
                    need(dve, s["used"], g - 1)
                    for j in range(8):
                        dve.tensor_scalar(low[:, u, j, :], k.iota_b, k.cols[:, 2, bass.ds(g * 8 + j, 1)], None,
                                          ALU.is_equal)
                        last = dve.tensor_scalar(high[:, u, j, :], k.iota_b[:, 0:NB],
                                                 k.cols[:, 3, bass.ds(g * 8 + j, 1)], None, ALU.is_equal)
                    last.then_inc(s["hot"], 1)
            dve.wait_ge(s["used"], ET // 8)
            dve.tensor_copy(k.start, k.ps[:, 0, 0:NB])

        @block.tensor
        def _(pe):
            pe.wait_ge(s["set"], 1)
            pe.matmul(k.ps[:, 0, 0:NB], zero, zero[:, 0:NB], start=True, stop=False, skip_group_check=True)
            for i in rounds(pe, ET // 16):
                for u in (0, 1):
                    g = 2 * i + u
                    pe.wait_ge(s["hot"], g + 1)
                    for j in range(8):
                        mm = pe.matmul(k.ps[:, 0, 0:NB], low[:, u, j, :], high[:, u, j, :], start=False, stop=False,
                                       skip_group_check=True)
                    mm.then_inc(s["used"], 1)


def phase_starts(nc, k):
    w = Space(k.arena, k.WORK0, k.COLS0)
    ones, one_b = w.f32(P), w.bf16(P)
    tot, count, tiles, ends, first = w.f32(NB), w.f32(NB, dt=I32), w.f32(NB), w.f32(NB), w.f32(NB)
    whole = w.f32(NB, dt=I32)
    end_col, after = w.f32(2), w.bf16(CH * STEPS)
    half = CH * STEPS // 2
    ps = k.ps
    with ExitStack() as ctx:
        s = sems(nc, k, "starts", "set sums turned col after blocks d")
        block = ctx.enter_context(nc.Block())

        @block.tensor
        def _(pe):
            pe.wait_ge(s["set"], 1)
            pe.matmul(ps[:, 1, 0:NB], ones, k.start, start=True, stop=True)
            pe.matmul(ps[:, 2, 0:NB], k.cst[:, C_AFTER:C_AFTER + P], k.start, start=True,
                      stop=True).then_inc(s["sums"], 1)
            pe.wait_ge(s["d"], 5)
            pe.transpose(ps[0:NB, 3, 0:P], ends, k.ident).then_inc(s["turned"], 1)
            pe.wait_ge(s["after"], 1)
            for c in range(2):
                mm = pe.matmul(ps[0:1, 4 + c, 0:half], one_b[0:NB, 0:1], after[0:NB, c * half:(c + 1) * half],
                               start=True, stop=True)
            mm.then_inc(s["blocks"], 1)

        @block.vector
        def _(dve):
            done = 0

            def then(ins):
                nonlocal done
                done += 1
                ins.then_inc(s["d"], 1)
                dve.wait_ge(s["d"], done)

            dve.memset(one_b, 1.0)
            dve.memset(ones, 1.0).then_inc(s["set"], 1)
            dve.wait_ge(s["sums"], 1)
            then(dve.tensor_scalar(tot, ps[:, 1, 0:NB], float(P - 1), None, ALU.add))
            then(dve.tensor_copy(count, tot))
            then(dve.tensor_scalar(whole, count, 7, None, ALU.arith_shift_right))
            then(dve.tensor_copy(tiles, whole))
            then(dve.tensor_tensor_scan(ends, ones[:, 0:NB], tiles, 0.0, ALU.mult, ALU.add))
            then(dve.tensor_tensor(first, ends, tiles, ALU.subtract))
            then(dve.scalar_tensor_tensor(k.start, first, float(P), ps[:, 2, 0:NB], ALU.mult, ALU.add))
            dve.wait_ge(s["turned"], 1)
            dve.tensor_copy(end_col[0:NB, 0:1], ps[0:NB, 3, 0:1]).then_inc(s["col"], 1)
            dve.wait_ge(s["col"], 1)
            dve.tensor_scalar(after[0:NB, :], k.cst[0:NB, C_TILE:C_END], end_col[0:NB, 0:1], None,
                              ALU.is_ge).then_inc(s["after"], 1)
            dve.wait_ge(s["blocks"], 1)
            for c in range(2):
                dve.tensor_scalar(k.blocks[0:1, c * half:(c + 1) * half], ps[0:1, 4 + c, 0:half], float(HB - 1),
                                  None, ALU.min)


def phase_scatter(nc, k):
    w = Space(k.arena, k.WORK0, k.COLS0)
    row_s, row_lo = w.f32(2, 8 * P), w.bf16(2, 8 * P)
    low_T, low, high = w.f32(2, 8, P), w.bf16(2, 8, P), w.bf16(2, 8, NB)
    table = w.f32(2, NB)
    junk_e, junk_g = w.f32(8, P), w.f32(8, NB)
    before, rank, slot = w.f32(2, 8), w.f32(2, 8), w.f32(2, 8, dt=I32)
    rec = w.f32(2, 8, REC)
    ps = k.ps
    with ExitStack() as ctx:
        s = sems(nc, k, "scatter", "passed set rows0 rows1 attr0 attr1 low_T hot fields seeded count table looked summed "
                 "ranked slots out0 out1")
        rows, attr, out = (s["rows0"], s["rows1"]), (s["attr0"], s["attr1"]), (s["out0"], s["out1"])
        block = ctx.enter_context(nc.Block())

        @block.sync
        def _(sp):
            sp.wait_ge(s["set"], 1)
            for i in rounds(sp, ET // 16):
                for u in (0, 1):
                    g = 2 * i + u
                    need(sp, s["slots"], g - 1)
                    sp.dma_start(row_s[:, u, :], k.row_s[bass.ds(g * 8 * P, 8 * P)].partition_broadcast(P)
                                 ).then_inc(rows[u], 16)
                    sp.dma_start(row_lo[:, u, :], k.row_lo[bass.ds(g * 8 * P, 8 * P)].partition_broadcast(P)
                                 ).then_inc(rows[u], 16)
                    need(sp, out[u], 128 * i)
                    sp.dma_start(rec[:, u, :, 0:R_ONE], k.attr[:, bass.ds(g * 8, 8), :]).then_inc(attr[u], 16)

        @block.scalar
        def _(act):
            act.wait_ge(s["set"], 1)
            act.wait_ge(s["seeded"], 1)
            act.copy(table[:, 0], ps[:, 0, 0:NB]).then_inc(s["table"], 1)
            for i in rounds(act, ET // 16):
                for u in (0, 1):
                    g = 2 * i + u
                    need(act, out[u], 128 * i)
                    act.copy(rec[:, u, :, R_T:R_LO + 1].rearrange("p e f -> p f e"),
                             k.cols[:, 0:3, bass.ds(g * 8, 8)]).then_inc(s["fields"], 1)
                    for j in range(8):
                        t = 8 * g + j
                        act.wait_ge(s["count"], t + 1)
                        need(act, s["looked"], t)
                        act.copy(table[:, (j + 1) % 2], ps[:, 0, 0:NB]).then_inc(s["table"], 1)

        @block.tensor
        def _(pe):
            pe.matmul(ps[:, 0, 0:NB], k.ident, k.start, start=True, stop=False,
                      skip_group_check=True).then_inc(s["seeded"], 1)
            for i in rounds(pe, ET // 16):
                for u in (0, 1):
                    g = 2 * i + u
                    pe.wait_ge(s["low_T"], g + 1)
                    pe.wait_ge(s["hot"], g + 1)
                    for j in range(8):
                        t = 8 * g + j
                        pe.wait_ge(s["table"], t + 1)
                        need(pe, s["summed"], t - 1)
                        pe.matmul(ps[:, 1 + j % 2, 0:NB], low_T[:, u, j, :], table[:, j % 2], start=True,
                                  stop=True).then_inc(s["looked"], 1)
                        pe.matmul(ps[:, 0, 0:NB], low[:, u, j, :], high[:, u, j, :], start=False, stop=False,
                                  skip_group_check=True).then_inc(s["count"], 1)

        @block.vector
        def _(dve):
            dve.memset(rec, 0.0).then_inc(s["ranked"], 1)
            dve.wait_ge(s["ranked"], 1)
            dve.memset(rec[:, :, :, R_ONE:R_ONE + 1], 1.0).then_inc(s["set"], 1)
            for i in rounds(dve, ET // 16):
                for u in (0, 1):
                    g = 2 * i + u
                    dve.wait_ge(rows[u], 32 * (i + 1))
                    need(dve, s["looked"], 8 * g - 8)
                    need(dve, s["count"], 8 * g - 8)
                    dve.tensor_scalar(low_T[:, u].rearrange("p j e -> p (j e)"), row_lo[:, u, :],
                                      k.cst[:, C_P:C_P + 1], None, ALU.is_equal).then_inc(s["low_T"], 1)
                    for j in range(8):
                        dve.tensor_scalar(low[:, u, j, :], k.iota_b, k.cols[:, 2, bass.ds(g * 8 + j, 1)], None,
                                          ALU.is_equal)
                        last = dve.tensor_scalar(high[:, u, j, :], k.iota_b[:, 0:NB],
                                                 k.cols[:, 3, bass.ds(g * 8 + j, 1)], None, ALU.is_equal)
                    last.then_inc(s["hot"], 1)
                    dve.wait_ge(s["hot"], g + 1)
                    for j in range(8):
                        dve.scalar_tensor_tensor(junk_e[:, j, :], row_s[:, u, j * P:(j + 1) * P],
                                                 k.cols[:, 1, bass.ds(g * 8 + j, 1)],
                                                 k.cst[:, C_BEFORE:C_BEFORE + P], ALU.is_equal, ALU.mult,
                                                 accum_out=before[:, u, j:j + 1])
                        dve.wait_ge(s["looked"], 8 * g + j + 1)
                        dve.tensor_tensor_reduce(junk_g[:, j, :], ps[:, 1 + j % 2, 0:NB], high[:, u, j, :], 1.0, 0.0,
                                                 ALU.mult, ALU.add, rank[:, u, j:j + 1]).then_inc(s["summed"], 1)
                    dve.wait_ge(s["summed"], 8 * g + 8)
                    need(dve, out[u], 128 * i)
                    dve.tensor_tensor(slot[:, u, :], before[:, u, :], rank[:, u, :], ALU.add).then_inc(s["slots"], 1)

        @block.gpsimd
        def _(pool):
            for i in rounds(pool, ET // 16):
                for u in (0, 1):
                    g = 2 * i + u
                    pool.wait_ge(attr[u], 16 * (i + 1))
                    pool.wait_ge(s["fields"], g + 1)
                    pool.wait_ge(s["slots"], g + 1)
                    pool.sem_inc(s["passed"])
                    for j in range(8):
                        pool.indirect_dma_start(out=k.records, out_offset=bass.IndirectOffsetOnAxis(
                            ap=slot[:, u, j:j + 1], axis=0), in_=rec[:, u, j, :], in_offset=None
                        ).then_inc(out[u], 16)
            for u in (0, 1):
                pool.wait_ge(out[u], 128 * (ET // 16))


def records_of(k, g):
    return k.records.rearrange("(c g e) f -> g e c f", c=CH, g=STEPS)[bass.ds(g, 1)].rearrange(
        "o e c f -> (o e) c f")


def blocks_of(nc, k, g, engine):
    return nc.values_load_multi_w_load_instructions(
        k.blocks[0:1, bass.ds(g * CH, CH)], engines=[engine], min_val=0, max_val=HB - 1,
        skip_runtime_bounds_check_because="phase_starts keeps them at most HB - 1")[1]


def phase_compat(nc, k):
    w = Space(k.arena, k.WORK0, k.BIG1)
    rec, kg = w.f32(2, CH, REC), w.f32(2, CH, P)
    t_int = w.f32(2, CH, dt=I32)
    hot, hot_T = w.bf16(2, CH, P), w.bf16(2, CH, P)
    rec_T = w.f32(2, 2, P)
    ks, prod = w.f32(2, 4, P), w.f32(2, 4, P)
    score, node = w.f32(2, CH, GH), w.f32(2, CH, GH)
    wr = w.f32(4, 2 * P)
    ps = k.ps
    with ExitStack() as ctx:
        s = sems(nc, k, "compat", "passed weights r_in0 r_in1 t k_in0 k_in1 hot hot_ps hot_T rec_ps rec_T qk ks prod score "
                 "node turned stored")
        r_in, k_in = (s["r_in0"], s["r_in1"]), (s["k_in0"], s["k_in1"])
        block = ctx.enter_context(nc.Block())

        @block.sync
        def _(sp):
            sp.dma_start(wr, k.rpe_w).then_inc(s["weights"], 16)
            for i in rounds(sp, STEPS // 2):
                for u in (0, 1):
                    g = 2 * i + u
                    need(sp, s["rec_ps"], g - 1)
                    need(sp, s["hot"], g - 1)
                    need(sp, s["node"], g - 1)
                    sp.dma_start(rec[:, u], records_of(k, g)).then_inc(r_in[u], 16)

        @block.gpsimd
        def _(pool):
            for i in rounds(pool, STEPS // 2):
                for u in (0, 1):
                    g = 2 * i + u
                    pool.wait_ge(s["t"], g + 1)
                    need(pool, s["ks"], 2 * g - 2)
                    pool.sem_inc(s["passed"])
                    for c in range(CH):
                        pool.indirect_dma_start(out=kg[:, u, c, :], out_offset=None, in_=k.k_rows,
                                                in_offset=bass.IndirectOffsetOnAxis(ap=t_int[:, u, c:c + 1], axis=0)
                                                ).then_inc(k_in[u], 16)

        @block.tensor
        def _(pe):
            def products(g, u):
                blk = blocks_of(nc, k, g, ENG.PE)
                pe.wait_ge(s["rec_T"], g + 1)
                pe.wait_ge(s["hot_T"], g + 1)
                for half in (0, 1):
                    need(pe, s["prod"], 2 * g + half - 1)
                    for j in range(4):
                        c = 4 * half + j
                        bank, at = 2 + 2 * half + j // 2, (j % 2) * 2 * P
                        pe.matmul(ps[:, bank, at:at + 2 * P], rec_T[:, u, half, :], wr[:, j, :], start=True,
                                  stop=False, skip_group_check=True)
                        for part in range(3):
                            q = k.qtab[:, bass.ds(blk[c], 1), part, :].rearrange("p o d -> p (o d)")
                            mm = pe.matmul(ps[:, bank, at:at + P], hot_T[:, u, c, :], q, start=False,
                                           stop=(part == 2), skip_group_check=True)
                    mm.then_inc(s["qk"], 1)

            def turn(g, u):
                pe.wait_ge(s["score"], 2 * g + 2)
                pe.wait_ge(s["node"], g + 1)
                need(pe, s["stored"], g)
                pe.transpose(ps[:, 6, 0:P], score[:, u].rearrange("p c h -> p (c h)"), k.ident)
                pe.transpose(ps[:, 6, P:2 * P], node[:, u].rearrange("p c h -> p (c h)"),
                             k.ident).then_inc(s["turned"], 1)

            pe.wait_ge(s["weights"], 16)
            for i in rounds(pe, STEPS // 2):
                for u in (0, 1):
                    g = 2 * i + u
                    pe.wait_ge(r_in[u], 16 * (i + 1))
                    need(pe, s["rec_T"], g)
                    for half in (0, 1):
                        mm = pe.transpose(ps[:, 1, half * P:(half + 1) * P],
                                          rec[:, u, 4 * half:4 * half + 4].rearrange("p c f -> p (c f)"), k.ident)
                    mm.then_inc(s["rec_ps"], 1)
                    pe.wait_ge(s["hot"], g + 1)
                    need(pe, s["hot_T"], g)
                    for c in range(CH):
                        mm = pe.transpose(k.ps_b[:, 0, c * P:(c + 1) * P], hot[:, u, c, :], k.ident_b)
                    mm.then_inc(s["hot_ps"], 1)
                    if not (isinstance(g, int) and g < 1):
                        products(g - 1, 1 - u)
                    if not (isinstance(g, int) and g < 2):
                        turn(g - 2, u)
            products(STEPS - 1, 1)
            turn(STEPS - 2, 0)
            turn(STEPS - 1, 1)

        @block.scalar
        def _(act):
            def store(g):
                act.wait_ge(s["turned"], g + 1)
                act.copy(k.scores[:, bass.ds(g * P, P)], ps[:, 6, 0:P])
                act.copy(k.owner[:, bass.ds(g * P, P)], ps[:, 6, P:2 * P]).then_inc(s["stored"], 1)

            for i in rounds(act, STEPS // 2):
                for u in (0, 1):
                    g = 2 * i + u
                    act.wait_ge(s["rec_ps"], g + 1)
                    need(act, s["qk"], 2 * g - 2)
                    act.copy(rec_T[:, u], split(ps[:, 1, 0:2 * P], (2, P))).then_inc(s["rec_T"], 1)
                    act.wait_ge(s["hot_ps"], g + 1)
                    act.copy(hot_T[:, u], split(k.ps_b[:, 0, :], (CH, P))).then_inc(s["hot_T"], 1)
                    act.wait_ge(r_in[u], 16 * (i + 1))
                    need(act, s["turned"], g - 1)
                    act.copy(node[:, u], over(rec[:, u, 0, R_S:], (REC, CH), (0, GH))).then_inc(s["node"], 1)
                    if not (isinstance(g, int) and g < 2):
                        store(g - 2)
            store(STEPS - 2)
            store(STEPS - 1)

        @block.vector
        def _(dve):
            def scores(g, u):
                dve.wait_ge(k_in[u], 64 * (g - u) + 128)
                for half in (0, 1):
                    qk = ps[:, 2 + 2 * half:4 + 2 * half, :].rearrange("p b (j w) -> p b j w", j=2)
                    n = 2 * g + half
                    sum_, product = (t[:, half].rearrange("p (b j) w -> p b j w", b=2) for t in (ks, prod))
                    dve.wait_ge(s["qk"], n + 1)
                    dve.tensor_tensor(sum_, qk[:, :, :, P:2 * P],
                                      kg[:, u, 4 * half:4 * half + 4, :].rearrange("p (b j) w -> p b j w", b=2),
                                      ALU.add).then_inc(s["ks"], 1)
                for half in (0, 1):
                    qk = ps[:, 2 + 2 * half:4 + 2 * half, :].rearrange("p b (j w) -> p b j w", j=2)
                    n = 2 * g + half
                    sum_, product = (t[:, half].rearrange("p (b j) w -> p b j w", b=2) for t in (ks, prod))
                    dve.wait_ge(s["ks"], n + 1)
                    dve.tensor_tensor(product, qk[:, :, :, 0:P], sum_, ALU.mult).then_inc(s["prod"], 1)
                need(dve, s["turned"], g - 1)
                for half in (0, 1):
                    dve.wait_ge(s["prod"], 2 * g + half + 1)
                    dve.tensor_reduce(score[:, u, 4 * half:4 * half + 4].rearrange("p c h -> p (c h)"),
                                      prod[:, half].rearrange("p c (h d) -> p (c h) d", d=GD), AX,
                                      ALU.add).then_inc(s["score"], 1)

            for i in rounds(dve, STEPS // 2):
                for u in (0, 1):
                    g = 2 * i + u
                    dve.wait_ge(r_in[u], 16 * (i + 1))
                    need(dve, k_in[u], 128 * i)
                    dve.tensor_copy(t_int[:, u, :], over(rec[:, u, 0, R_T:], (REC, CH))).then_inc(s["t"], 1)
                    need(dve, s["hot_ps"], g - 1)
                    for c in range(CH):
                        last = dve.tensor_scalar(hot[:, u, c, :], k.iota_b, rec[:, u, c, R_LO:R_LO + 1], None,
                                                 ALU.is_equal)
                    last.then_inc(s["hot"], 1)
                    if not (isinstance(g, int) and g < 1):
                        scores(g - 1, 1 - u)
            scores(STEPS - 1, 1)


def phase_seg_max(nc, k):
    L = STEPS * P
    w = Space(k.arena, k.WORK0, k.FL0)
    ends, row, carry, col = w.f32(4), w.f32(4, CH, GH), w.f32(6, CH, GH), w.f32(2)
    breaks = k.breaks
    ps = k.ps
    with ExitStack() as ctx:
        s = sems(nc, k, "segmax", "d ends turned carry back")
        block = ctx.enter_context(nc.Block())

        @block.tensor
        def _(pe):
            pe.wait_ge(s["ends"], 1)
            for n in range(4):
                mm = pe.transpose(ps[0:1, 0, n * P:(n + 1) * P], ends[:, n:n + 1], k.ident)
            mm.then_inc(s["turned"], 1)
            pe.wait_ge(s["carry"], 1)
            for n in range(2):
                mm = pe.matmul(ps[:, 1, n:n + 1], carry[0:1, n].rearrange("p c h -> p (c h)"),
                               k.ident[0:1, 0:1], start=True, stop=True)
            mm.then_inc(s["back"], 1)

        @block.vector
        def _(dve):
            done = 0

            def then(ins):
                nonlocal done
                done += 1
                ins.then_inc(s["d"], 1)
                dve.wait_ge(s["d"], done)

            back = lambda ap: over(ap[:, L - 1:L], (-1, L))
            then(dve.memset(breaks, 0.0))
            then(dve.tensor_tensor(breaks[:, 1:L], k.owner[:, 1:L], k.owner[:, 0:L - 1], ALU.not_equal))
            then(dve.tensor_scalar(breaks[:, 1:L], breaks[:, 1:L], NEG, None, ALU.mult))
            dve.tensor_copy(ends[:, 0:1], k.owner[:, 0:1])
            then(dve.tensor_copy(ends[:, 1:2], k.owner[:, L - 1:L]))
            then(dve.tensor_tensor_scan(k.owner, breaks[:, 0:L], k.scores, NEG, ALU.add, ALU.max))
            then(dve.tensor_copy(ends[:, 2:3], k.owner[:, L - 1:L]))
            then(dve.tensor_tensor_scan(back(k.owner), back(breaks[:, 1:L + 1]), back(k.scores), NEG, ALU.add,
                                        ALU.max))
            dve.tensor_copy(ends[:, 3:4], k.owner[:, 0:1]).then_inc(s["ends"], 1)
            dve.wait_ge(s["turned"], 1)
            then(dve.tensor_copy(row[0:1], split(ps[0:1, 0, :], (4, CH, GH))))
            first, last, fwd, bwd = (row[0:1, n] for n in range(4))
            from_left, from_right, apart, many, both = (carry[0:1, n] for n in range(5))
            then(dve.memset(carry[0:1], NEG))
            dve.tensor_tensor(apart[:, 1:CH], first[:, 1:CH], last[:, 0:CH - 1], ALU.not_equal)
            then(dve.tensor_tensor(many, first, last, ALU.not_equal))
            dve.tensor_scalar(apart[:, 1:CH], apart[:, 1:CH], NEG, None, ALU.mult)
            then(dve.tensor_scalar(many, many, NEG, None, ALU.mult))
            for c in range(1, CH):
                then(dve.tensor_tensor(both[:, c], from_left[:, c - 1], many[:, c - 1], ALU.add))
                then(dve.tensor_tensor(both[:, c], both[:, c], fwd[:, c - 1], ALU.max))
                then(dve.tensor_tensor(from_left[:, c], both[:, c], apart[:, c], ALU.add))
            for c in range(CH - 2, -1, -1):
                then(dve.tensor_tensor(both[:, c], from_right[:, c + 1], many[:, c + 1], ALU.add))
                then(dve.tensor_tensor(both[:, c], both[:, c], bwd[:, c + 1], ALU.max))
                then(dve.tensor_tensor(from_right[:, c], both[:, c], apart[:, c + 1], ALU.add))
            dve.nop().then_inc(s["carry"], 1)
            dve.wait_ge(s["back"], 1)
            then(dve.tensor_copy(col, ps[:, 1, 0:2]))
            then(dve.tensor_tensor_scan(k.owner, breaks[:, 0:L], k.scores, col[:, 0:1], ALU.add, ALU.max))
            then(dve.tensor_tensor_scan(back(k.owner), back(breaks[:, 1:L + 1]), back(k.owner), col[:, 1:2],
                                        ALU.add, ALU.max))
            then(dve.tensor_tensor(k.scores, k.scores, k.owner, ALU.subtract))


def phase_messages(nc, k):
    w = Space(k.arena, k.Q0, k.BIG1)
    rec, vg = w.f32(2, CH, REC), w.f32(2, CH, D)
    t_int = w.f32(2, CH, dt=I32)
    ex, msg, hot = w.f32(2, P), w.f32(2, CH, D + GH), w.f32(2, CH, P)
    ps = k.ps
    with ExitStack() as ctx:
        s = sems(nc, k, "msg", "passed cleared r_in0 r_in1 t v_in0 v_in1 ex ex_ps weight hot msg sums acc")
        r_in, v_in = (s["r_in0"], s["r_in1"]), (s["v_in0"], s["v_in1"])
        block = ctx.enter_context(nc.Block())

        @block.sync
        def _(sp):
            for i in rounds(sp, STEPS // 2):
                for u in (0, 1):
                    g = 2 * i + u
                    need(sp, s["hot"], g - 1)
                    sp.dma_start(rec[:, u], records_of(k, g)).then_inc(r_in[u], 16)

        @block.gpsimd
        def _(pool):
            for i in rounds(pool, STEPS // 2):
                for u in (0, 1):
                    g = 2 * i + u
                    pool.wait_ge(s["t"], g + 1)
                    need(pool, s["msg"], g - 1)
                    pool.sem_inc(s["passed"])
                    for c in range(CH):
                        pool.indirect_dma_start(out=vg[:, u, c, :], out_offset=None, in_=k.v_rows,
                                                in_offset=bass.IndirectOffsetOnAxis(ap=t_int[:, u, c:c + 1], axis=0)
                                                ).then_inc(v_in[u], 16)

        @block.scalar
        def _(act):
            def weigh(g, u):
                act.wait_ge(s["ex_ps"], g + 1)
                need(act, s["sums"], 8 * g - 8)
                act.copy(msg[:, u, :, D:], split(ps[:, u, 0:P], (CH, GH))).then_inc(s["weight"], 1)

            for i in rounds(act, STEPS // 2):
                for u in (0, 1):
                    g = 2 * i + u
                    need(act, s["ex_ps"], g - 1)
                    act.activation(ex[:, u, :], k.scores[:, bass.ds(g * P, P)], ACT.Exp).then_inc(s["ex"], 1)
                    if not (isinstance(g, int) and g == 0):
                        weigh(g - 1, 1 - u)
            weigh(STEPS - 1, 1)

        @block.tensor
        def _(pe):
            def sums(g, u):
                pe.wait_ge(s["msg"], g + 1)
                for c in range(CH):
                    n = 8 * g + c
                    need(pe, s["acc"], n - 3)
                    pe.matmul(ps[:, 2 + c % 4, 0:D + GH], hot[:, u, c, :], msg[:, u, c, :], start=True,
                              stop=True).then_inc(s["sums"], 1)

            for i in rounds(pe, STEPS // 2):
                for u in (0, 1):
                    g = 2 * i + u
                    pe.wait_ge(s["ex"], g + 1)
                    need(pe, s["weight"], g - 1)
                    pe.transpose(ps[:, u, 0:P], ex[:, u, :], k.ident).then_inc(s["ex_ps"], 1)
                    if not (isinstance(g, int) and g == 0):
                        sums(g - 1, 1 - u)
            sums(STEPS - 1, 1)

        @block.vector
        def _(dve):
            def add(g):
                blk = blocks_of(nc, k, g, ENG.DVE)
                for c in range(CH):
                    n = 8 * g + c
                    acc = k.acc[:, bass.ds(blk[c], 1), :].rearrange("p o w -> p (o w)")
                    dve.wait_ge(s["sums"], n + 1)
                    need(dve, s["acc"], n)
                    dve.tensor_tensor(acc, ps[:, 2 + c % 4, 0:D + GH], acc, ALU.add).then_inc(s["acc"], 1)

            def messages(g, u):
                dve.wait_ge(v_in[u], 64 * (g - u) + 128)
                dve.wait_ge(s["weight"], g + 1)
                dve.tensor_tensor(msg[:, u, :, 0:D].rearrange("p c (h d) -> p c h d", d=16),
                                  vg[:, u].rearrange("p c (h d) -> p c h d", d=16),
                                  over(msg[:, u, 0, D:], (D + GH, CH), (1, GH), (0, 16)),
                                  ALU.mult).then_inc(s["msg"], 1)

            dve.memset(k.acc, 0.0).then_inc(s["cleared"], 1)
            dve.wait_ge(s["cleared"], 1)
            for i in rounds(dve, STEPS // 2):
                for u in (0, 1):
                    g = 2 * i + u
                    dve.wait_ge(r_in[u], 16 * (i + 1))
                    need(dve, v_in[u], 128 * i)
                    dve.tensor_copy(t_int[:, u, :], over(rec[:, u, 0, R_T:], (REC, CH))).then_inc(s["t"], 1)
                    if not (isinstance(g, int) and g < 2):
                        add(g - 2)
                    for c in range(CH):
                        last = dve.tensor_scalar(hot[:, u, c, :], k.iota_b, rec[:, u, c, R_LO:R_LO + 1], None,
                                                 ALU.is_equal)
                    last.then_inc(s["hot"], 1)
                    if not (isinstance(g, int) and g < 1):
                        messages(g - 1, 1 - u)
            add(STEPS - 2)
            messages(STEPS - 1, 1)
            add(STEPS - 1)


def phase_norm2(nc, k):
    w = Space(k.arena, k.ROUTE_END, k.BIG1)
    wr, bias, ones = w.f32(2, NE), w.f32(NE), w.f32(P)
    xm, x1, xn, g1 = w.f32(2, D), w.f32(2, D), w.f32(2, D), w.f32(2, D)
    den, inv_den, stat = w.f32(2, GH), w.f32(2, GH), w.f32(2, 16)
    top, ssum, sinv = w.f32(NB), w.f32(NB), w.f32(NB)
    ps = k.ps
    with ExitStack() as ctx:
        s = sems(nc, k, "norm2", "passed weights set x_in0 x_in1 den inv_den g1 x1 stats mean var root inv xn xT_ps xT "
                 "logit_ps logit out0 out1 d e")
        x_in, out = (s["x_in0"], s["x_in1"]), (s["out0"], s["out1"])
        block = ctx.enter_context(nc.Block())

        @block.sync
        def _(sp):
            sp.dma_start(wr, k.route_w).then_inc(s["weights"], 16)
            sp.dma_start(bias[0:1, :], k.route_bias).then_inc(s["weights"], 16)
            for i in rounds(sp, NB // 2):
                for u in (0, 1):
                    b = 2 * i + u
                    need(sp, s["x1"], b - 1)
                    sp.dma_start(xm[:, u, :], k.xm_rows[bass.ds(b * P, P), :]).then_inc(x_in[u], 16)

        @block.gpsimd
        def _(pool):
            for i in rounds(pool, NB // 2):
                for u in (0, 1):
                    b = 2 * i + u
                    pool.wait_ge(s["x1"], b + 1)
                    pool.dma_start(k.x1_rows[bass.ds(b * P, P), :], x1[:, u, :]).then_inc(out[u], 16)
            for u in (0, 1):
                pool.wait_ge(out[u], 16 * (NB // 2))

        @block.tensor
        def _(pe):
            pe.wait_ge(s["weights"], 32)
            pe.wait_ge(s["set"], 1)
            for i in rounds(pe, NB // 2):
                for u in (0, 1):
                    b = 2 * i + u
                    pe.wait_ge(s["xn"], b + 1)
                    need(pe, s["xT"], b)
                    for c in range(2):
                        mm = pe.transpose(ps[:, 0, c * P:(c + 1) * P], xn[:, u, c * P:(c + 1) * P], k.ident)
                    mm.then_inc(s["xT_ps"], 1)
                    pe.wait_ge(s["xT"], b + 1)
                    need(pe, s["logit"], b - 1)
                    for c in range(2):
                        pe.matmul(ps[0:NE, 1 + u, 0:P], wr[:, c, :], k.x2T[:, c, bass.ds(b * P, P)], start=(c == 0),
                                  stop=False)
                    pe.matmul(ps[0:NE, 1 + u, 0:P], bias[0:1, :], ones[0:1, :], start=False,
                              stop=True).then_inc(s["logit_ps"], 1)

        @block.scalar
        def _(act):
            def logits(b, u):
                act.wait_ge(s["logit_ps"], b + 1)
                act.copy(k.logit_T[0:NE, bass.ds(b * P, P)], ps[0:NE, 1 + u, 0:P]).then_inc(s["logit"], 1)

            for i in rounds(act, NB // 2):
                for u in (0, 1):
                    b = 2 * i + u
                    act.wait_ge(s["var"], b + 1)
                    act.activation(stat[:, u, 9:10], stat[:, u, 8:9], ACT.Sqrt).then_inc(s["root"], 1)
                    if not (isinstance(b, int) and b == 0):
                        logits(b - 1, 1 - u)
                    act.wait_ge(s["xT_ps"], b + 1)
                    act.copy(k.x2T[:, :, bass.ds(b * P, P)], split(ps[:, 0, 0:2 * P], (2, P))).then_inc(s["xT"], 1)
            logits(NB - 1, 1)

        @block.vector
        def _(dve):
            dve.memset(ones, 1.0).then_inc(s["set"], 1)
            for i in rounds(dve, NB // 2):
                for u in (0, 1):
                    b = 2 * i + u
                    acc = k.acc[:, bass.ds(b, 1), :].rearrange("p o w -> p (o w)")
                    dve.tensor_scalar(den[:, u, :], acc[:, D:], 1e-16, None, ALU.add).then_inc(s["den"], 1)
                    dve.wait_ge(s["den"], b + 1)
                    dve.reciprocal(inv_den[:, u, :], den[:, u, :]).then_inc(s["inv_den"], 1)
                    dve.wait_ge(s["inv_den"], b + 1)
                    dve.tensor_tensor(split(g1[:, u, :], (GH, 16)), split(acc[:, 0:D], (GH, 16)),
                                      over(inv_den[:, u, :], (1, GH), (0, 16)), ALU.mult).then_inc(s["g1"], 1)
                    dve.wait_ge(s["g1"], b + 1)
                    dve.wait_ge(x_in[u], 16 * (i + 1))
                    need(dve, out[u], 16 * i)
                    dve.tensor_tensor(x1[:, u, :], g1[:, u, :], xm[:, u, :], ALU.add).then_inc(s["x1"], 1)
                    dve.wait_ge(s["x1"], b + 1)
                    dve.bn_stats(stat[:, u, 0:6], x1[:, u, :]).then_inc(s["stats"], 1)
                    dve.wait_ge(s["stats"], b + 1)
                    dve.sem_inc(s["passed"])
                    dve.bn_aggr(stat[:, u, 6:8], stat[:, u, 0:6]).then_inc(s["mean"], 1)
                    dve.wait_ge(s["mean"], b + 1)
                    dve.tensor_scalar(stat[:, u, 8:9], stat[:, u, 7:8], 1e-5, None, ALU.add).then_inc(s["var"], 1)
                    dve.wait_ge(s["root"], b + 1)
                    dve.reciprocal(stat[:, u, 10:11], stat[:, u, 9:10]).then_inc(s["inv"], 1)
                    dve.wait_ge(s["inv"], b + 1)
                    need(dve, s["xT_ps"], b - 1)
                    dve.tensor_scalar(xn[:, u, :], x1[:, u, :], stat[:, u, 6:7], stat[:, u, 10:11],
                                      ALU.subtract, ALU.mult).then_inc(s["xn"], 1)


def phase_route(nc, k):
    w = Space(k.arena, k.ROUTE_END, k.BIG1)
    top, ssum, sinv = w.f32(NB), w.f32(NB), w.f32(NB)
    low = w.f32(NB, NE)
    v = [w.f32(16) for _ in range(8)]
    ps = k.ps
    with ExitStack() as ctx:
        s = sems(nc, k, "route", "turned low ex d turn_w wT bn root bn_in")
        block = ctx.enter_context(nc.Block())

        @block.sync
        def _(sp):
            for n, src in enumerate(k.bn):
                sp.dma_start(k.bn_sb[:, n, :], src).then_inc(s["bn_in"], 16)

        @block.tensor
        def _(pe):
            for b in range(NB):
                mm = pe.transpose(ps[:, 0, b * NE:(b + 1) * NE], k.logit_T[0:NE, b * P:(b + 1) * P],
                                  k.ident[0:NE, 0:NE])
            mm.then_inc(s["turned"], 1)
            pe.wait_ge(s["d"], 4)
            for b in range(NB):
                n = b // 4
                if n >= 2 and b % 4 == 0:
                    pe.wait_ge(s["wT"], n - 1)
                mm = pe.transpose(ps[0:NE, 1 + n % 2, (b % 4) * P:(b % 4 + 1) * P], k.gate[:, b, :], k.ident)
                if b % 4 == 3 or b == NB - 1:
                    mm.then_inc(s["turn_w"], 1)

        @block.scalar
        def _(act):
            act.wait_ge(s["low"], 1)
            act.activation(low, low, ACT.Exp).then_inc(s["ex"], 1)
            act.wait_ge(s["bn"], 2)
            act.activation(v[0], v[1], ACT.Sqrt)
            act.activation(v[2], v[3], ACT.Sqrt).then_inc(s["root"], 1)
            for n in range((NB + 3) // 4):
                m = min(4, NB - 4 * n) * P
                act.wait_ge(s["turn_w"], n + 1)
                act.copy(k.logit_T[0:NE, 4 * n * P:4 * n * P + m], ps[0:NE, 1 + n % 2, 0:m]).then_inc(s["wT"], 1)

        @block.vector
        def _(dve):
            done = 0

            def then(ins):
                nonlocal done
                done += 1
                ins.then_inc(s["d"], 1)
                dve.wait_ge(s["d"], done)

            logit = split(ps[:, 0, 0:NB * NE], (NB, NE))
            dve.wait_ge(s["turned"], 1)
            then(dve.tensor_reduce(top, logit, AX, ALU.max))
            dve.tensor_tensor(low, logit, over(top, (1, NB), (0, NE)), ALU.subtract).then_inc(s["low"], 1)
            dve.wait_ge(s["ex"], 1)
            then(dve.tensor_reduce(ssum, low, AX, ALU.add))
            then(dve.reciprocal(sinv, ssum))
            then(dve.tensor_tensor(k.gate, low, over(sinv, (1, NB), (0, NE)), ALU.mult))
            dve.wait_ge(s["bn_in"], 16 * 10)
            for layer in (0, 1):
                dve.tensor_scalar(v[1 + 2 * layer], k.bn_sb[:, 5 * layer + 4, :], 1e-3, None,
                                  ALU.add).then_inc(s["bn"], 1)
            dve.wait_ge(s["root"], 1)
            for layer in (0, 1):
                bias, gain, shift, mean, _var = (k.bn_sb[:, 5 * layer + n, :] for n in range(5))
                then(dve.reciprocal(v[4], v[2 * layer]))
                then(dve.tensor_tensor(k.scale[:, layer, :], gain, v[4], ALU.mult))
                then(dve.tensor_tensor(v[5], bias, mean, ALU.subtract))
                then(dve.tensor_tensor(v[6], v[5], k.scale[:, layer, :], ALU.mult))
                then(dve.tensor_tensor(k.shift[:, layer, :], v[6], shift, ALU.add))


def phase_experts(nc, k):
    w = Space(k.arena, k.ROUTE_END, k.BIG1)
    w1, w2 = w.f32(NE, 2, D), w.f32(NE, 2, D)
    h1, h2 = w.f32(2, CB * P), w.f32(2, CB * P)
    bo, gate_T = w.f32(D), w.f32(CB * P)
    y, x1 = w.f32(CB, D), w.f32(CB, D)
    w3 = split(k.acc_words[:, 0:NE * 2 * D], (NE, 2, D))
    HALF = CB * P // 2
    ps = k.ps
    ROUNDS = NB // CB
    with ExitStack() as ctx:
        s = sems(nc, k, "experts", "weights x_in h_ps h y_ps y out gate seed_ps seed")
        block = ctx.enter_context(nc.Block())

        @block.sync
        def _(sp):
            for dst, src in ((w1, k.w1), (w2, k.w2), (w3, k.w3)):
                sp.dma_start(dst, src).then_inc(s["weights"], 16)
            sp.dma_start(bo[0:NE, :], k.out_bias).then_inc(s["weights"], 16)
            for r in rounds(sp, ROUNDS):
                need(sp, s["seed"], CB * r)
                sp.dma_start(x1, k.x1_rows[bass.ds(r * CB * P, CB * P), :].rearrange("(n p) d -> p n d", p=P)
                             ).then_inc(s["x_in"], 16)
                sp.wait_ge(s["y"], NE * CB * (r + 1))
                sp.dma_start(k.out[bass.ds(r * CB * P, CB * P), :].rearrange("(n p) d -> p n d", p=P), y
                             ).then_inc(s["out"], 16)
            sp.wait_ge(s["out"], 16 * ROUNDS)

        @block.tensor
        def _(pe):
            def hidden(r, e, layer, wt):
                for ot in (0, 1):
                    m = 4 * e + 2 * layer + ot
                    need(pe, s["h"], 4 * NE * r + m - 1)
                    for half in (0, 1):
                        for c in (0, 1):
                            if layer == 0:
                                moving = k.x2T[:, c, bass.ds(r * CB * P + half * HALF, HALF)]
                            else:
                                moving = h1[:, c, half * HALF:(half + 1) * HALF]
                            mm = pe.matmul(ps[:, 2 * (m % 2) + half, 0:HALF], wt[:, e, c, ot * P:(ot + 1) * P],
                                           moving, start=(c == 0), stop=(c == 1))
                    mm.then_inc(s["h_ps"], 1)

            def last(r, e):
                pe.wait_ge(s["h"], 4 * NE * r + 4 * e + 4)
                for nb in range(CB):
                    need(pe, s["y"], CB * NE * r + CB * e + nb - 3)
                    bank = 4 + (CB * e + nb) % 4
                    for c in (0, 1):
                        mm = pe.matmul(ps[:, bank, 0:D], h2[:, c, nb * P:(nb + 1) * P], w3[:, e, c, :],
                                       start=(c == 0), stop=(c == 1))
                    mm.then_inc(s["y_ps"], 1)

            pe.wait_ge(s["weights"], 64)
            for r in rounds(pe, ROUNDS):
                need(pe, s["y"], NE * CB * r)
                pe.wait_ge(s["gate"], r + 1)
                for nb in range(CB):
                    need(pe, s["seed"], CB * r + nb)
                    pe.matmul(ps[:, 4, 0:D], gate_T[0:NE, nb * P:(nb + 1) * P], bo[0:NE, :], start=True,
                              stop=True).then_inc(s["seed_ps"], 1)
                need(pe, s["seed"], CB * r + CB)
                for e in range(NE):
                    hidden(r, e, 0, w1)
                    if e >= 1:
                        last(r, e - 1)
                    pe.wait_ge(s["h"], 4 * NE * r + 4 * e + 2)
                    hidden(r, e, 1, w2)
                last(r, NE - 1)

        @block.scalar
        def _(act):
            for r in rounds(act, ROUNDS):
                need(act, s["seed_ps"], CB * r)
                act.copy(gate_T[0:NE, :], k.logit_T[0:NE, bass.ds(r * CB * P, CB * P)]).then_inc(s["gate"], 1)
                for e in range(NE):
                    for layer in (0, 1):
                        for ot in (0, 1):
                            m = 4 * e + 2 * layer + ot
                            act.wait_ge(s["h_ps"], 4 * NE * r + m + 1)
                            if layer == 1:
                                need(act, s["y_ps"], CB * NE * r + CB * e)
                            act.activation(split((h1, h2)[layer][:, ot], (2, HALF)),
                                           ps[:, 2 * (m % 2):2 * (m % 2) + 2, 0:HALF], ACT.Relu,
                                           bias=k.shift[:, layer, 2 * e + ot:2 * e + ot + 1],
                                           scale=k.scale[:, layer, 2 * e + ot:2 * e + ot + 1]).then_inc(s["h"], 1)

        @block.vector
        def _(dve):
            for r in rounds(dve, ROUNDS):
                dve.wait_ge(s["x_in"], 16 * (r + 1))
                need(dve, s["out"], 16 * r)
                for nb in range(CB):
                    dve.wait_ge(s["seed_ps"], CB * r + nb + 1)
                    dve.tensor_tensor(y[:, nb, :], ps[:, 4, 0:D], x1[:, nb, :], ALU.add).then_inc(s["seed"], 1)
                dve.wait_ge(s["seed"], CB * r + CB)
                for e in range(NE):
                    for nb in range(CB):
                        n = CB * NE * r + CB * e + nb
                        dve.wait_ge(s["y_ps"], n + 1)
                        need(dve, s["y"], n - CB + 1)
                        gate = k.gate[:, bass.ds(r * CB + nb, 1), e:e + 1].rearrange("p a b -> p (a b)")
                        dve.scalar_tensor_tensor(y[:, nb, :], ps[:, 4 + (CB * e + nb) % 4, 0:D], gate, y[:, nb, :],
                                                 ALU.mult, ALU.add).then_inc(s["y"], 1)


def build(nc, x, src_lin, src_col, dst_col, attr, consts, gnn_w, mix_w, node_bias, temperature, proj_w, proj_bias,
          rpe_w, route_w, route_bias, w1, w2, w3, out_bias, bn, out, upto=99, probes=None):
    k = Shared()
    k.x, k.src_lin, k.src_col, k.dst_col, k.attr = x, src_lin, src_col, dst_col, attr
    k.consts, k.gnn_w, k.mix_w, k.node_bias, k.temperature = consts, gnn_w, mix_w, node_bias, temperature
    k.proj_w, k.proj_bias, k.rpe_w, k.route_w, k.route_bias = proj_w, proj_bias, rpe_w, route_w, route_bias
    k.w1, k.w2, k.w3, k.out_bias, k.bn = w1, w2, w3, out_bias, bn
    k.out = out
    scratch = lambda n, shape, dt=F32: nc.dram_tensor(n, shape, dt).ap()
    k.row_s, k.row_lo = scratch("row_s", [EP]), scratch("row_lo", [EP], BF16)
    k.records = scratch("records", [SLOTS, REC])
    k.k_rows, k.v_rows = scratch("k_rows", [NP, P]), scratch("v_rows", [NP, D])
    k.kext_rows, k.v1_rows = scratch("kext_rows", [NP, MH * 48]), scratch("v1_rows", [NP, MH * 33])
    k.qT_rows = scratch("qT_rows", [NB * 97, MH * P], BF16)
    k.xm_rows, k.x1_rows = scratch("xm_rows", [NP, D]), scratch("x1_rows", [NP, D])
    with ExitStack() as ctx:
        q_words, breaks_words, score_words, acc_words = NB * 3 * P // 2, STEPS * P // 2 + 16, STEPS * P, NB * (D + GH)
        total = 53200
        arena = ctx.enter_context(nc.sbuf_tensor("arena", [P, total], F32))
        k.arena = arena
        k.sems = []
        c = Space(arena, 0, total)
        k.cst = c.f32(C_END + C_END % 2)[:, 0:C_END]
        k.ident_b, k.iota_b, k.sel_b = c.bf16(P), c.bf16(P), c.bf16(7, P)
        k.start, k.blocks = c.f32(NB), c.f32(CH * STEPS, dt=I32)
        k.ident = k.cst[:, C_ID:C_ID + P]
        k.Q0 = c.at
        k.WORK0 = k.Q0 + q_words
        big2 = total - acc_words
        k.BIG1 = big2 - score_words
        fl0 = k.BIG1 - breaks_words
        k.COLS0 = total - 4 * ET
        k.MT0 = k.COLS0 - 20 * P
        k.FL0 = fl0
        at = lambda a, b: Space(arena, a, b)
        k.qtab = at(k.Q0, k.WORK0).bf16(NB, 3, P)
        k.cols = at(k.COLS0, total).f32(4, ET)
        k.mt = at(k.MT0, k.COLS0).f32(20, P)
        k.breaks = at(fl0, k.BIG1).bf16(STEPS * P + 2)
        k.scores = at(k.BIG1, big2).f32(STEPS * P)
        k.x2T = at(k.BIG1, big2).f32(2, NP)
        k.owner = at(big2, total).f32(STEPS * P)
        k.acc_words = at(big2, total).f32(acc_words)
        k.acc = split(k.acc_words, (NB, D + GH))
        r = at(k.Q0, k.BIG1)
        k.gate, k.logit_T, k.scale, k.shift, k.bn_sb = (r.f32(NB, NE), r.f32(NP), r.f32(2, 16), r.f32(2, 16),
                                                       r.f32(10, 16))
        k.ROUTE_END = r.at
        psum = ctx.enter_context(nc.psum_tensor("banks", [P, 8, 512], F32))
        k.ps = psum[:, :, :]
        k.ps_b = psum[:, :, :].rearrange("p b w -> p (b w)").bitcast(BF16).rearrange("p (b w) -> p b w", b=8)
        phases = [phase_setup, phase_nodes, phase_kv_sums, phase_mix_out, phase_histogram, phase_starts,
                  phase_scatter, phase_compat, phase_seg_max, phase_messages, phase_norm2, phase_route,
                  phase_experts]
        for n, phase in enumerate(phases[:upto]):
            phase(nc, k)
            if phase is phase_scatter or n == len(phases) - 1:
                nc.clear_and_free_semaphores(k.sems)
                nc.all_engine_barrier()
                k.sems = []
        if probes:
            probes(nc, k)


def layout(inputs):
    a = {n: np.asarray(v) for n, v in inputs.items()}
    f = np.float32
    pad_rows = lambda v, n, fill=0: np.concatenate([v, np.full((n - v.shape[0],) + v.shape[1:], fill, v.dtype)])
    src = pad_rows(a["src"], EP, FAKE)
    dst = pad_rows(a["dst"], EP)
    attr = pad_rows(a["edge_attr_18"], EP)
    tiles = lambda v: np.ascontiguousarray(v.reshape(ET, P, *v.shape[1:]).swapaxes(0, 1))
    inner = lambda wt: np.ascontiguousarray(wt.reshape(2, P, -1).swapaxes(0, 1))
    experts = lambda wt: np.ascontiguousarray(wt.reshape(NE, 2, P, D).transpose(2, 0, 1, 3))
    units = lambda v: np.ascontiguousarray(v.reshape(NE, 2, P).transpose(2, 0, 1).reshape(P, 2 * NE))
    row = lambda v: np.ascontiguousarray(v.reshape(1, -1))
    one = np.concatenate([np.concatenate([a["L0_gnn_Wq_rpe"], a["L0_gnn_Wk_rpe"]], 1),
                          np.concatenate([row(a["L0_gnn_bq_rpe"]), row(a["L0_gnn_bk_rpe"])], 1),
                          np.zeros((REC - 19, 2 * P), f)])
    rpe = np.zeros((4, REC, 4, 2 * P), f)
    for j in range(4):
        rpe[j, :, j] = one
    r = {
        "x": pad_rows(a["x"], NP), "src_lin": src.reshape(P, ET), "src_col": tiles(src), "dst_col": tiles(dst),
        "attr": tiles(attr), "consts": constants(),
        "gnn_w": inner(a["L0_gnn_Wqkv"]), "mix_w": inner(a["L0_mix_Wqkv"].T),
        "node_bias": np.concatenate([row(a["L0_gnn_bqkv"]), row(a["L0_mix_bqkv"])], 1),
        "temperature": row(a["L0_mix_temperature"]),
        "proj_w": inner(a["L0_mix_Wproj"].T), "proj_bias": row(a["L0_mix_bproj"]),
        "rpe_w": rpe.reshape(P, 4, 2 * P),
        "route_w": inner(a["L0_ffn_Wr"]), "route_bias": row(a["L0_ffn_br"]),
        "w1": experts(a["L0_ffn_W1"]), "w2": experts(a["L0_ffn_W2"]), "w3": experts(a["L0_ffn_Wo"]),
        "out_bias": a["L0_ffn_bo"],
    }
    for layer in ("1", "2"):
        for n in ("b", "g", "be", "m", "v"):
            r[f"bn_{n}{layer}"] = units(a[f"L0_ffn_{n}{layer}"])
    return {n: np.ascontiguousarray(v) for n, v in r.items()}


def kernel(**inputs):
    import concourse.bacc as bacc
    from concourse.bass_utils import run_bass_kernel_spmd

    arrays = layout(inputs)
    nc = bacc.Bacc("TRN2", target_bir_lowering=False, num_devices=1)
    args = {n: nc.dram_tensor(f"in_{n}", v.shape, mybir.dt.from_np(v.dtype), kind="ExternalInput").ap()
            for n, v in arrays.items()}
    out = nc.dram_tensor("out", [NP, D], F32, kind="ExternalOutput").ap()
    bn = [args.pop(n) for n in list(args) if n.startswith("bn_")]
    build(nc, **args, bn=bn, out=out)
    result = run_bass_kernel_spmd(nc, [{f"in_{n}": v for n, v in arrays.items()}], core_ids=[0])
    return result.results[0]["out"][:N]
```

```python
from contextlib import ExitStack

import numpy as np

import concourse.bass as bass
from concourse import mybir

F32 = mybir.dt.float32
BF16 = mybir.dt.bfloat16
I32 = mybir.dt.int32
ALU = mybir.AluOpType
ACT = mybir.ActivationFunctionType
AX = mybir.AxisListType.X
ENG = mybir.EngineType

P = 128
N, D = 6250, 256
NB = 49
NP = NB * P
E = 100000
ET = 784
EP = ET * P
FAKE = NB * P - 1
CH = 8
STEPS = 104
SLOTS = CH * STEPS * P
REC = 32
R_ONE, R_T, R_S, R_LO = 18, 19, 20, 21
GH, GD = 16, 8
MH, MD = 8, 32
ND = 17
PAIRS = ND * MD + MD + 1
NE = 8
CB = 7
NEG = -1.0e38
MSCALE = float(MD) ** 0.25

C_ID, C_IOTA, C_BEFORE, C_AFTER = 0, 128, 256, 384
C_SEL = 512
C_P = C_SEL + 7 * 128
C_MASK = C_P + 1
C_TILE = C_MASK + NB
C_END = C_TILE + CH * STEPS


def constants():
    c = np.zeros((P, C_END), np.float32)
    r = np.arange(P)
    c[:, C_ID:C_ID + P] = np.eye(P)
    c[:, C_IOTA:C_IOTA + P] = r[None, :]
    c[:, C_BEFORE:C_BEFORE + P] = r[None, :] < r[:, None]
    c[:, C_AFTER:C_AFTER + P] = r[:, None] < r[None, :]
    sel = c[:, C_SEL:C_SEL + 7 * P].reshape(P, 7, P)
    i = np.arange(MD)
    for part in range(3):
        for dd in range(4):
            sel[part * MD + i, 0, dd * MD + i] = 1
            for j in range(4):
                sel[part * MD + (i + 4 * j + dd) % MD, 1 + j, dd * MD + i] = 1
        sel[part * MD + i, 5, i] = 1
        sel[part * MD + (i + 16) % MD, 6, i] = 1
        sel[part * MD + i, 6, MD + i] = 1
    sel[96, 5, MD:2 * MD + 1] = 1
    sel[96, 6, 2 * MD] = 1
    c[:, C_P] = r
    node = np.arange(NP).reshape(NB, P).T
    c[:, C_MASK:C_MASK + NB] = (node < N) / np.float32(N)
    tile = np.arange(CH)[None, :] * STEPS + np.arange(STEPS)[:, None]
    c[:, C_TILE:C_END] = tile.reshape(-1)[None, :]
    return c


class Space:

    def __init__(self, arena, at, end):
        self.arena, self.at, self.end = arena, at, end

    def f32(self, *shape, dt=None):
        n = int(np.prod(shape))
        assert self.at + n <= self.end, (self.at, n, self.end)
        ap = self.arena[:, self.at:self.at + n]
        self.at += n
        if dt is not None:
            ap = ap.bitcast(dt)
        return split(ap, shape)

    def bf16(self, *shape):
        n = int(np.prod(shape))
        assert n % 2 == 0 and self.at + n // 2 <= self.end, (self.at, n, self.end)
        ap = self.arena[:, self.at:self.at + n // 2].bitcast(BF16)
        self.at += n // 2
        return split(ap, shape)


def split(ap, shape):
    if len(shape) == 1:
        return ap
    names = "abcd"[:len(shape)]
    return ap.rearrange(f"p ({' '.join(names)}) -> p {' '.join(names)}",
                        **{k: v for k, v in zip(names[1:], shape[1:])})


def over(ap, *dims):
    return bass.AP(tensor=ap.tensor, offset=ap.offset, ap=[list(ap.ap[0]), *[list(d) for d in dims]])


class Shared:
    pass


def rounds(eng, n):
    yield 0
    with eng.Fori(1, n) as i:
        yield i


def fours(eng, n):
    for v in range(4):
        yield v, v
    with eng.Fori(1, n // 4) as i:
        for v in range(4):
            yield 4 * i + v, v


def blocks(eng):
    yield 0, 0
    yield 1, 1
    with eng.Fori(1, NB // 2) as i:
        for u in (0, 1):
            yield 2 * i + u, u
    yield NB - 1, 0


def at_start(b, n):
    return isinstance(b, int) and b < n


def need(eng, sem, value):
    if isinstance(value, int) and value <= 0:
        return
    eng.wait_ge(sem, value)


def sems(nc, k, phase, names):
    s = {n: nc.alloc_semaphore(f"{phase}_{n}") for n in names.split()}
    k.sems += s.values()
    return s


def one_hot_rows(k, dve, low, high, n):
    col = lambda row: k.cols[:, row, bass.ds(n * 8, 8)].rearrange("p (j o) -> p j o", o=1)
    dve.tensor_tensor(high, over(k.iota_b[:, 0:NB], (0, 8), (1, NB)), col(3).to_broadcast([P, 8, NB]), ALU.is_equal)
    return dve.tensor_tensor(low, over(k.iota_b, (0, 8), (1, P)), col(2).to_broadcast([P, 8, P]), ALU.is_equal)


def phase_setup(nc, k):
    w = Space(k.arena, k.WORK0, k.BIG2)
    lin, scol_i, tcol_i, half = (w.f32(ET, dt=I32) for _ in range(4))
    bias = w.f32(k.bias3.shape[1])
    rest, part2, part3 = w.f32(k.bias3.shape[1]), w.bf16(k.bias3.shape[1]), w.bf16(k.bias3.shape[1])
    kept = Space(k.arena, k.BIG2, k.MT0)
    slin, llin, blank = kept.f32(ET), kept.bf16(ET), kept.f32(64, REC)
    with ExitStack() as ctx:
        s = sems(nc, k, "setup", "loaded low_row ints blanked stored consts bias parts moved")
        k.rows_stored, k.blanks_stored = nc.alloc_semaphore("rows_stored"), nc.alloc_semaphore("blanks_stored")
        k.sems += [k.rows_stored, k.blanks_stored]
        block = ctx.enter_context(nc.Block())

        @block.sync
        def _(sp):
            sp.dma_start(scol_i, k.src_col).then_inc(s["loaded"], 16)
            sp.dma_start(lin, k.src_lin).then_inc(s["loaded"], 16)
            sp.dma_start(tcol_i, k.dst_col).then_inc(s["loaded"], 16)
            sp.dma_start(bias[0:1, 0:1280], k.node_bias).then_inc(s["bias"], 16)
            sp.dma_start(bias[0:1, 1280:], k.proj_bias).then_inc(s["bias"], 16)
            sp.dma_start(k.cst, k.consts).then_inc(s["consts"], 16)
            sp.wait_ge(s["parts"], 4)
            sp.dma_start(k.bias3[1:2, :], part2[0:1, :]).then_inc(s["moved"], 16)
            sp.dma_start(k.bias3[2:3, :], part3[0:1, :]).then_inc(s["moved"], 16)
            sp.wait_ge(s["low_row"], 2)
            sp.dma_start(k.row_s.rearrange("(p c) -> p c", p=P), slin).then_inc(k.rows_stored, 16)
            sp.dma_start(k.row_lo.rearrange("(p c) -> p c", p=P), llin).then_inc(k.rows_stored, 16)
            sp.wait_ge(s["blanked"], 2)
            for n in range(SLOTS // (64 * P)):
                sp.dma_start(k.records[n * 64 * P:(n + 1) * 64 * P, :].rearrange("(p r) f -> p r f", p=P),
                             blank).then_inc(k.blanks_stored, 16)
            sp.wait_ge(s["moved"], 32)

        @block.scalar
        def _(act):
            act.wait_ge(s["consts"], 16)
            act.copy(k.ident_b, k.cst[:, C_ID:C_ID + P])
            act.copy(k.iota_b, k.cst[:, C_IOTA:C_IOTA + P])
            act.copy(k.sel_b, split(k.cst[:, C_SEL:C_SEL + 7 * P], (7, P)))

        @block.vector
        def _(dve):
            dve.memset(k.ones_b, 1.0)
            dve.memset(blank, 0.0).then_inc(s["blanked"], 1)
            dve.wait_ge(s["blanked"], 1)
            dve.memset(blank[:, :, R_S:R_S + 2], 300.0).then_inc(s["blanked"], 1)
            dve.wait_ge(s["bias"], 32)
            dve.tensor_copy(k.bias3[0:1, :], bias[0:1, :]).then_inc(s["parts"], 1)
            dve.wait_ge(s["parts"], 1)
            dve.tensor_tensor(rest[0:1, :], bias[0:1, :], k.bias3[0:1, :], ALU.subtract).then_inc(s["parts"], 1)
            dve.wait_ge(s["parts"], 2)
            dve.tensor_copy(part2[0:1, :], rest[0:1, :]).then_inc(s["parts"], 1)
            dve.wait_ge(s["parts"], 3)
            dve.tensor_tensor(part3[0:1, :], rest[0:1, :], part2[0:1, :], ALU.subtract).then_inc(s["parts"], 1)
            dve.wait_ge(s["loaded"], 48)
            dve.tensor_copy(slin, lin).then_inc(s["low_row"], 1)
            dve.tensor_scalar(half, lin, 127, None, ALU.bitwise_and).then_inc(s["ints"], 1)
            dve.wait_ge(s["ints"], 1)
            dve.tensor_copy(llin, half).then_inc(s["low_row"], 1)
            dve.tensor_copy(k.cols[:, 0], tcol_i)
            dve.tensor_copy(k.cols[:, 1], scol_i)
            dve.wait_ge(s["low_row"], 2)
            dve.tensor_scalar(half, scol_i, 127, None, ALU.bitwise_and).then_inc(s["ints"], 1)
            dve.wait_ge(s["ints"], 2)
            dve.tensor_copy(k.cols[:, 2], half).then_inc(s["ints"], 1)
            dve.wait_ge(s["ints"], 3)
            dve.tensor_scalar(half, scol_i, 7, None, ALU.arith_shift_right).then_inc(s["ints"], 1)
            dve.wait_ge(s["ints"], 4)
            dve.tensor_copy(k.cols[:, 3], half)


def phase_nodes(nc, k):
    w = Space(k.arena, k.WORK0, k.BIG2)
    wg, wm = w.f32(2, 512), w.f32(2, 768)
    ones, factor = w.f32(P), w.f32(16)
    low, high, zero = w.bf16(4, 8, P), w.bf16(4, 8, NB), w.bf16(P)
    xb, xn, xT = w.f32(2, D), w.f32(2, D), w.f32(2, 2, P)
    stat, gnn = w.f32(2, 16), w.f32(2, 512)
    qs, rest = w.f32(2, P), w.f32(2, P)
    mix, sq = w.f32(2, 24, MD), w.f32(2, 16, MD)
    nrm = w.f32(2, 5, 16)
    kext, v1, qn, qrest = w.f32(2, MH, 48), w.f32(2, MH, 33), w.f32(2, MH, MD), w.f32(2, MH, MD)
    parts, qTs = w.bf16(2, MH, 98), w.bf16(2, MH, P)
    ps = k.ps
    with ExitStack() as ctx:
        s = sems(nc, k, "nodes", "passed weights set x_in0 x_in1 stats mean var root_v inv xn xT_ps xT proj gnn mixed "
                 "squared qpart v1 norm2 root_n clip recip factor normed split qT_ps qT "
                 "k_out0 k_out1 v_out0 v_out1 e_out0 e_out1 w_out0 w_out1 q_out0 q_out1 hot hist")
        x_in, k_out, v_out, e_out, w_out, q_out = (
            (a, b) for a, b in ((s["x_in0"], s["x_in1"]), (s["k_out0"], s["k_out1"]), (s["v_out0"], s["v_out1"]),
                                (s["e_out0"], s["e_out1"]), (s["w_out0"], s["w_out1"]), (s["q_out0"], s["q_out1"])))
        block = ctx.enter_context(nc.Block())

        @block.sync
        def _(sp):
            sp.dma_start(wg, k.gnn_w).then_inc(s["weights"], 16)
            sp.dma_start(wm, k.mix_w).then_inc(s["weights"], 16)
            sp.dma_start(factor[:, 0:MH], k.temperature.to_broadcast([P, MH])).then_inc(s["weights"], 16)
            for b, u in blocks(sp):
                need(sp, s["xn"], b - 1)
                sp.dma_start(xb[:, u, :], k.x[bass.ds(b * P, P), :]).then_inc(x_in[u], 16)

        @block.gpsimd
        def _(pool):
            for b, u in blocks(pool):
                pool.wait_ge(s["gnn"], b + 1)
                pool.dma_start(k.k_rows[bass.ds(b * P, P), :], gnn[:, u, P:2 * P]).then_inc(k_out[u], 16)
                pool.dma_start(k.v_rows[bass.ds(b * P, P), :], gnn[:, u, 2 * P:]).then_inc(v_out[u], 16)
                pool.wait_ge(s["v1"], 2 * b + 2)
                pool.dma_start(k.v1_rows[bass.ds(b * P, P), :],
                               v1[:, u].rearrange("p h i -> p (h i)")).then_inc(w_out[u], 16)
                pool.wait_ge(s["normed"], 3 * b + 3)
                pool.dma_start(k.kext_rows[bass.ds(b * P, P), :],
                               kext[:, u].rearrange("p h i -> p (h i)")).then_inc(e_out[u], 16)
                pool.wait_ge(s["qT"], b + 1)
                pool.dma_start(k.qT_rows[bass.ds(b * 97, 97), :],
                               qTs[0:97, u].rearrange("p h i -> p (h i)")).then_inc(q_out[u], 16)
            for u in (0, 1):
                for sem in (k_out[u], v_out[u], w_out[u], e_out[u], q_out[u]):
                    pool.wait_ge(sem, 16 * ((NB + 1 - u) // 2))

        @block.tensor
        def _(pe):
            def histogram(b, u):
                for half in (0, 1):
                    pe.wait_ge(s["hot"], 2 * b + half + 1)
                    for j in range(8):
                        mm = pe.matmul(ps[:, 5, 0:NB], low[:, 2 * u + half, j, :], high[:, 2 * u + half, j, :],
                                       start=False, stop=False, skip_group_check=True)
                    mm.then_inc(s["hist"], 1)

            def queries_T(b, u):
                pe.wait_ge(s["split"], 4 * b + 4)
                need(pe, s["qT"], b)
                for h in range(MH):
                    mm = pe.transpose(k.ps_b[0:97, 4, h * P:(h + 1) * P], parts[:, u, h, 0:97], k.ident_b)
                mm.then_inc(s["qT_ps"], 1)

            pe.wait_ge(s["weights"], 48)
            pe.wait_ge(s["set"], 1)
            pe.matmul(ps[:, 5, 0:NB], zero, zero[:, 0:NB], start=True, stop=False, skip_group_check=True)
            for b, u in blocks(pe):
                pe.wait_ge(s["xn"], b + 1)
                need(pe, s["xT"], b)
                for c in range(2):
                    mm = pe.transpose(ps[:, 0, c * P:(c + 1) * P], xn[:, u, c * P:(c + 1) * P], k.ident)
                mm.then_inc(s["xT_ps"], 1)
                if not at_start(b, 1):
                    histogram(b - 1, 1 - u)
                pe.wait_ge(s["xT"], b + 1)
                need(pe, s["mixed"], 3 * b)
                for bank, wt, c0, n, at in ((1, wg, 0, 512, 0), (2, wm, 0, 512, 512), (3, wm, 512, 256, 1024)):
                    for c in range(2):
                        pe.matmul(ps[:, bank, 0:n], xT[:, u, c, :], wt[:, c, c0:c0 + n],
                                  start=(c == 0), stop=False)
                    mm = pe.matmul(ps[:, bank, 0:n], k.ones_b[0:3, :], k.bias3[0:3, at:at + n],
                                   start=False, stop=True)
                mm.then_inc(s["proj"], 1)
                if not at_start(b, 1):
                    queries_T(b - 1, 1 - u)
            histogram(NB - 1, 0)
            queries_T(NB - 1, 0)

        @block.scalar
        def _(act):
            def root_of_norms(b, u):
                act.wait_ge(s["norm2"], b + 1)
                act.activation(nrm[:, u, 1], nrm[:, u, 0], ACT.Sqrt).then_inc(s["root_n"], 1)

            def queries_T(b, u):
                act.wait_ge(s["qT_ps"], b + 1)
                need(act, q_out[u], 8 * (b - u))
                act.copy(qTs[0:97, u], split(k.ps_b[0:97, 4, :], (MH, P))).then_inc(s["qT"], 1)

            for b, u in blocks(act):
                act.wait_ge(s["var"], b + 1)
                act.activation(stat[:, u, 9:10], stat[:, u, 8:9], ACT.Sqrt).then_inc(s["root_v"], 1)
                act.wait_ge(s["xT_ps"], b + 1)
                act.copy(xT[:, u], split(ps[:, 0, 0:2 * P], (2, P))).then_inc(s["xT"], 1)
                if not at_start(b, 1):
                    root_of_norms(b - 1, 1 - u)
                act.wait_ge(s["proj"], b + 1)
                need(act, k_out[u], 8 * (b - u))
                need(act, v_out[u], 8 * (b - u))
                need(act, s["split"], 4 * b - 4)
                act.copy(gnn[:, u, :], ps[:, 1, :]).then_inc(s["gnn"], 1)
                act.activation(mix[:, u, 0:8], split(ps[:, 2, 0:D], (8, MD)), ACT.Copy,
                               scale=MSCALE).then_inc(s["mixed"], 1)
                act.copy(mix[:, u, 8:16], split(ps[:, 2, D:], (8, MD))).then_inc(s["mixed"], 1)
                act.copy(mix[:, u, 16:24], split(ps[:, 3, 0:D], (8, MD))).then_inc(s["mixed"], 1)
                act.wait_ge(s["mixed"], 3 * b + 3)
                act.activation(sq[:, u], mix[:, u, 0:16], ACT.Square).then_inc(s["squared"], 1)
                if not at_start(b, 1):
                    queries_T(b - 1, 1 - u)
            root_of_norms(NB - 1, 0)
            queries_T(NB - 1, 0)

        @block.vector
        def _(dve):
            def one_hot(b, u, half):
                n = 2 * b + half
                need(dve, s["hist"], n - 3)
                one_hot_rows(k, dve, low[:, 2 * u + half], high[:, 2 * u + half], n).then_inc(s["hot"], 1)

            def layer_norm(b, u):
                dve.wait_ge(x_in[u], 8 * (b - u) + 16)
                need(dve, s["xT_ps"], b - 1)
                dve.bn_stats(stat[:, u, 0:6], xb[:, u, :]).then_inc(s["stats"], 1)
                dve.wait_ge(s["stats"], b + 1)
                dve.sem_inc(s["passed"])
                dve.bn_aggr(stat[:, u, 6:8], stat[:, u, 0:6]).then_inc(s["mean"], 1)
                dve.wait_ge(s["mean"], b + 1)
                dve.tensor_scalar(stat[:, u, 8:9], stat[:, u, 7:8], 1e-5, None, ALU.add).then_inc(s["var"], 1)
                one_hot(b, u, 0)
                dve.wait_ge(s["root_v"], b + 1)
                dve.reciprocal(stat[:, u, 10:11], stat[:, u, 9:10]).then_inc(s["inv"], 1)
                dve.wait_ge(s["inv"], b + 1)
                dve.tensor_scalar(xn[:, u, :], xb[:, u, :], stat[:, u, 6:7], stat[:, u, 10:11],
                                  ALU.subtract, ALU.mult).then_inc(s["xn"], 1)

            def attention_inputs(b, u):
                first = at_start(b, 2)
                q = k.qtab[:, bass.ds(b, 1)].rearrange("p o t d -> p (o t) d")
                dve.wait_ge(s["gnn"], b + 1)
                dve.tensor_scalar(qs[:, u, :], gnn[:, u, 0:P], GD ** -0.5, None, ALU.mult).then_inc(s["qpart"], 1)
                dve.wait_ge(s["mixed"], 3 * b + 3)
                if not first:
                    dve.wait_ge(w_out[u], 8 * (b - u))
                mask = k.cst[:, bass.ds(C_MASK + b, 1)]
                dve.tensor_scalar(v1[:, u, :, 1:33], mix[:, u, 16:24], mask, None, ALU.mult).then_inc(s["v1"], 1)
                dve.tensor_scalar(v1[:, u, :, 0:1], split(ones[:, 0:MH], (MH, 1)), mask, None,
                                  ALU.mult).then_inc(s["v1"], 1)
                dve.wait_ge(s["qpart"], 5 * b + 1)
                dve.tensor_copy(q[:, 0], qs[:, u, :]).then_inc(s["qpart"], 1)
                dve.wait_ge(s["squared"], b + 1)
                dve.tensor_reduce(nrm[:, u, 0], sq[:, u], AX, ALU.add).then_inc(s["norm2"], 1)
                dve.wait_ge(s["qpart"], 5 * b + 2)
                dve.tensor_tensor(rest[:, u, :], qs[:, u, :], q[:, 0], ALU.subtract).then_inc(s["qpart"], 1)
                dve.wait_ge(s["root_n"], b + 1)
                dve.tensor_scalar(nrm[:, u, 2], nrm[:, u, 1], 1e-12, None, ALU.max).then_inc(s["clip"], 1)
                dve.wait_ge(s["qpart"], 5 * b + 3)
                dve.tensor_copy(q[:, 1], rest[:, u, :]).then_inc(s["qpart"], 1)
                dve.wait_ge(s["clip"], b + 1)
                dve.reciprocal(nrm[:, u, 3], nrm[:, u, 2]).then_inc(s["recip"], 1)
                dve.wait_ge(s["qpart"], 5 * b + 4)
                dve.tensor_tensor(q[:, 2], rest[:, u, :], q[:, 1], ALU.subtract).then_inc(s["qpart"], 1)
                dve.wait_ge(s["recip"], b + 1)
                dve.scalar_tensor_tensor(nrm[:, u, 4], nrm[:, u, 3], MSCALE, factor, ALU.mult,
                                         ALU.mult).then_inc(s["factor"], 1)
                dve.wait_ge(s["factor"], b + 1)
                if not first:
                    dve.wait_ge(e_out[u], 8 * (b - u))
                fac = nrm[:, u, 4]
                dve.tensor_tensor(qn[:, u], mix[:, u, 0:8], over(fac, (1, 8), (0, MD)),
                                  ALU.mult).then_inc(s["normed"], 1)
                fk = nrm[:, u, 4, 8:16]
                dve.tensor_tensor(kext[:, u, :, 0:32], mix[:, u, 8:16], over(fk, (1, 8), (0, 32)),
                                  ALU.mult).then_inc(s["normed"], 1)
                dve.tensor_tensor(kext[:, u, :, 32:48], mix[:, u, 8:16, 0:16], over(fk, (1, 8), (0, 16)),
                                  ALU.mult).then_inc(s["normed"], 1)
                dve.wait_ge(s["normed"], 3 * b + 1)
                need(dve, s["qT_ps"], b - 1)
                dve.tensor_copy(parts[:, u, :, 0:32], qn[:, u]).then_inc(s["split"], 1)
                dve.wait_ge(s["split"], 4 * b + 1)
                dve.tensor_tensor(qrest[:, u], qn[:, u], parts[:, u, :, 0:32], ALU.subtract).then_inc(s["split"], 1)
                dve.wait_ge(s["split"], 4 * b + 2)
                dve.tensor_copy(parts[:, u, :, 32:64], qrest[:, u]).then_inc(s["split"], 1)
                dve.wait_ge(s["split"], 4 * b + 3)
                dve.tensor_tensor(parts[:, u, :, 64:96], qrest[:, u], parts[:, u, :, 32:64],
                                  ALU.subtract).then_inc(s["split"], 1)

            dve.memset(factor[:, MH:], 1.0)
            dve.memset(parts[:, :, :, 96:97], 1.0)
            dve.memset(zero, 0.0)
            dve.memset(ones, 1.0).then_inc(s["set"], 1)
            dve.wait_ge(s["set"], 1)
            dve.wait_ge(s["weights"], 48)
            for b, u in blocks(dve):
                layer_norm(b, u)
                if not at_start(b, 1):
                    attention_inputs(b - 1, 1 - u)
                one_hot(b, u, 1)
            attention_inputs(NB - 1, 0)
            dve.wait_ge(s["hist"], 2 * NB)
            dve.tensor_copy(k.start, ps[:, 5, 0:NB])


def phase_kv_sums(nc, k):
    w = Space(k.arena, k.WORK0, k.MT0)
    kext, v1 = w.f32(2, MH, 48), w.f32(2, MH, 33)
    kk = w.f32(2, 4, PAIRS)
    zero = w.f32(512)
    sums = w.f32(4, 640)
    ps = k.ps
    with ExitStack() as ctx:
        s = sems(nc, k, "kv", "set in0 in1 pairs lin used summed copied turned")
        arrived = (s["in0"], s["in1"])
        block = ctx.enter_context(nc.Block())

        @block.sync
        def _(sp):
            for b, u in blocks(sp):
                need(sp, s["used"], 2 * b - 2)
                sp.dma_start(kext[:, u].rearrange("p h i -> p (h i)"),
                             k.kext_rows[bass.ds(b * P, P), :]).then_inc(arrived[u], 16)
                sp.dma_start(v1[:, u].rearrange("p h i -> p (h i)"),
                             k.v1_rows[bass.ds(b * P, P), :]).then_inc(arrived[u], 16)

        @block.vector
        def _(dve):
            dve.memset(zero, 0.0)
            dve.memset(k.mt, 0.0)
            dve.memset(kk[:, :, :, PAIRS - 1:], 1.0)
            dve.memset(sums, 0.0).then_inc(s["set"], 1)
            for b, u in blocks(dve):
                dve.wait_ge(arrived[u], 16 * (b - u) + 32)
                for half in (0, 1):
                    need(dve, s["used"], 2 * b + half - 1)
                    a = kext[:, u, 4 * half:4 * half + 4]
                    dve.tensor_tensor(over(kk[:, half], (PAIRS, 4), (MD, ND), (1, MD)),
                                      over(a, (48, 4), (0, ND), (1, MD)),
                                      over(a, (48, 4), (1, ND), (1, MD)), ALU.mult).then_inc(s["pairs"], 1)

        @block.tensor
        def _(pe):
            pe.wait_ge(s["set"], 1)
            for side in (0, 64):
                for bank in range(5):
                    n = 512 if bank < 4 else 4 * 65
                    pe.matmul(ps[side:side + 33, bank, 0:n], zero[:, 0:33], zero[:, 0:n], start=True, stop=False,
                              skip_group_check=True)
            for b, u in blocks(pe):
                for half in (0, 1):
                    pe.wait_ge(s["pairs"], 2 * b + half + 1)
                    pe.wait_ge(s["lin"], 2 * b + half + 1)
                    for j in range(4):
                        h = 4 * half + j
                        hp, side = h // 2, 64 * (h % 2)
                        pe.matmul(ps[side:side + 33, hp, :], v1[:, u, h, :], kk[:, half, j, 0:512],
                                  start=False, stop=False, skip_group_check=True)
                        mm = pe.matmul(ps[side:side + 33, 4, 65 * hp:65 * hp + 65], v1[:, u, h, :],
                                       kk[:, half, j, 512:PAIRS], start=False, stop=False,
                                       skip_group_check=True)
                    mm.then_inc(s["used"], 1)
            pe.wait_ge(s["copied"], 1)
            for t in range(20):
                mm = pe.transpose(ps[:, t // 4, (t % 4) * P:(t % 4 + 1) * P],
                                  sums[:, t // 5, (t % 5) * P:(t % 5 + 1) * P], k.ident)
            mm.then_inc(s["turned"], 1)

        @block.scalar
        def _(act):
            for b, u in blocks(act):
                act.wait_ge(arrived[u], 16 * (b - u) + 32)
                for half in (0, 1):
                    need(act, s["used"], 2 * b + half - 1)
                    act.copy(over(kk[:, half, 0, 544:], (PAIRS, 4), (1, MD)),
                             kext[:, u, 4 * half:4 * half + 4, 0:32]).then_inc(s["lin"], 1)
            act.wait_ge(s["used"], 2 * NB)
            for side in (0, 64):
                r = slice(side, side + 33)
                for hp in range(4):
                    act.mul(sums[r, hp, 0:32], ps[r, hp, 0:32], 0.5)
                    act.copy(sums[r, hp, 32:512], ps[r, hp, 32:512])
                    act.mul(sums[r, hp, 512:544], ps[r, 4, 65 * hp:65 * hp + 32], 0.5)
                    act.mul(sums[r, hp, 544:576], ps[r, 4, 65 * hp + 32:65 * hp + 64], MSCALE ** 2)
                    last = act.mul(sums[r, hp, 576:577], ps[r, 4, 65 * hp + 64:65 * hp + 65], MSCALE ** 4)
            last.then_inc(s["copied"], 1)
            act.wait_ge(s["turned"], 1)
            for bank in range(5):
                for side in (0, 1):
                    src = split(ps[:, bank, :], (4, P))[:, :, 64 * side:64 * side + 33]
                    dst = k.mt[:, 4 * bank:4 * bank + 4, side, :]
                    act.copy(dst[:, :, 32 * side:32 * side + 32], src[:, :, 1:33])
                    act.copy(dst[:, :, 64 + 32 * side:96 + 32 * side], src[:, :, 0:1].to_broadcast([P, 4, 32]))


def phase_starts(nc, k):
    w = Space(k.arena, k.WORK0, k.COLS0)
    ones, one_b = w.f32(P), w.bf16(P)
    tot, count, tiles, ends, first = w.f32(NB), w.f32(NB, dt=I32), w.f32(NB), w.f32(NB), w.f32(NB)
    whole = w.f32(NB, dt=I32)
    end_col, after = w.f32(2), w.bf16(CH * STEPS)
    half = CH * STEPS // 2
    ps = k.ps
    with ExitStack() as ctx:
        s = sems(nc, k, "starts", "set sums turned col after blocks d")
        block = ctx.enter_context(nc.Block())

        @block.tensor
        def _(pe):
            pe.wait_ge(s["set"], 1)
            pe.matmul(ps[:, 1, 0:NB], ones, k.start, start=True, stop=True)
            pe.matmul(ps[:, 2, 0:NB], k.cst[:, C_AFTER:C_AFTER + P], k.start, start=True,
                      stop=True).then_inc(s["sums"], 1)
            pe.wait_ge(s["d"], 5)
            pe.transpose(ps[0:NB, 3, 0:P], ends, k.ident).then_inc(s["turned"], 1)
            pe.wait_ge(s["after"], 1)
            for c in range(2):
                mm = pe.matmul(ps[0:1, 4 + c, 0:half], one_b[0:NB, 0:1], after[0:NB, c * half:(c + 1) * half],
                               start=True, stop=True)
            mm.then_inc(s["blocks"], 1)

        @block.vector
        def _(dve):
            done = 0

            def then(ins):
                nonlocal done
                done += 1
                ins.then_inc(s["d"], 1)
                dve.wait_ge(s["d"], done)

            dve.memset(one_b, 1.0)
            dve.memset(ones, 1.0).then_inc(s["set"], 1)
            dve.wait_ge(s["sums"], 1)
            then(dve.tensor_scalar(tot, ps[:, 1, 0:NB], float(P - 1), None, ALU.add))
            then(dve.tensor_copy(count, tot))
            then(dve.tensor_scalar(whole, count, 7, None, ALU.arith_shift_right))
            then(dve.tensor_copy(tiles, whole))
            then(dve.tensor_tensor_scan(ends, ones[:, 0:NB], tiles, 0.0, ALU.mult, ALU.add))
            then(dve.tensor_tensor(first, ends, tiles, ALU.subtract))
            then(dve.scalar_tensor_tensor(k.start, first, float(P), ps[:, 2, 0:NB], ALU.mult, ALU.add))
            dve.wait_ge(s["turned"], 1)
            dve.tensor_copy(end_col[0:NB, 0:1], ps[0:NB, 3, 0:1]).then_inc(s["col"], 1)
            dve.wait_ge(s["col"], 1)
            dve.tensor_scalar(after[0:NB, :], k.cst[0:NB, C_TILE:C_END], end_col[0:NB, 0:1], None,
                              ALU.is_ge).then_inc(s["after"], 1)
            dve.wait_ge(s["blocks"], 1)
            for c in range(2):
                dve.tensor_scalar(k.blocks[0:1, c * half:(c + 1) * half], ps[0:1, 4 + c, 0:half], float(NB - 1),
                                  None, ALU.min)


def phase_mix_scatter(nc, k):
    w = Space(k.arena, k.WORK0, k.MT0)
    wp = w.f32(4, D)
    qT = w.bf16(2, 4, P)
    a_sb = w.f32(2, 2, 4 * P)
    qq = w.f32(2, 5, 4 * P)
    xb, yT, xo, rn = w.f32(2, D), w.f32(4, P), w.f32(2, D), w.f32(4, P)
    row_s, row_lo = w.f32(2, 8 * P), w.bf16(2, 8 * P)
    low_T, low, high = w.f32(2, 8, P), w.bf16(2, 8, P), w.bf16(2, 8, NB)
    table = w.f32(2, 8, NB)
    junk_e, junk_g = w.f32(8, P), w.f32(8, NB)
    before, rank, slot = w.f32(2, 8), w.f32(2, 8), w.f32(4, 8, dt=I32)
    rec = w.f32(4, 8, REC)
    ps = k.ps
    LAST = 2 * NB - 1
    with ExitStack() as ctx:
        s = sems(nc, k, "mix", "weights q_in0 q_in1 x_in0 x_in1 a_ps a4_ps b_ps a_sb a4_sb qq y recip yT "
                 "proj xo out0 out1")
        q_in, x_in, out = (s["q_in0"], s["q_in1"]), (s["x_in0"], s["x_in1"]), (s["out0"], s["out1"])
        e = sems(nc, k, "edges", "passed set rows0 rows1 attr0 attr1 attr2 attr3 hot high fields count table looked "
                 "summed ranked ranks slots stored0 stored1 stored2 stored3")
        rows = (e["rows0"], e["rows1"])
        attr = (e["attr0"], e["attr1"], e["attr2"], e["attr3"])
        stored = (e["stored0"], e["stored1"], e["stored2"], e["stored3"])
        block = ctx.enter_context(nc.Block())

        @block.sync
        def _(sp):
            sp.dma_start(wp[0:64], k.proj_w).then_inc(s["weights"], 16)
            sp.wait_ge(e["set"], 1)
            sp.wait_ge(k.rows_stored, 32)
            for b, u in blocks(sp):
                for half in (0, 1):
                    n = 2 * b + half
                    need(sp, e["ranks"], n - 1)
                    sp.dma_start(row_s[:, half, :], k.row_s[bass.ds(n * 8 * P, 8 * P)].partition_broadcast(P)
                                 ).then_inc(rows[half], 16)
                    sp.dma_start(row_lo[:, half, :], k.row_lo[bass.ds(n * 8 * P, 8 * P)].partition_broadcast(P)
                                 ).then_inc(rows[half], 16)
                    need(sp, stored[2 * u + half], 64 * (b - u))
                    sp.dma_start(rec[:, 2 * u + half, :, 0:R_ONE], k.attr[:, bass.ds(n * 8, 8), :]
                                 ).then_inc(attr[2 * u + half], 16)
                    need(sp, s["qq"], 5 * n - 5)
                    sp.dma_start(qT[0:97, half],
                                 k.qT_rows[bass.ds(b * 97, 97), 512 * half:512 * half + 512].rearrange(
                                     "p (h n) -> p h n", h=4)).then_inc(q_in[half], 16)
                need(sp, s["xo"], b - 1)
                sp.dma_start(xb[:, u, :], k.x[bass.ds(b * P, P), :]).then_inc(x_in[u], 16)

        @block.gpsimd
        def _(pool):
            def store(b, u):
                pool.wait_ge(s["xo"], b + 1)
                pool.dma_start(k.xm_rows[bass.ds(b * P, P), :], xo[:, u, :]).then_inc(out[u], 16)

            pool.wait_ge(k.blanks_stored, 16 * (SLOTS // (64 * P)))
            for b, u in blocks(pool):
                for half in (0, 1):
                    v = 2 * u + half
                    pool.wait_ge(attr[v], 8 * (b - u) + 16)
                    pool.wait_ge(e["fields"], 2 * b + half + 1)
                    pool.wait_ge(e["slots"], 2 * b + half + 1)
                    pool.sem_inc(e["passed"])
                    for j in range(8):
                        pool.indirect_dma_start(out=k.records, out_offset=bass.IndirectOffsetOnAxis(
                            ap=slot[:, v, j:j + 1], axis=0), in_=rec[:, v, j, :], in_offset=None
                        ).then_inc(stored[v], 16)
                if not at_start(b, 2):
                    store(b - 2, u)
            store(NB - 2, 1)
            store(NB - 1, 0)
            for u in (0, 1):
                n = (NB + 1 - u) // 2
                pool.wait_ge(out[u], 16 * n)
                pool.wait_ge(stored[2 * u], 128 * n)
                pool.wait_ge(stored[2 * u + 1], 128 * n)

        @block.tensor
        def _(pe):
            def sum_head(b, half, j):
                n = 2 * b + half
                if j == 0:
                    pe.wait_ge(s["qq"], 5 * n + 5)
                    if half == 0:
                        need(pe, s["yT"], b)
                hp, side = (4 * half + j) // 2, j % 2
                for g in range(5):
                    r = slice(0, P) if g < 4 else slice(0, 65)
                    mm = pe.matmul(ps[:, 4, hp * P:(hp + 1) * P], k.mt[r, 5 * hp + g, side, :],
                                   qq[r, half, g, j * P:(j + 1) * P], start=(g == 0 and side == 0),
                                   stop=(g == 4 and side == 1))
                if j == 3:
                    mm.then_inc(s["y"], 1)

            def project(b):
                pe.wait_ge(s["yT"], b + 1)
                need(pe, s["xo"], b)
                for hp in range(4):
                    pe.matmul(ps[:, 5, 0:D], yT[0:64, hp, :], wp[0:64, hp, :], start=(hp == 0), stop=False)
                pe.matmul(ps[:, 5, 0:D], k.ones_b[0:3, :], k.bias3[0:3, 1280:], start=False,
                          stop=True).then_inc(s["proj"], 1)

            def count(n, u, part):
                for j in range(8):
                    c0, m = (j + 1, 7 - j) if part == 0 else (0, j + 1)
                    if m:
                        mm = pe.matmul(ps[:, 6, c0 * NB:(c0 + m) * NB], low[:, u, j, :],
                                       over(high[:, u, j, :], (0, m), (1, NB)), start=False, stop=False,
                                       skip_group_check=True)
                return mm

            def count_own(n, u):
                pe.wait_ge(e["hot"], n + 1)
                count(n, u, 0).then_inc(e["count"], 1)

            def look_up(n, u):
                pe.wait_ge(e["table"], n + 1)
                count(n, u, 1)
                need(pe, e["summed"], n)
                for j in range(8):
                    mm = pe.matmul(ps[:, 7, j * NB:(j + 1) * NB], low_T[:, u, j, :], table[:, u, j, :],
                                   start=True, stop=True)
                mm.then_inc(e["looked"], 1)

            pe.matmul(ps[:, 6, 0:8 * NB], k.ident, over(k.start, (0, 8), (1, NB)), start=True, stop=False,
                      skip_group_check=True)
            def first_factors(b, half):
                n = 2 * b + half
                q = qT[0:97, half].rearrange("p h n -> p (h n)")
                pe.wait_ge(q_in[half], 16 * (b + 1))
                need(pe, s["a_sb"], n)
                pe.matmul(ps[:, 0, :], k.sel_b[0:97, 0, :], q, start=True, stop=True).then_inc(s["a_ps"], 1)
                need(pe, s["a4_sb"], n)
                pe.matmul(ps[0:65, 1, :], k.sel_b[0:97, 5, 0:65], q, start=True,
                          stop=True).then_inc(s["a4_ps"], 1)

            pe.wait_ge(s["weights"], 16)
            first_factors(0, 0)
            for b, _ in blocks(pe):
                first = at_start(b, 1)
                for half in (0, 1):
                    n = 2 * b + half
                    q = qT[0:97, half].rearrange("p h n -> p (h n)")
                    for g in range(5):
                        m = 5 * half + g
                        need(pe, s["qq"], 10 * b + m - 1)
                        if g < 4:
                            pe.matmul(ps[:, 2 + m % 2, :], k.sel_b[0:97, 1 + g, :], q, start=True,
                                      stop=True).then_inc(s["b_ps"], 1)
                        else:
                            pe.matmul(ps[0:65, 2 + m % 2, :], k.sel_b[0:97, 6, 0:65], q, start=True,
                                      stop=True).then_inc(s["b_ps"], 1)
                        if g >= 1:
                            if half == 1:
                                sum_head(b, 0, g - 1)
                            elif not first:
                                sum_head(b - 1, 1, g - 1)
                        if g in (0, 2) and not (first and n == 0):
                            (count_own, look_up)[g // 2](n - 1, 1 - half)
                        if g == 3 and not (isinstance(b, int) and n == LAST):
                            first_factors(b + half, 1 - half)
                        if half == 1 and not first and g == 4:
                            project(b - 1)
            for j in range(4):
                sum_head(NB - 1, 1, j)
            count_own(LAST, 1)
            project(NB - 1)
            look_up(LAST, 1)

        @block.scalar
        def _(act):
            def tables(n, u):
                act.wait_ge(e["count"], n + 1)
                need(act, e["looked"], n - 1)
                act.copy(table[:, u], split(ps[:, 6, 0:8 * NB], (8, NB))).then_inc(e["table"], 1)

            def first_factors(n, half):
                act.wait_ge(s["a_ps"], n + 1)
                need(act, s["qq"], 5 * n - 5)
                act.copy(a_sb[:, half, 0], ps[:, 0, :]).then_inc(s["a_sb"], 1)
                act.wait_ge(s["a4_ps"], n + 1)
                act.copy(a_sb[0:65, half, 1], ps[0:65, 1, :]).then_inc(s["a4_sb"], 1)

            act.wait_ge(e["set"], 1)
            first_factors(0, 0)
            for b, u in blocks(act):
                for half in (0, 1):
                    n = 2 * b + half
                    if not at_start(n, 1):
                        tables(n - 1, 1 - half)
                    if not (isinstance(b, int) and n == LAST):
                        first_factors(n + 1, 1 - half)
                    v = 2 * u + half
                    need(act, stored[v], 64 * (b - u))
                    act.copy(rec[:, v, :, R_T:R_LO + 1].rearrange("p e f -> p f e"),
                             k.cols[:, 0:3, bass.ds(n * 8, 8)]).then_inc(e["fields"], 1)
            tables(LAST, 1)

        @block.vector
        def _(dve):
            def divide(b):
                dve.wait_ge(s["y"], 2 * b + 2)
                y = split(ps[:, 4, :], (4, P))
                dve.reciprocal(rn[0:64], y[64:128]).then_inc(s["recip"], 1)
                dve.wait_ge(s["recip"], b + 1)
                need(dve, s["proj"], b)
                dve.tensor_tensor(yT[0:64], y[0:64], rn[0:64], ALU.mult).then_inc(s["yT"], 1)

            def add(b, u):
                dve.wait_ge(s["proj"], b + 1)
                dve.wait_ge(x_in[u], 8 * (b - u) + 16)
                if not at_start(b, 2):
                    dve.wait_ge(out[u], 8 * (b - u))
                dve.tensor_tensor(xo[:, u, :], ps[:, 5, 0:D], xb[:, u, :], ALU.add).then_inc(s["xo"], 1)

            def one_hot(b, u, part):
                n = 2 * b + u
                if part == 0:
                    dve.wait_ge(rows[u], 32 * (b + 1))
                    need(dve, e["looked"], n - 1)
                    dve.tensor_scalar(low_T[:, u].rearrange("p j e -> p (j e)"), row_lo[:, u, :],
                                      k.cst[:, C_P:C_P + 1], None, ALU.is_equal)
                if part == 1:
                    need(dve, e["slots"], n - 1)
                    one_hot_rows(k, dve, low[:, u], high[:, u], n).then_inc(e["hot"], 1)
                if part >= 2:
                    for j in range(4 * part - 8, 4 * part - 4):
                        last = dve.scalar_tensor_tensor(junk_e[:, j, :], row_s[:, u, j * P:(j + 1) * P],
                                                        k.cols[:, 1, bass.ds(n * 8 + j, 1)],
                                                        k.cst[:, C_BEFORE:C_BEFORE + P], ALU.is_equal, ALU.mult,
                                                        accum_out=before[:, u, j:j + 1])
                if part == 3:
                    last.then_inc(e["ranks"], 1)

            def slots(n, u, v, b):
                dve.wait_ge(e["looked"], n + 1)
                dve.tensor_tensor(junk_g, split(ps[:, 7, 0:8 * NB], (8, NB)), high[:, u], ALU.mult
                                  ).then_inc(e["summed"], 1)
                dve.wait_ge(e["summed"], n + 1)
                dve.tensor_reduce(rank[:, u, :], junk_g, AX, ALU.add).then_inc(e["ranked"], 1)
                dve.wait_ge(e["ranked"], n + 1)
                need(dve, stored[v], 64 * (b - v // 2))
                dve.tensor_tensor(slot[:, v, :], before[:, u, :], rank[:, u, :], ALU.add).then_inc(e["slots"], 1)

            dve.memset(rec, 0.0).then_inc(e["high"], 1)
            dve.wait_ge(e["high"], 1)
            dve.memset(rec[:, :, :, R_ONE:R_ONE + 1], 1.0).then_inc(e["set"], 1)
            for b, u in blocks(dve):
                start = at_start(b, 1)
                for half in (0, 1):
                    n = 2 * b + half
                    dve.wait_ge(s["a_sb"], n + 1)
                    dve.wait_ge(s["a4_sb"], n + 1)
                    need(dve, s["y"], n - 1)
                    for g in range(5):
                        m = 5 * half + g
                        r = slice(0, P) if g < 4 else slice(0, 65)
                        dve.wait_ge(s["b_ps"], 10 * b + m + 1)
                        dve.tensor_tensor(qq[r, half, g], ps[r, 2 + m % 2, :], a_sb[r, half, int(g == 4)],
                                          ALU.mult).then_inc(s["qq"], 1)
                        if g == 0 and half == 1 and not start:
                            divide(b - 1)
                        if g == 1 and half == 0 and not at_start(b, 2):
                            add(b - 2, u)
                        if g < 4:
                            one_hot(b, half, g)
                        elif half == 1:
                            slots(n - 1, 0, 2 * u, b)
                        elif not start:
                            slots(n - 1, 1, 3 - 2 * u, b - 1)
            add(NB - 2, 1)
            divide(NB - 1)
            slots(LAST, 1, 1, NB - 1)
            add(NB - 1, 0)


def records_of(k, g):
    return k.records.rearrange("(c g e) f -> g e c f", c=CH, g=STEPS)[bass.ds(g, 1)].rearrange(
        "o e c f -> (o e) c f")


def blocks_of(nc, k, g, engine):
    return nc.values_load_multi_w_load_instructions(
        k.blocks[0:1, bass.ds(g * CH, CH)], engines=[engine], min_val=0, max_val=NB - 1,
        skip_runtime_bounds_check_because="phase_starts keeps them at most NB - 1")[1]


def phase_compat(nc, k):
    w = Space(k.arena, k.WORK0, k.BIG1)
    rec, kg = w.f32(4, CH, REC), w.f32(4, CH, P)
    t_int = w.f32(4, CH, dt=I32)
    hot, hot_T = w.bf16(2, CH, P), w.bf16(2, CH, P)
    rec_T = w.f32(2, 2, P)
    ks, prod = w.f32(2, 4, P), w.f32(2, 4, P)
    score, node = w.f32(4, CH, GH), w.f32(4, CH, GH)
    wr = w.f32(4, 2 * P)
    ps = k.ps
    with ExitStack() as ctx:
        s = sems(nc, k, "compat", "passed weights r_in0 r_in1 r_in2 r_in3 t k_in0 k_in1 k_in2 k_in3 hot hot_ps hot_T "
                 "rec_ps rec_T qk ks prod score node turned stored")
        r_in = (s["r_in0"], s["r_in1"], s["r_in2"], s["r_in3"])
        k_in = (s["k_in0"], s["k_in1"], s["k_in2"], s["k_in3"])
        block = ctx.enter_context(nc.Block())

        @block.sync
        def _(sp):
            sp.dma_start(wr, k.rpe_w).then_inc(s["weights"], 16)
            for g, v in fours(sp, STEPS):
                need(sp, s["rec_ps"], g - 3)
                need(sp, s["hot"], g - 3)
                need(sp, s["node"], g - 3)
                sp.dma_start(rec[:, v], records_of(k, g)).then_inc(r_in[v], 16)

        @block.gpsimd
        def _(pool):
            for g, v in fours(pool, STEPS):
                pool.wait_ge(s["t"], g + 1)
                need(pool, s["ks"], 2 * g - 6)
                pool.sem_inc(s["passed"])
                for c in range(CH):
                    pool.indirect_dma_start(out=kg[:, v, c, :], out_offset=None, in_=k.k_rows,
                                            in_offset=bass.IndirectOffsetOnAxis(ap=t_int[:, v, c:c + 1], axis=0)
                                            ).then_inc(k_in[v], 16)

        @block.tensor
        def _(pe):
            def products(g, v):
                u = v % 2
                blk = blocks_of(nc, k, g, ENG.PE)
                pe.wait_ge(s["rec_T"], g + 1)
                pe.wait_ge(s["hot_T"], g + 1)
                for half in (0, 1):
                    need(pe, s["prod"], 2 * g + half - 1)
                    for j in range(4):
                        c = 4 * half + j
                        bank, at = 2 + 2 * half + j // 2, (j % 2) * 2 * P
                        pe.matmul(ps[:, bank, at:at + 2 * P], rec_T[:, u, half, :], wr[:, j, :], start=True,
                                  stop=False, skip_group_check=True)
                        for part in range(3):
                            q = k.qtab[:, bass.ds(blk[c], 1), part, :].rearrange("p o d -> p (o d)")
                            mm = pe.matmul(ps[:, bank, at:at + P], hot_T[:, u, c, :], q, start=False,
                                           stop=(part == 2), skip_group_check=True)
                    mm.then_inc(s["qk"], 1)

            def turn(g, v):
                pe.wait_ge(s["score"], 2 * g + 2)
                pe.wait_ge(s["node"], g + 1)
                need(pe, s["stored"], g)
                pe.transpose(ps[:, 6, 0:P], score[:, v].rearrange("p c h -> p (c h)"), k.ident)
                pe.transpose(ps[:, 6, P:2 * P], node[:, v].rearrange("p c h -> p (c h)"),
                             k.ident).then_inc(s["turned"], 1)

            pe.wait_ge(s["weights"], 16)
            for g, v in fours(pe, STEPS):
                pe.wait_ge(r_in[v], 4 * (g - v) + 16)
                need(pe, s["rec_T"], g)
                for half in (0, 1):
                    mm = pe.transpose(ps[:, 1, half * P:(half + 1) * P],
                                      rec[:, v, 4 * half:4 * half + 4].rearrange("p c f -> p (c f)"), k.ident)
                mm.then_inc(s["rec_ps"], 1)
                pe.wait_ge(s["hot"], g + 1)
                need(pe, s["hot_T"], g)
                for c in range(CH):
                    mm = pe.transpose(k.ps_b[:, 0, c * P:(c + 1) * P], hot[:, v % 2, c, :], k.ident_b)
                mm.then_inc(s["hot_ps"], 1)
                if not at_start(g, 1):
                    products(g - 1, (v - 1) % 4)
                if not at_start(g, 3):
                    turn(g - 3, (v - 3) % 4)
            products(STEPS - 1, 3)
            for g in (STEPS - 3, STEPS - 2, STEPS - 1):
                turn(g, g % 4)

        @block.scalar
        def _(act):
            def store(g):
                act.wait_ge(s["turned"], g + 1)
                act.copy(k.scores[:, bass.ds(g * P, P)], ps[:, 6, 0:P])
                act.copy(k.owner[:, bass.ds(g * P, P)], ps[:, 6, P:2 * P]).then_inc(s["stored"], 1)

            for g, v in fours(act, STEPS):
                act.wait_ge(s["rec_ps"], g + 1)
                need(act, s["qk"], 2 * g - 2)
                act.copy(rec_T[:, v % 2], split(ps[:, 1, 0:2 * P], (2, P))).then_inc(s["rec_T"], 1)
                act.wait_ge(s["hot_ps"], g + 1)
                act.copy(hot_T[:, v % 2], split(k.ps_b[:, 0, :], (CH, P))).then_inc(s["hot_T"], 1)
                act.wait_ge(r_in[v], 4 * (g - v) + 16)
                need(act, s["turned"], g - 3)
                act.copy(node[:, v], over(rec[:, v, 0, R_S:], (REC, CH), (0, GH))).then_inc(s["node"], 1)
                if not at_start(g, 3):
                    store(g - 3)
            for g in (STEPS - 3, STEPS - 2, STEPS - 1):
                store(g)

        @block.vector
        def _(dve):
            def scores(g, v):
                dve.wait_ge(k_in[v], 32 * (g - v) + 128)
                for half in (0, 1):
                    qk = ps[:, 2 + 2 * half:4 + 2 * half, :].rearrange("p b (j w) -> p b j w", j=2)
                    n = 2 * g + half
                    sum_, product = (t[:, half].rearrange("p (b j) w -> p b j w", b=2) for t in (ks, prod))
                    dve.wait_ge(s["qk"], n + 1)
                    need(dve, s["prod"], n - 1)
                    dve.tensor_tensor(sum_, qk[:, :, :, P:2 * P],
                                      kg[:, v, 4 * half:4 * half + 4, :].rearrange("p (b j) w -> p b j w", b=2),
                                      ALU.add).then_inc(s["ks"], 1)
                    dve.wait_ge(s["ks"], n + 1)
                    need(dve, s["score"], n - 1)
                    dve.tensor_tensor(product, qk[:, :, :, 0:P], sum_, ALU.mult).then_inc(s["prod"], 1)
                need(dve, s["turned"], g - 2)
                for half in (0, 1):
                    dve.wait_ge(s["prod"], 2 * g + half + 1)
                    dve.tensor_reduce(score[:, v, 4 * half:4 * half + 4].rearrange("p c h -> p (c h)"),
                                      prod[:, half].rearrange("p c (h d) -> p (c h) d", d=GD), AX,
                                      ALU.add).then_inc(s["score"], 1)

            for g, v in fours(dve, STEPS):
                dve.wait_ge(r_in[v], 4 * (g - v) + 16)
                need(dve, k_in[v], 32 * (g - v))
                dve.tensor_copy(t_int[:, v, :], over(rec[:, v, 0, R_T:], (REC, CH))).then_inc(s["t"], 1)
                need(dve, s["hot_ps"], g - 1)
                for c in range(CH):
                    last = dve.tensor_scalar(hot[:, v % 2, c, :], k.iota_b, rec[:, v, c, R_LO:R_LO + 1], None,
                                             ALU.is_equal)
                last.then_inc(s["hot"], 1)
                if not at_start(g, 2):
                    scores(g - 2, (v - 2) % 4)
            scores(STEPS - 2, 2)
            scores(STEPS - 1, 3)


def phase_seg_max(nc, k):
    L = STEPS * P
    w = Space(k.arena, k.WORK0, k.FL0)
    ends, row, carry, col = w.f32(4), w.f32(4, CH, GH), w.f32(6, CH, GH), w.f32(2)
    breaks = k.breaks
    ps = k.ps
    with ExitStack() as ctx:
        s = sems(nc, k, "segmax", "d ends turned carry back")
        block = ctx.enter_context(nc.Block())

        @block.tensor
        def _(pe):
            pe.wait_ge(s["ends"], 1)
            for n in range(4):
                mm = pe.transpose(ps[0:1, 0, n * P:(n + 1) * P], ends[:, n:n + 1], k.ident)
            mm.then_inc(s["turned"], 1)
            pe.wait_ge(s["carry"], 1)
            for n in range(2):
                mm = pe.matmul(ps[:, 1, n:n + 1], carry[0:1, n].rearrange("p c h -> p (c h)"),
                               k.ident[0:1, 0:1], start=True, stop=True)
            mm.then_inc(s["back"], 1)

        @block.vector
        def _(dve):
            done = 0

            def then(ins):
                nonlocal done
                done += 1
                ins.then_inc(s["d"], 1)
                dve.wait_ge(s["d"], done)

            back = lambda ap: over(ap[:, L - 1:L], (-1, L))
            then(dve.memset(breaks, 0.0))
            then(dve.tensor_tensor(breaks[:, 1:L], k.owner[:, 1:L], k.owner[:, 0:L - 1], ALU.not_equal))
            then(dve.tensor_scalar(breaks[:, 1:L], breaks[:, 1:L], NEG, None, ALU.mult))
            dve.tensor_copy(ends[:, 0:1], k.owner[:, 0:1])
            then(dve.tensor_copy(ends[:, 1:2], k.owner[:, L - 1:L]))
            then(dve.tensor_tensor_scan(k.owner, breaks[:, 0:L], k.scores, NEG, ALU.add, ALU.max))
            then(dve.tensor_copy(ends[:, 2:3], k.owner[:, L - 1:L]))
            then(dve.tensor_tensor_scan(back(k.owner), back(breaks[:, 1:L + 1]), back(k.scores), NEG, ALU.add,
                                        ALU.max))
            dve.tensor_copy(ends[:, 3:4], k.owner[:, 0:1]).then_inc(s["ends"], 1)
            dve.wait_ge(s["turned"], 1)
            then(dve.tensor_copy(row[0:1], split(ps[0:1, 0, :], (4, CH, GH))))
            first, last, fwd, bwd = (row[0:1, n] for n in range(4))
            from_left, from_right, apart, many, both = (carry[0:1, n] for n in range(5))
            then(dve.memset(carry[0:1], NEG))
            dve.tensor_tensor(apart[:, 1:CH], first[:, 1:CH], last[:, 0:CH - 1], ALU.not_equal)
            then(dve.tensor_tensor(many, first, last, ALU.not_equal))
            dve.tensor_scalar(apart[:, 1:CH], apart[:, 1:CH], NEG, None, ALU.mult)
            then(dve.tensor_scalar(many, many, NEG, None, ALU.mult))
            for c in range(1, CH):
                then(dve.tensor_tensor(both[:, c], from_left[:, c - 1], many[:, c - 1], ALU.add))
                then(dve.tensor_tensor(both[:, c], both[:, c], fwd[:, c - 1], ALU.max))
                then(dve.tensor_tensor(from_left[:, c], both[:, c], apart[:, c], ALU.add))
            for c in range(CH - 2, -1, -1):
                then(dve.tensor_tensor(both[:, c], from_right[:, c + 1], many[:, c + 1], ALU.add))
                then(dve.tensor_tensor(both[:, c], both[:, c], bwd[:, c + 1], ALU.max))
                then(dve.tensor_tensor(from_right[:, c], both[:, c], apart[:, c + 1], ALU.add))
            dve.nop().then_inc(s["carry"], 1)
            dve.wait_ge(s["back"], 1)
            then(dve.tensor_copy(col, ps[:, 1, 0:2]))
            then(dve.tensor_tensor_scan(k.owner, breaks[:, 0:L], k.scores, col[:, 0:1], ALU.add, ALU.max))
            then(dve.tensor_tensor_scan(back(k.owner), back(breaks[:, 1:L + 1]), back(k.owner), col[:, 1:2],
                                        ALU.add, ALU.max))
            then(dve.tensor_tensor(k.scores, k.scores, k.owner, ALU.subtract))


def phase_messages(nc, k):
    w = Space(k.arena, k.Q0, k.BIG1)
    rec, vg = w.f32(4, CH, REC), w.f32(4, CH, D)
    t_int = w.f32(4, CH, dt=I32)
    ex, msg, hot = w.f32(2, P), w.f32(2, CH, D + GH), w.f32(4, CH, P)
    ps = k.ps
    with ExitStack() as ctx:
        s = sems(nc, k, "msg", "passed cleared r_in0 r_in1 r_in2 r_in3 t v_in0 v_in1 v_in2 v_in3 ex ex_ps weight hot "
                 "msg sums acc")
        r_in = (s["r_in0"], s["r_in1"], s["r_in2"], s["r_in3"])
        v_in = (s["v_in0"], s["v_in1"], s["v_in2"], s["v_in3"])
        block = ctx.enter_context(nc.Block())

        @block.sync
        def _(sp):
            for g, v in fours(sp, STEPS):
                need(sp, s["hot"], g - 3)
                sp.dma_start(rec[:, v], records_of(k, g)).then_inc(r_in[v], 16)

        @block.gpsimd
        def _(pool):
            for g, v in fours(pool, STEPS):
                pool.wait_ge(s["t"], g + 1)
                need(pool, s["msg"], 2 * g - 6)
                pool.sem_inc(s["passed"])
                for c in range(CH):
                    pool.indirect_dma_start(out=vg[:, v, c, :], out_offset=None, in_=k.v_rows,
                                            in_offset=bass.IndirectOffsetOnAxis(ap=t_int[:, v, c:c + 1], axis=0)
                                            ).then_inc(v_in[v], 16)

        @block.scalar
        def _(act):
            def weigh(g, v):
                act.wait_ge(s["ex_ps"], g + 1)
                need(act, s["sums"], 8 * g - 8)
                act.copy(msg[:, v % 2, :, D:], split(ps[:, v % 2, 0:P], (CH, GH))).then_inc(s["weight"], 1)

            for g, v in fours(act, STEPS):
                need(act, s["ex_ps"], g - 1)
                act.activation(ex[:, v % 2, :], k.scores[:, bass.ds(g * P, P)], ACT.Exp).then_inc(s["ex"], 1)
                if not at_start(g, 1):
                    weigh(g - 1, (v - 1) % 4)
            weigh(STEPS - 1, 3)

        @block.tensor
        def _(pe):
            def sums(g, v):
                pe.wait_ge(s["hot"], g + 1)
                for c in range(CH):
                    n = 8 * g + c
                    if c % 4 == 0:
                        pe.wait_ge(s["msg"], 2 * g + c // 4 + 1)
                    need(pe, s["acc"], n - 3)
                    pe.matmul(ps[:, 2 + c % 4, 0:D + GH], hot[:, v, c, :], msg[:, v % 2, c, :], start=True,
                              stop=True).then_inc(s["sums"], 1)

            for g, v in fours(pe, STEPS):
                pe.wait_ge(s["ex"], g + 1)
                need(pe, s["weight"], g - 1)
                pe.transpose(ps[:, v % 2, 0:P], ex[:, v % 2, :], k.ident).then_inc(s["ex_ps"], 1)
                if not at_start(g, 2):
                    sums(g - 2, (v - 2) % 4)
            sums(STEPS - 2, 2)
            sums(STEPS - 1, 3)

        @block.vector
        def _(dve):
            def add(g, half, blk):
                for c in range(4 * half, 4 * half + 4):
                    n = 8 * g + c
                    acc = k.acc[:, bass.ds(blk[c], 1), :].rearrange("p o w -> p (o w)")
                    dve.wait_ge(s["sums"], n + 1)
                    need(dve, s["acc"], n)
                    dve.tensor_tensor(acc, ps[:, 2 + c % 4, 0:D + GH], acc, ALU.add).then_inc(s["acc"], 1)

            def messages(g, v, half):
                if half == 0:
                    dve.wait_ge(v_in[v], 32 * (g - v) + 128)
                    dve.wait_ge(s["weight"], g + 1)
                c = slice(4 * half, 4 * half + 4)
                dve.tensor_tensor(msg[:, v % 2, c, 0:D].rearrange("p c (h d) -> p c h d", d=16),
                                  vg[:, v, c].rearrange("p c (h d) -> p c h d", d=16),
                                  over(msg[:, v % 2, 4 * half, D:], (D + GH, 4), (1, GH), (0, 16)),
                                  ALU.mult).then_inc(s["msg"], 1)

            def both(g, v):
                blk = None if at_start(g, 1) else blocks_of(nc, k, g - 1, ENG.DVE)
                for half in (0, 1):
                    if blk:
                        add(g - 1, half, blk)
                    if not (isinstance(g, int) and g == STEPS):
                        messages(g, v, half)

            dve.memset(k.acc, 0.0).then_inc(s["cleared"], 1)
            dve.wait_ge(s["cleared"], 1)
            for g, v in fours(dve, STEPS):
                dve.wait_ge(r_in[v], 4 * (g - v) + 16)
                need(dve, v_in[v], 32 * (g - v))
                dve.tensor_copy(t_int[:, v, :], over(rec[:, v, 0, R_T:], (REC, CH))).then_inc(s["t"], 1)
                for c in range(CH):
                    last = dve.tensor_scalar(hot[:, v, c, :], k.iota_b, rec[:, v, c, R_LO:R_LO + 1], None,
                                             ALU.is_equal)
                last.then_inc(s["hot"], 1)
                if not at_start(g, 2):
                    both(g - 2, (v - 2) % 4)
            for g in (STEPS - 2, STEPS - 1, STEPS):
                both(g, g % 4)


def phase_norm2(nc, k):
    w = Space(k.arena, k.ROUTE_END, k.BIG1)
    wr, bias, ones = w.f32(2, NE), w.f32(NE), w.f32(P)
    xm, x1, xn, g1 = w.f32(2, D), w.f32(2, D), w.f32(2, D), w.f32(2, D)
    den, inv_den, stat = w.f32(2, GH), w.f32(2, GH), w.f32(2, 16)
    top, ssum, sinv = w.f32(NB), w.f32(NB), w.f32(NB)
    ps = k.ps
    with ExitStack() as ctx:
        s = sems(nc, k, "norm2", "passed weights set x_in0 x_in1 den inv_den g1 x1 stats mean var root inv xn xT_ps xT "
                 "logit_ps logit out0 out1 d e")
        x_in, out = (s["x_in0"], s["x_in1"]), (s["out0"], s["out1"])
        block = ctx.enter_context(nc.Block())

        @block.sync
        def _(sp):
            sp.dma_start(wr, k.route_w).then_inc(s["weights"], 16)
            sp.dma_start(bias[0:1, :], k.route_bias).then_inc(s["weights"], 16)
            for b, u in blocks(sp):
                need(sp, s["x1"], b - 1)
                sp.dma_start(xm[:, u, :], k.xm_rows[bass.ds(b * P, P), :]).then_inc(x_in[u], 16)

        @block.gpsimd
        def _(pool):
            for b, u in blocks(pool):
                pool.wait_ge(s["x1"], b + 1)
                pool.dma_start(k.x1_rows[bass.ds(b * P, P), :], x1[:, u, :]).then_inc(out[u], 16)
            for u in (0, 1):
                pool.wait_ge(out[u], 16 * ((NB + 1 - u) // 2))

        @block.tensor
        def _(pe):
            pe.wait_ge(s["weights"], 32)
            pe.wait_ge(s["set"], 1)
            for b, u in blocks(pe):
                pe.wait_ge(s["xn"], b + 1)
                need(pe, s["xT"], b)
                for c in range(2):
                    mm = pe.transpose(ps[:, 0, c * P:(c + 1) * P], xn[:, u, c * P:(c + 1) * P], k.ident)
                mm.then_inc(s["xT_ps"], 1)
                pe.wait_ge(s["xT"], b + 1)
                need(pe, s["logit"], b - 1)
                for c in range(2):
                    pe.matmul(ps[0:NE, 1 + u, 0:P], wr[:, c, :], k.x2T[:, c, bass.ds(b * P, P)], start=(c == 0),
                              stop=False)
                pe.matmul(ps[0:NE, 1 + u, 0:P], bias[0:1, :], ones[0:1, :], start=False,
                          stop=True).then_inc(s["logit_ps"], 1)

        @block.scalar
        def _(act):
            def logits(b, u):
                act.wait_ge(s["logit_ps"], b + 1)
                act.copy(k.logit_T[0:NE, bass.ds(b * P, P)], ps[0:NE, 1 + u, 0:P]).then_inc(s["logit"], 1)

            for b, u in blocks(act):
                act.wait_ge(s["var"], b + 1)
                act.activation(stat[:, u, 9:10], stat[:, u, 8:9], ACT.Sqrt).then_inc(s["root"], 1)
                if not at_start(b, 1):
                    logits(b - 1, 1 - u)
                act.wait_ge(s["xT_ps"], b + 1)
                act.copy(k.x2T[:, :, bass.ds(b * P, P)], split(ps[:, 0, 0:2 * P], (2, P))).then_inc(s["xT"], 1)
            logits(NB - 1, 0)

        @block.vector
        def _(dve):
            dve.memset(ones, 1.0).then_inc(s["set"], 1)
            for b, u in blocks(dve):
                acc = k.acc[:, bass.ds(b, 1), :].rearrange("p o w -> p (o w)")
                dve.tensor_scalar(den[:, u, :], acc[:, D:], 1e-16, None, ALU.add).then_inc(s["den"], 1)
                dve.wait_ge(s["den"], b + 1)
                dve.reciprocal(inv_den[:, u, :], den[:, u, :]).then_inc(s["inv_den"], 1)
                dve.wait_ge(s["inv_den"], b + 1)
                dve.tensor_tensor(split(g1[:, u, :], (GH, 16)), split(acc[:, 0:D], (GH, 16)),
                                  over(inv_den[:, u, :], (1, GH), (0, 16)), ALU.mult).then_inc(s["g1"], 1)
                dve.wait_ge(s["g1"], b + 1)
                dve.wait_ge(x_in[u], 8 * (b - u) + 16)
                need(dve, out[u], 8 * (b - u))
                dve.tensor_tensor(x1[:, u, :], g1[:, u, :], xm[:, u, :], ALU.add).then_inc(s["x1"], 1)
                dve.wait_ge(s["x1"], b + 1)
                dve.bn_stats(stat[:, u, 0:6], x1[:, u, :]).then_inc(s["stats"], 1)
                dve.wait_ge(s["stats"], b + 1)
                dve.sem_inc(s["passed"])
                dve.bn_aggr(stat[:, u, 6:8], stat[:, u, 0:6]).then_inc(s["mean"], 1)
                dve.wait_ge(s["mean"], b + 1)
                dve.tensor_scalar(stat[:, u, 8:9], stat[:, u, 7:8], 1e-5, None, ALU.add).then_inc(s["var"], 1)
                dve.wait_ge(s["root"], b + 1)
                dve.reciprocal(stat[:, u, 10:11], stat[:, u, 9:10]).then_inc(s["inv"], 1)
                dve.wait_ge(s["inv"], b + 1)
                need(dve, s["xT_ps"], b - 1)
                dve.tensor_scalar(xn[:, u, :], x1[:, u, :], stat[:, u, 6:7], stat[:, u, 10:11],
                                  ALU.subtract, ALU.mult).then_inc(s["xn"], 1)


def phase_route(nc, k):
    w = Space(k.arena, k.ROUTE_END, k.BIG1)
    top, ssum, sinv = w.f32(NB), w.f32(NB), w.f32(NB)
    low = w.f32(NB, NE)
    v = [w.f32(16) for _ in range(8)]
    ps = k.ps
    with ExitStack() as ctx:
        s = sems(nc, k, "route", "turned low ex d turn_w wT bn root bn_in")
        block = ctx.enter_context(nc.Block())

        @block.sync
        def _(sp):
            for n, src in enumerate(k.bn):
                sp.dma_start(k.bn_sb[:, n, :], src).then_inc(s["bn_in"], 16)

        @block.tensor
        def _(pe):
            for b in range(NB):
                mm = pe.transpose(ps[:, 0, b * NE:(b + 1) * NE], k.logit_T[0:NE, b * P:(b + 1) * P],
                                  k.ident[0:NE, 0:NE])
            mm.then_inc(s["turned"], 1)
            pe.wait_ge(s["d"], 4)
            for b in range(NB):
                n = b // 4
                if n >= 2 and b % 4 == 0:
                    pe.wait_ge(s["wT"], n - 1)
                mm = pe.transpose(ps[0:NE, 1 + n % 2, (b % 4) * P:(b % 4 + 1) * P], k.gate[:, b, :], k.ident)
                if b % 4 == 3 or b == NB - 1:
                    mm.then_inc(s["turn_w"], 1)

        @block.scalar
        def _(act):
            act.wait_ge(s["low"], 1)
            act.activation(low, low, ACT.Exp).then_inc(s["ex"], 1)
            act.wait_ge(s["bn"], 2)
            act.activation(v[0], v[1], ACT.Sqrt)
            act.activation(v[2], v[3], ACT.Sqrt).then_inc(s["root"], 1)
            for n in range((NB + 3) // 4):
                m = min(4, NB - 4 * n) * P
                act.wait_ge(s["turn_w"], n + 1)
                act.copy(k.logit_T[0:NE, 4 * n * P:4 * n * P + m], ps[0:NE, 1 + n % 2, 0:m]).then_inc(s["wT"], 1)

        @block.vector
        def _(dve):
            done = 0

            def then(ins):
                nonlocal done
                done += 1
                ins.then_inc(s["d"], 1)
                dve.wait_ge(s["d"], done)

            logit = split(ps[:, 0, 0:NB * NE], (NB, NE))
            dve.wait_ge(s["turned"], 1)
            then(dve.tensor_reduce(top, logit, AX, ALU.max))
            dve.tensor_tensor(low, logit, over(top, (1, NB), (0, NE)), ALU.subtract).then_inc(s["low"], 1)
            dve.wait_ge(s["ex"], 1)
            then(dve.tensor_reduce(ssum, low, AX, ALU.add))
            then(dve.reciprocal(sinv, ssum))
            then(dve.tensor_tensor(k.gate, low, over(sinv, (1, NB), (0, NE)), ALU.mult))
            dve.wait_ge(s["bn_in"], 16 * 10)
            for layer in (0, 1):
                dve.tensor_scalar(v[1 + 2 * layer], k.bn_sb[:, 5 * layer + 4, :], 1e-3, None,
                                  ALU.add).then_inc(s["bn"], 1)
            dve.wait_ge(s["root"], 1)
            for layer in (0, 1):
                bias, gain, shift, mean, _var = (k.bn_sb[:, 5 * layer + n, :] for n in range(5))
                then(dve.reciprocal(v[4], v[2 * layer]))
                then(dve.tensor_tensor(k.scale[:, layer, :], gain, v[4], ALU.mult))
                then(dve.tensor_tensor(v[5], bias, mean, ALU.subtract))
                then(dve.tensor_tensor(v[6], v[5], k.scale[:, layer, :], ALU.mult))
                then(dve.tensor_tensor(k.shift[:, layer, :], v[6], shift, ALU.add))


def phase_experts(nc, k):
    w = Space(k.arena, k.ROUTE_END, k.BIG1)
    w1, w2 = w.f32(NE, 2, D), w.f32(NE, 2, D)
    h1, h2 = w.f32(2, CB * P), w.f32(2, CB * P)
    bo, gate_T = w.f32(D), w.f32(CB * P)
    y = w.f32(CB, D)
    rest = Space(k.acc_words, 0, NB * (D + GH))
    w3, x1 = rest.f32(NE, 2, D), rest.f32(CB, D)
    HALF = CB * P // 2
    ps = k.ps
    ROUNDS = NB // CB
    with ExitStack() as ctx:
        s = sems(nc, k, "experts", "weights x_in h_ps h y_ps y out gate seed_ps seed")
        block = ctx.enter_context(nc.Block())

        @block.sync
        def _(sp):
            for dst, src in ((w1, k.w1), (w2, k.w2), (w3, k.w3)):
                sp.dma_start(dst, src).then_inc(s["weights"], 16)
            sp.dma_start(bo[0:NE, :], k.out_bias).then_inc(s["weights"], 16)
            for r in rounds(sp, ROUNDS):
                need(sp, s["seed"], CB * r)
                sp.dma_start(x1, k.x1_rows[bass.ds(r * CB * P, CB * P), :].rearrange("(n p) d -> p n d", p=P)
                             ).then_inc(s["x_in"], 16)
                sp.wait_ge(s["y"], NE * CB * (r + 1))
                sp.dma_start(k.out[bass.ds(r * CB * P, CB * P), :].rearrange("(n p) d -> p n d", p=P), y
                             ).then_inc(s["out"], 16)
            sp.wait_ge(s["out"], 16 * ROUNDS)

        @block.tensor
        def _(pe):
            def hidden(r, e, layer, wt):
                for ot in (0, 1):
                    m = 4 * e + 2 * layer + ot
                    need(pe, s["h"], 4 * NE * r + m - 1)
                    for half in (0, 1):
                        for c in (0, 1):
                            if layer == 0:
                                moving = k.x2T[:, c, bass.ds(r * CB * P + half * HALF, HALF)]
                            else:
                                moving = h1[:, c, half * HALF:(half + 1) * HALF]
                            mm = pe.matmul(ps[:, 2 * (m % 2) + half, 0:HALF], wt[:, e, c, ot * P:(ot + 1) * P],
                                           moving, start=(c == 0), stop=(c == 1))
                    mm.then_inc(s["h_ps"], 1)

            def last(r, e):
                pe.wait_ge(s["h"], 4 * NE * r + 4 * e + 4)
                for nb in range(CB):
                    need(pe, s["y"], CB * NE * r + CB * e + nb - 3)
                    bank = 4 + (CB * e + nb) % 4
                    for c in (0, 1):
                        mm = pe.matmul(ps[:, bank, 0:D], h2[:, c, nb * P:(nb + 1) * P], w3[:, e, c, :],
                                       start=(c == 0), stop=(c == 1))
                    mm.then_inc(s["y_ps"], 1)

            pe.wait_ge(s["weights"], 64)
            for r in rounds(pe, ROUNDS):
                need(pe, s["y"], NE * CB * r)
                pe.wait_ge(s["gate"], r + 1)
                for nb in range(CB):
                    need(pe, s["seed"], CB * r + nb)
                    pe.matmul(ps[:, 4, 0:D], gate_T[0:NE, nb * P:(nb + 1) * P], bo[0:NE, :], start=True,
                              stop=True).then_inc(s["seed_ps"], 1)
                need(pe, s["seed"], CB * r + CB)
                for e in range(NE):
                    hidden(r, e, 0, w1)
                    if e >= 1:
                        last(r, e - 1)
                    pe.wait_ge(s["h"], 4 * NE * r + 4 * e + 2)
                    hidden(r, e, 1, w2)
                last(r, NE - 1)

        @block.scalar
        def _(act):
            for r in rounds(act, ROUNDS):
                need(act, s["seed_ps"], CB * r)
                act.copy(gate_T[0:NE, :], k.logit_T[0:NE, bass.ds(r * CB * P, CB * P)]).then_inc(s["gate"], 1)
                for e in range(NE):
                    for layer in (0, 1):
                        for ot in (0, 1):
                            m = 4 * e + 2 * layer + ot
                            act.wait_ge(s["h_ps"], 4 * NE * r + m + 1)
                            if layer == 1:
                                need(act, s["y_ps"], CB * NE * r + CB * e)
                            act.activation(split((h1, h2)[layer][:, ot], (2, HALF)),
                                           ps[:, 2 * (m % 2):2 * (m % 2) + 2, 0:HALF], ACT.Relu,
                                           bias=k.shift[:, layer, 2 * e + ot:2 * e + ot + 1],
                                           scale=k.scale[:, layer, 2 * e + ot:2 * e + ot + 1]).then_inc(s["h"], 1)

        @block.vector
        def _(dve):
            for r in rounds(dve, ROUNDS):
                dve.wait_ge(s["x_in"], 16 * (r + 1))
                need(dve, s["out"], 16 * r)
                for nb in range(CB):
                    dve.wait_ge(s["seed_ps"], CB * r + nb + 1)
                    dve.tensor_tensor(y[:, nb, :], ps[:, 4, 0:D], x1[:, nb, :], ALU.add).then_inc(s["seed"], 1)
                dve.wait_ge(s["seed"], CB * r + CB)
                for e in range(NE):
                    for nb in range(CB):
                        n = CB * NE * r + CB * e + nb
                        dve.wait_ge(s["y_ps"], n + 1)
                        need(dve, s["y"], n - CB + 1)
                        gate = k.gate[:, bass.ds(r * CB + nb, 1), e:e + 1].rearrange("p a b -> p (a b)")
                        dve.scalar_tensor_tensor(y[:, nb, :], ps[:, 4 + (CB * e + nb) % 4, 0:D], gate, y[:, nb, :],
                                                 ALU.mult, ALU.add).then_inc(s["y"], 1)


def build(nc, x, src_lin, src_col, dst_col, attr, consts, gnn_w, mix_w, node_bias, temperature, proj_w, proj_bias,
          rpe_w, route_w, route_bias, w1, w2, w3, out_bias, bn, out, upto=99, probes=None):
    k = Shared()
    k.x, k.src_lin, k.src_col, k.dst_col, k.attr = x, src_lin, src_col, dst_col, attr
    k.consts, k.gnn_w, k.mix_w, k.node_bias, k.temperature = consts, gnn_w, mix_w, node_bias, temperature
    k.proj_w, k.proj_bias, k.rpe_w, k.route_w, k.route_bias = proj_w, proj_bias, rpe_w, route_w, route_bias
    k.w1, k.w2, k.w3, k.out_bias, k.bn = w1, w2, w3, out_bias, bn
    k.out = out
    scratch = lambda n, shape, dt=F32: nc.dram_tensor(n, shape, dt).ap()
    k.row_s, k.row_lo = scratch("row_s", [EP]), scratch("row_lo", [EP], BF16)
    k.records = scratch("records", [SLOTS, REC])
    k.k_rows, k.v_rows = scratch("k_rows", [NP, P]), scratch("v_rows", [NP, D])
    k.kext_rows, k.v1_rows = scratch("kext_rows", [NP, MH * 48]), scratch("v1_rows", [NP, MH * 33])
    k.qT_rows = scratch("qT_rows", [NB * 97, MH * P], BF16)
    k.xm_rows, k.x1_rows = scratch("xm_rows", [NP, D]), scratch("x1_rows", [NP, D])
    with ExitStack() as ctx:
        q_words, breaks_words, score_words, acc_words = NB * 3 * P // 2, STEPS * P // 2 + 16, STEPS * P, NB * (D + GH)
        total = 53200
        arena = ctx.enter_context(nc.sbuf_tensor("arena", [P, total], F32))
        k.arena = arena
        k.sems = []
        c = Space(arena, 0, total)
        k.cst = c.f32(C_END + C_END % 2)[:, 0:C_END]
        k.ident_b, k.iota_b, k.sel_b = c.bf16(P), c.bf16(P), c.bf16(7, P)
        k.bias3, k.ones_b = c.bf16(1280 + D), c.bf16(P)
        k.start, k.blocks = c.f32(NB), c.f32(CH * STEPS, dt=I32)
        k.ident = k.cst[:, C_ID:C_ID + P]
        k.Q0 = c.at
        k.WORK0 = k.Q0 + q_words
        big2 = total - acc_words
        k.BIG1 = big2 - score_words
        fl0 = k.BIG1 - breaks_words
        k.BIG2 = big2
        k.COLS0 = total - 4 * ET
        k.MT0 = k.COLS0 - 40 * P
        k.FL0 = fl0
        at = lambda a, b: Space(arena, a, b)
        k.qtab = at(k.Q0, k.WORK0).bf16(NB, 3, P)
        k.cols = at(k.COLS0, total).f32(4, ET)
        k.mt = at(k.MT0, k.COLS0).f32(20, 2, P)
        k.breaks = at(fl0, k.BIG1).bf16(STEPS * P + 2)
        k.scores = at(k.BIG1, big2).f32(STEPS * P)
        k.x2T = at(k.BIG1, big2).f32(2, NP)
        k.owner = at(big2, total).f32(STEPS * P)
        k.acc_words = at(big2, total).f32(acc_words)
        k.acc = split(k.acc_words, (NB, D + GH))
        r = at(k.Q0, k.BIG1)
        k.gate, k.logit_T, k.scale, k.shift, k.bn_sb = (r.f32(NB, NE), r.f32(NP), r.f32(2, 16), r.f32(2, 16),
                                                       r.f32(10, 16))
        k.ROUTE_END = r.at
        psum = ctx.enter_context(nc.psum_tensor("banks", [P, 8, 512], F32))
        k.ps = psum[:, :, :]
        k.ps_b = psum[:, :, :].rearrange("p b w -> p (b w)").bitcast(BF16).rearrange("p (b w) -> p b w", b=8)
        phases = [phase_setup, phase_nodes, phase_kv_sums, phase_starts,
                  phase_mix_scatter, phase_compat, phase_seg_max, phase_messages, phase_norm2, phase_route,
                  phase_experts]
        for n, phase in enumerate(phases[:upto]):
            phase(nc, k)
            if phase is phase_mix_scatter or n == len(phases) - 1:
                nc.clear_and_free_semaphores(k.sems)
                nc.all_engine_barrier()
                k.sems = []
        if probes:
            probes(nc, k)


def layout(inputs):
    a = {n: np.asarray(v) for n, v in inputs.items()}
    f = np.float32
    pad_rows = lambda v, n, fill=0: np.concatenate([v, np.full((n - v.shape[0],) + v.shape[1:], fill, v.dtype)])
    src = pad_rows(a["src"], EP, FAKE)
    dst = pad_rows(a["dst"], EP)
    attr = pad_rows(a["edge_attr_18"], EP)
    tiles = lambda v: np.ascontiguousarray(v.reshape(ET, P, *v.shape[1:]).swapaxes(0, 1))
    inner = lambda wt: np.ascontiguousarray(wt.reshape(2, P, -1).swapaxes(0, 1))
    experts = lambda wt: np.ascontiguousarray(wt.reshape(NE, 2, P, D).transpose(2, 0, 1, 3))
    units = lambda v: np.ascontiguousarray(v.reshape(NE, 2, P).transpose(2, 0, 1).reshape(P, 2 * NE))
    row = lambda v: np.ascontiguousarray(v.reshape(1, -1))
    one = np.concatenate([np.concatenate([a["L0_gnn_Wq_rpe"], a["L0_gnn_Wk_rpe"]], 1),
                          np.concatenate([row(a["L0_gnn_bq_rpe"]), row(a["L0_gnn_bk_rpe"])], 1),
                          np.zeros((REC - 19, 2 * P), f)])
    rpe = np.zeros((4, REC, 4, 2 * P), f)
    for j in range(4):
        rpe[j, :, j] = one
    r = {
        "x": pad_rows(a["x"], NP), "src_lin": src.reshape(P, ET), "src_col": tiles(src), "dst_col": tiles(dst),
        "attr": tiles(attr), "consts": constants(),
        "gnn_w": inner(a["L0_gnn_Wqkv"]), "mix_w": inner(a["L0_mix_Wqkv"].T),
        "node_bias": np.concatenate([row(a["L0_gnn_bqkv"]), row(a["L0_mix_bqkv"])], 1),
        "temperature": row(a["L0_mix_temperature"]),
        "proj_w": np.ascontiguousarray(a["L0_mix_Wproj"].T.reshape(4, 64, D).swapaxes(0, 1)), "proj_bias": row(a["L0_mix_bproj"]),
        "rpe_w": rpe.reshape(P, 4, 2 * P),
        "route_w": inner(a["L0_ffn_Wr"]), "route_bias": row(a["L0_ffn_br"]),
        "w1": experts(a["L0_ffn_W1"]), "w2": experts(a["L0_ffn_W2"]), "w3": experts(a["L0_ffn_Wo"]),
        "out_bias": a["L0_ffn_bo"],
    }
    for layer in ("1", "2"):
        for n in ("b", "g", "be", "m", "v"):
            r[f"bn_{n}{layer}"] = units(a[f"L0_ffn_{n}{layer}"])
    return {n: np.ascontiguousarray(v) for n, v in r.items()}


def kernel(**inputs):
    import concourse.bacc as bacc
    from concourse.bass_utils import run_bass_kernel_spmd

    arrays = layout(inputs)
    nc = bacc.Bacc("TRN2", target_bir_lowering=False, num_devices=1)
    args = {n: nc.dram_tensor(f"in_{n}", v.shape, mybir.dt.from_np(v.dtype), kind="ExternalInput").ap()
            for n, v in arrays.items()}
    out = nc.dram_tensor("out", [NP, D], F32, kind="ExternalOutput").ap()
    bn = [args.pop(n) for n in list(args) if n.startswith("bn_")]
    build(nc, **args, bn=bn, out=out)
    result = run_bass_kernel_spmd(nc, [{f"in_{n}": v for n, v in arrays.items()}], core_ids=[0])
    return result.results[0]["out"][:N]
```

```python
from contextlib import ExitStack

import numpy as np

import concourse.bass as bass
from concourse import mybir

F32 = mybir.dt.float32
BF16 = mybir.dt.bfloat16
I32 = mybir.dt.int32
F32R = mybir.dt.float32r
ALU = mybir.AluOpType
ACT = mybir.ActivationFunctionType
AX = mybir.AxisListType.X
ENG = mybir.EngineType

P = 128
N, D = 6250, 256
NB = -(-N // P)
NP = NB * P
E = 100000
ET = -(-E // (16 * P)) * 16
EP = ET * P
FAKE = NB * P - 1
CH = 8
STEPS = -(-(ET + NB - 1) // (4 * CH)) * 4
SLOTS = CH * STEPS * P
REC = 32
R_ONE, R_T, R_S, R_LO = 18, 19, 20, 21
GH, GD = 16, 8
MH, MD = 8, 32
ND = 17
PAIRS = ND * MD + MD + 1
SBUF_WORDS = 53200
BLANK = 16
NE = 8
CB = 7
NEG = -1.0e38
MSCALE = float(MD) ** 0.25

C_ID, C_IOTA, C_BEFORE, C_AFTER = 0, 128, 256, 384
C_SEL = 512
C_P = C_SEL + 7 * 128
C_MASK = C_P + 1
C_TILE = C_MASK + NB
C_END = C_TILE + CH * STEPS


def constants():
    c = np.zeros((P, C_END), np.float32)
    r = np.arange(P)
    c[:, C_ID:C_ID + P] = np.eye(P)
    c[:, C_IOTA:C_IOTA + P] = r[None, :]
    c[:, C_BEFORE:C_BEFORE + P] = r[None, :] < r[:, None]
    c[:, C_AFTER:C_AFTER + P] = r[:, None] < r[None, :]
    sel = c[:, C_SEL:C_SEL + 7 * P].reshape(P, 7, P)
    i = np.arange(MD)
    for part in range(3):
        for dd in range(4):
            sel[part * MD + i, 0, dd * MD + i] = 1
            for j in range(4):
                sel[part * MD + (i + 4 * j + dd) % MD, 1 + j, dd * MD + i] = 1
        sel[part * MD + i, 5, i] = 1
        sel[part * MD + (i + 16) % MD, 6, i] = 1
        sel[part * MD + i, 6, MD + i] = 1
    sel[96, 5, MD:2 * MD + 1] = 1
    sel[96, 6, 2 * MD] = 1
    c[:, C_P] = r
    node = np.arange(NP).reshape(NB, P).T
    c[:, C_MASK:C_MASK + NB] = (node < N) / np.float32(N)
    tile = np.arange(CH)[None, :] * STEPS + np.arange(STEPS)[:, None]
    c[:, C_TILE:C_END] = tile.reshape(-1)[None, :]
    return c


class Space:

    def __init__(self, arena, at, end):
        self.arena, self.at, self.end = arena, at, end

    def f32(self, *shape, dt=None):
        n = int(np.prod(shape))
        assert self.at + n <= self.end, (self.at, n, self.end)
        ap = self.arena[:, self.at:self.at + n]
        self.at += n
        if dt is not None:
            ap = ap.bitcast(dt)
        return split(ap, shape)

    def bf16(self, *shape):
        n = int(np.prod(shape))
        assert n % 2 == 0 and self.at + n // 2 <= self.end, (self.at, n, self.end)
        ap = self.arena[:, self.at:self.at + n // 2].bitcast(BF16)
        self.at += n // 2
        return split(ap, shape)


def split(ap, shape):
    if len(shape) == 1:
        return ap
    names = "abcd"[:len(shape)]
    return ap.rearrange(f"p ({' '.join(names)}) -> p {' '.join(names)}",
                        **{k: v for k, v in zip(names[1:], shape[1:])})


def over(ap, *dims):
    return bass.AP(tensor=ap.tensor, offset=ap.offset, ap=[list(ap.ap[0]), *[list(d) for d in dims]])


class Shared:
    pass


def rounds(eng, n):
    yield 0
    with eng.Fori(1, n) as i:
        yield i


def inner_rounds(eng, n):
    yield 0
    with eng.Fori(1, n - 1) as i:
        yield i
    yield n - 1


def twos(eng, n):
    for r in range(3):
        yield r, r % 2
    with eng.Fori(2, n // 2 + 1) as i:
        yield 2 * i - 1, 1
        yield 2 * i, 0


def fours(eng, n):
    for v in range(4):
        yield v, v
    with eng.Fori(1, n // 4) as i:
        for v in range(4):
            yield 4 * i + v, v


def blocks(eng):
    yield 0, 0
    yield 1, 1
    with eng.Fori(1, NB // 2) as i:
        for u in (0, 1):
            yield 2 * i + u, u
    yield NB - 1, 0


def at_start(b, n):
    return isinstance(b, int) and b < n


def need(eng, sem, value):
    if isinstance(value, int) and value <= 0:
        return
    eng.wait_ge(sem, value)


def sems(nc, k, phase, names):
    s = {n: nc.alloc_semaphore(f"{phase}_{n}") for n in names.split()}
    k.sems += s.values()
    return s


def one_hot_high(k, dve, high, n):
    col = k.cols[:, 3, bass.ds(n * 8, 8)].rearrange("p (j o) -> p j o", o=1)
    return dve.tensor_tensor(high, over(k.iota_b[:, 0:NB], (0, 8), (1, NB)), col.to_broadcast([P, 8, NB]), ALU.is_equal)


def one_hot_low(k, dve, low, n):
    col = k.cols[:, 2, bass.ds(n * 8, 8)].rearrange("p (j o) -> p j o", o=1)
    return dve.tensor_tensor(low, over(k.iota_b, (0, 8), (1, P)), col.to_broadcast([P, 8, P]), ALU.is_equal)


def phase_setup(nc, k):
    w = Space(k.arena, k.WORK0, k.BIG2)
    lin, scol_i, tcol_i, half = (w.f32(ET, dt=I32) for _ in range(4))
    bias = w.f32(k.bias3.shape[1])
    rest, part2, part3 = w.f32(k.bias3.shape[1]), w.bf16(k.bias3.shape[1]), w.bf16(k.bias3.shape[1])
    kept = Space(k.arena, k.BIG2, k.MT0)
    slin, llin, k.blank = kept.f32(ET), kept.bf16(ET), kept.f32(BLANK, REC)
    with ExitStack() as ctx:
        s = sems(nc, k, "setup", "loaded low_row ints blanked consts bias parts moved")
        k.rows_stored, k.blanks_stored = nc.alloc_semaphore("rows_stored"), nc.alloc_semaphore("blanks_stored")
        k.sems += [k.rows_stored, k.blanks_stored]
        block = ctx.enter_context(nc.Block())

        @block.sync
        def _(sp):
            sp.dma_start(scol_i, k.src_col).then_inc(s["loaded"], 16)
            sp.dma_start(lin, k.src_lin).then_inc(s["loaded"], 16)
            sp.dma_start(tcol_i, k.dst_col).then_inc(s["loaded"], 16)
            sp.dma_start(bias[0:1, 0:1280], k.node_bias).then_inc(s["bias"], 16)
            sp.dma_start(bias[0:1, 1280:], k.proj_bias).then_inc(s["bias"], 16)
            sp.dma_start(k.cst, k.consts).then_inc(s["consts"], 16)
            sp.wait_ge(s["parts"], 4)
            sp.dma_start(k.bias3[1:2, :], part2[0:1, :]).then_inc(s["moved"], 16)
            sp.dma_start(k.bias3[2:3, :], part3[0:1, :]).then_inc(s["moved"], 16)
            sp.wait_ge(s["low_row"], 2)
            sp.dma_start(k.row_s.rearrange("(p c) -> p c", p=P), slin).then_inc(k.rows_stored, 16)
            sp.dma_start(k.row_lo.rearrange("(p c) -> p c", p=P), llin).then_inc(k.rows_stored, 16)
            sp.wait_ge(s["moved"], 32)

        @block.scalar
        def _(act):
            act.wait_ge(s["consts"], 16)
            act.copy(k.ident_b, k.cst[:, C_ID:C_ID + P])
            act.copy(k.iota_b, k.cst[:, C_IOTA:C_IOTA + P])
            act.copy(k.sel_b, split(k.cst[:, C_SEL:C_SEL + 7 * P], (7, P)))

        @block.vector
        def _(dve):
            dve.memset(k.ones_b, 1.0)
            dve.memset(k.blank, 0.0).then_inc(s["blanked"], 1)
            dve.wait_ge(s["blanked"], 1)
            dve.memset(k.blank[:, :, R_S:R_S + 2], 300.0).then_inc(s["blanked"], 1)
            dve.wait_ge(s["bias"], 32)
            dve.tensor_copy(k.bias3[0:1, :], bias[0:1, :]).then_inc(s["parts"], 1)
            dve.wait_ge(s["parts"], 1)
            dve.tensor_tensor(rest[0:1, :], bias[0:1, :], k.bias3[0:1, :], ALU.subtract).then_inc(s["parts"], 1)
            dve.wait_ge(s["parts"], 2)
            dve.tensor_copy(part2[0:1, :], rest[0:1, :]).then_inc(s["parts"], 1)
            dve.wait_ge(s["parts"], 3)
            dve.tensor_tensor(part3[0:1, :], rest[0:1, :], part2[0:1, :], ALU.subtract).then_inc(s["parts"], 1)
            dve.wait_ge(s["loaded"], 48)
            dve.tensor_copy(slin, lin).then_inc(s["low_row"], 1)
            dve.tensor_scalar(half, lin, 127, None, ALU.bitwise_and).then_inc(s["ints"], 1)
            dve.wait_ge(s["ints"], 1)
            dve.tensor_copy(llin, half).then_inc(s["low_row"], 1)
            dve.tensor_copy(k.cols[:, 0], tcol_i)
            dve.tensor_copy(k.cols[:, 1], scol_i)
            dve.wait_ge(s["low_row"], 2)
            dve.tensor_scalar(half, scol_i, 127, None, ALU.bitwise_and).then_inc(s["ints"], 1)
            dve.wait_ge(s["ints"], 2)
            dve.tensor_copy(k.cols[:, 2], half).then_inc(s["ints"], 1)
            dve.wait_ge(s["ints"], 3)
            dve.tensor_scalar(half, scol_i, 7, None, ALU.arith_shift_right).then_inc(s["ints"], 1)
            dve.wait_ge(s["ints"], 4)
            dve.tensor_copy(k.cols[:, 3], half)


def phase_nodes(nc, k):
    w = Space(k.arena, k.WORK0, k.BIG2)
    wg, wm = w.f32(2, 512), w.f32(2, 768)
    ones, factor = w.f32(P), w.f32(16)
    low, high, zero = w.bf16(4, 8, P), w.bf16(4, 8, NB), w.bf16(P)
    xb, xn, xT = w.f32(2, D), w.f32(2, D), w.f32(2, 2, P)
    stat, gnn = w.f32(2, 16), w.f32(2, 512)
    qs, rest = w.f32(2, P), w.f32(2, P)
    mix, sq = w.f32(2, 16, MD), w.f32(2, 16, MD)
    nrm = w.f32(2, 5, 16)
    kext, v1, qn, qrest = w.f32(2, MH, 48), w.f32(2, MH, 33), w.f32(2, MH, MD), w.f32(2, MH, MD)
    parts, qTs = w.bf16(2, MH, 98), w.bf16(2, MH, P)
    ps = k.ps
    with ExitStack() as ctx:
        s = sems(nc, k, "nodes", "passed weights set x_in0 x_in1 stats mean var root_v inv xn xT_ps xT proj gnn mixed "
                 "squared scaled qpart v1 norm2 root_n clip recip factor normed keys split qT_ps qT "
                 "k_out0 k_out1 v_out0 v_out1 e_out0 e_out1 w_out0 w_out1 q_out0 q_out1 hot hist")
        x_in, k_out, v_out, e_out, w_out, q_out = (
            (a, b) for a, b in ((s["x_in0"], s["x_in1"]), (s["k_out0"], s["k_out1"]), (s["v_out0"], s["v_out1"]),
                                (s["e_out0"], s["e_out1"]), (s["w_out0"], s["w_out1"]), (s["q_out0"], s["q_out1"])))
        block = ctx.enter_context(nc.Block())

        @block.sync
        def _(sp):
            sp.dma_start(wg, k.gnn_w).then_inc(s["weights"], 16)
            sp.dma_start(wm, k.mix_w).then_inc(s["weights"], 16)
            sp.dma_start(factor[:, 0:MH], k.temperature.to_broadcast([P, MH])).then_inc(s["weights"], 16)

            def default_records(first):
                sp.dma_start(k.records[bass.ds(first, BLANK * P), :].rearrange("(p r) f -> p r f", p=P),
                             k.blank).then_inc(k.blanks_stored, 16)

            for b, u in blocks(sp):
                need(sp, s["xn"], b - 1)
                sp.dma_start(xb[:, u, :], k.x[bass.ds(b * P, P), :]).then_inc(x_in[u], 16)
                default_records(b * BLANK * P)
            for n in range(NB * BLANK * P, SLOTS, BLANK * P):
                default_records(n)

        @block.gpsimd
        def _(pool):
            for b, u in blocks(pool):
                pool.wait_ge(s["gnn"], b + 1)
                pool.dma_start(k.k_rows[bass.ds(b * P, P), :], gnn[:, u, P:2 * P]).then_inc(k_out[u], 16)
                pool.dma_start(k.v_rows[bass.ds(b * P, P), :], gnn[:, u, 2 * P:]).then_inc(v_out[u], 16)
                pool.wait_ge(s["v1"], 2 * b + 2)
                pool.dma_start(k.v1_rows[bass.ds(b * P, P), :],
                               v1[:, u].rearrange("p h i -> p (h i)")).then_inc(w_out[u], 16)
                pool.wait_ge(s["factor"], b + 1)
                if not at_start(b, 2):
                    pool.wait_ge(e_out[u], 8 * (b - u))
                fk = nrm[:, u, 4, 8:16]
                pool.tensor_tensor(kext[:, u, :, 0:32], mix[:, u, 8:16], over(fk, (1, 8), (0, 32)),
                                   ALU.mult).then_inc(s["keys"], 1)
                pool.tensor_tensor(kext[:, u, :, 32:48], mix[:, u, 8:16, 0:16], over(fk, (1, 8), (0, 16)),
                                   ALU.mult).then_inc(s["keys"], 1)
                pool.wait_ge(s["keys"], 2 * b + 2)
                pool.dma_start(k.kext_rows[bass.ds(b * P, P), :],
                               kext[:, u].rearrange("p h i -> p (h i)")).then_inc(e_out[u], 16)
                pool.wait_ge(s["qT"], b + 1)
                pool.dma_start(k.qT_rows[bass.ds(b * 97, 97), :],
                               qTs[0:97, u].rearrange("p h i -> p (h i)")).then_inc(q_out[u], 16)
            for u in (0, 1):
                for sem in (k_out[u], v_out[u], w_out[u], e_out[u], q_out[u]):
                    pool.wait_ge(sem, 16 * ((NB + 1 - u) // 2))

        @block.tensor
        def _(pe):
            def histogram(b, u):
                for half in (0, 1):
                    pe.wait_ge(s["hot"], 2 * b + half + 1)
                    for j in range(8):
                        mm = pe.matmul(ps[:, 5, 0:NB], low[:, 2 * u + half, j, :], high[:, 2 * u + half, j, :],
                                       start=False, stop=False, skip_group_check=True)
                    mm.then_inc(s["hist"], 1)

            def project(b, u):
                pe.wait_ge(s["xT"], b + 1)
                need(pe, s["squared"], b)
                for bank, wt, c0, n, at in ((1, wg, 0, 512, 0), (2, wm, 0, 512, 512), (3, wm, 512, 256, 1024)):
                    for c in range(2):
                        pe.matmul(ps[:, bank, 0:n], xT[:, u, c, :], wt[:, c, c0:c0 + n],
                                  start=(c == 0), stop=False)
                    mm = pe.matmul(ps[:, bank, 0:n], k.ones_b[0:3, :], k.bias3[0:3, at:at + n],
                                   start=False, stop=True)
                mm.then_inc(s["proj"], 1)

            def queries_T(b, u):
                pe.wait_ge(s["split"], 4 * b + 4)
                need(pe, s["qT"], b)
                for h in range(MH):
                    mm = pe.transpose(k.ps_b[0:97, 4, h * P:(h + 1) * P], parts[:, u, h, 0:97], k.ident_b)
                mm.then_inc(s["qT_ps"], 1)

            pe.wait_ge(s["weights"], 48)
            pe.wait_ge(s["set"], 1)
            pe.matmul(ps[:, 5, 0:NB], zero, zero[:, 0:NB], start=True, stop=False, skip_group_check=True)
            for b, u in blocks(pe):
                pe.wait_ge(s["xn"], b + 1)
                need(pe, s["xT"], b)
                for c in range(2):
                    mm = pe.transpose(ps[:, 0, c * P:(c + 1) * P], xn[:, u, c * P:(c + 1) * P], k.ident)
                mm.then_inc(s["xT_ps"], 1)
                if not at_start(b, 1):
                    histogram(b - 1, 1 - u)
                    project(b - 1, 1 - u)
                if not at_start(b, 2):
                    queries_T(b - 2, u)
            histogram(NB - 1, 0)
            project(NB - 1, 0)
            queries_T(NB - 2, 1)
            queries_T(NB - 1, 0)

        @block.scalar
        def _(act):
            def root_of_norms(b, u):
                act.wait_ge(s["norm2"], b + 1)
                act.activation(nrm[:, u, 1], nrm[:, u, 0], ACT.Sqrt).then_inc(s["root_n"], 1)

            def queries_T(b, u):
                act.wait_ge(s["qT_ps"], b + 1)
                need(act, q_out[u], 8 * (b - u))
                act.copy(qTs[0:97, u], split(k.ps_b[0:97, 4, :], (MH, P))).then_inc(s["qT"], 1)

            def keep(b, u):
                act.wait_ge(s["proj"], b + 1)
                need(act, k_out[u], 8 * (b - u))
                need(act, v_out[u], 8 * (b - u))
                need(act, s["split"], 4 * b - 4)
                need(act, s["keys"], 2 * b - 2)
                act.copy(gnn[:, u, P:], ps[:, 1, P:]).then_inc(s["gnn"], 1)
                act.activation(qs[:, u, :], ps[:, 1, 0:P], ACT.Copy, scale=GD ** -0.5).then_inc(s["scaled"], 1)
                q = k.qtab[:, bass.ds(b, 1), 0, :].rearrange("p o d -> p (o d)")
                act.activation(q, ps[:, 1, 0:P], ACT.Copy, scale=GD ** -0.5).then_inc(s["scaled"], 1)
                act.activation(mix[:, u, 0:8], split(ps[:, 2, 0:D], (8, MD)), ACT.Copy,
                               scale=MSCALE).then_inc(s["mixed"], 1)
                act.copy(mix[:, u, 8:16], split(ps[:, 2, D:], (8, MD))).then_inc(s["mixed"], 1)
                need(act, w_out[u], 8 * (b - u))
                mask = k.cst[:, bass.ds(C_MASK + b, 1)]
                act.activation(v1[:, u, :, 1:33], split(ps[:, 3, 0:D], (8, MD)), ACT.Copy, scale=mask
                               ).then_inc(s["v1"], 1)
                act.activation(v1[:, u, :, 0:1], split(ones[:, 0:MH], (MH, 1)), ACT.Copy, scale=mask
                               ).then_inc(s["v1"], 1)
                act.wait_ge(s["mixed"], 2 * b + 2)
                act.activation(sq[:, u], mix[:, u, 0:16], ACT.Square).then_inc(s["squared"], 1)

            def root_of_variance(b, u):
                act.wait_ge(s["var"], b + 1)
                act.activation(stat[:, u, 9:10], stat[:, u, 8:9], ACT.Sqrt).then_inc(s["root_v"], 1)

            root_of_variance(0, 0)
            for b, u in blocks(act):
                act.wait_ge(s["xT_ps"], b + 1)
                need(act, s["proj"], b - 1)
                act.copy(xT[:, u], split(ps[:, 0, 0:2 * P], (2, P))).then_inc(s["xT"], 1)
                if not (isinstance(b, int) and b == NB - 1):
                    root_of_variance(b + 1, 1 - u)
                if not at_start(b, 2):
                    root_of_norms(b - 2, u)
                if not at_start(b, 1):
                    keep(b - 1, 1 - u)
                if not at_start(b, 2):
                    queries_T(b - 2, u)
            keep(NB - 1, 0)
            for b in (NB - 2, NB - 1):
                root_of_norms(b, b % 2)
                queries_T(b, b % 2)

        @block.vector
        def _(dve):
            def one_hot(b, u, half, part):
                n = 2 * b + half
                if part == 0:
                    need(dve, s["hist"], n - 3)
                    one_hot_high(k, dve, high[:, 2 * u + half], n)
                else:
                    one_hot_low(k, dve, low[:, 2 * u + half], n).then_inc(s["hot"], 1)

            def variance(b, u, between):
                dve.wait_ge(x_in[u], 8 * (b - u) + 16)
                dve.bn_stats(stat[:, u, 0:6], xb[:, u, :]).then_inc(s["stats"], 1)
                if between:
                    one_hot(b - 1, 1 - u, 0, 1)
                dve.wait_ge(s["stats"], b + 1)
                dve.sem_inc(s["passed"])
                dve.bn_aggr(stat[:, u, 6:8], stat[:, u, 0:6]).then_inc(s["mean"], 1)
                if between:
                    one_hot(b - 1, 1 - u, 1, 0)
                dve.wait_ge(s["mean"], b + 1)
                dve.tensor_scalar(stat[:, u, 8:9], stat[:, u, 7:8], 1e-5, None, ALU.add).then_inc(s["var"], 1)

            def layer_norm(b, u):
                dve.wait_ge(s["root_v"], b + 1)
                dve.reciprocal(stat[:, u, 10:11], stat[:, u, 9:10]).then_inc(s["inv"], 1)
                one_hot(b, u, 0, 0)
                dve.wait_ge(s["inv"], b + 1)
                need(dve, s["xT_ps"], b - 1)
                dve.tensor_scalar(xn[:, u, :], xb[:, u, :], stat[:, u, 6:7], stat[:, u, 10:11],
                                  ALU.subtract, ALU.mult).then_inc(s["xn"], 1)

            def attention_inputs(b, u, between):
                q = k.qtab[:, bass.ds(b, 1)].rearrange("p o t d -> p (o t) d")
                dve.wait_ge(s["scaled"], 2 * b + 2)
                dve.tensor_tensor(rest[:, u, :], qs[:, u, :], q[:, 0], ALU.subtract).then_inc(s["qpart"], 1)
                dve.wait_ge(s["squared"], b + 1)
                dve.tensor_reduce(nrm[:, u, 0], sq[:, u], AX, ALU.add).then_inc(s["norm2"], 1)
                if between:
                    one_hot(*between, 1, 1)
                dve.wait_ge(s["root_n"], b + 1)
                dve.tensor_scalar(nrm[:, u, 2], nrm[:, u, 1], 1e-12, None, ALU.max).then_inc(s["clip"], 1)
                dve.wait_ge(s["qpart"], 3 * b + 1)
                dve.tensor_copy(q[:, 1], rest[:, u, :]).then_inc(s["qpart"], 1)
                dve.wait_ge(s["clip"], b + 1)
                dve.reciprocal(nrm[:, u, 3], nrm[:, u, 2]).then_inc(s["recip"], 1)
                dve.wait_ge(s["qpart"], 3 * b + 2)
                dve.tensor_tensor(q[:, 2], rest[:, u, :], q[:, 1], ALU.subtract).then_inc(s["qpart"], 1)
                dve.wait_ge(s["recip"], b + 1)
                dve.scalar_tensor_tensor(nrm[:, u, 4], nrm[:, u, 3], MSCALE, factor, ALU.mult,
                                         ALU.mult).then_inc(s["factor"], 1)
                dve.wait_ge(s["factor"], b + 1)
                fac = nrm[:, u, 4]
                dve.tensor_tensor(qn[:, u], mix[:, u, 0:8], over(fac, (1, 8), (0, MD)),
                                  ALU.mult).then_inc(s["normed"], 1)
                dve.wait_ge(s["normed"], b + 1)
                need(dve, s["qT_ps"], b)
                dve.tensor_copy(parts[:, u, :, 0:32], qn[:, u]).then_inc(s["split"], 1)
                dve.wait_ge(s["split"], 4 * b + 1)
                dve.tensor_tensor(qrest[:, u], qn[:, u], parts[:, u, :, 0:32], ALU.subtract).then_inc(s["split"], 1)
                dve.wait_ge(s["split"], 4 * b + 2)
                dve.tensor_copy(parts[:, u, :, 32:64], qrest[:, u]).then_inc(s["split"], 1)
                dve.wait_ge(s["split"], 4 * b + 3)
                dve.tensor_tensor(parts[:, u, :, 64:96], qrest[:, u], parts[:, u, :, 32:64],
                                  ALU.subtract).then_inc(s["split"], 1)

            dve.memset(factor[:, MH:], 1.0)
            dve.memset(parts[:, :, :, 96:97], 1.0)
            dve.memset(zero, 0.0)
            dve.memset(ones, 1.0).then_inc(s["set"], 1)
            dve.wait_ge(s["set"], 1)
            dve.wait_ge(s["weights"], 48)
            variance(0, 0, between=False)
            for b, u in blocks(dve):
                layer_norm(b, u)
                if isinstance(b, int) and b == NB - 1:
                    one_hot(b, u, 0, 1)
                    one_hot(b, u, 1, 0)
                else:
                    variance(b + 1, 1 - u, between=True)
                if at_start(b, 2):
                    one_hot(b, u, 1, 1)
                else:
                    attention_inputs(b - 2, u, between=(b, u))
            attention_inputs(NB - 2, 1, between=None)
            attention_inputs(NB - 1, 0, between=None)
            dve.wait_ge(s["hist"], 2 * NB)
            dve.tensor_copy(k.start, ps[:, 5, 0:NB])


def phase_kv_sums(nc, k):
    w = Space(k.arena, k.WORK0, k.MT0)
    kext, v1 = w.f32(2, MH, 48), w.f32(2, MH, 33)
    kk = w.f32(2, 4, PAIRS)
    zero = w.f32(512)
    sums = w.f32(4, 640)
    FIRST_D = 12
    ps = k.ps
    with ExitStack() as ctx:
        s = sems(nc, k, "kv", "set k_in0 k_in1 v_in0 v_in1 pairs more_pairs lin used copied turned")
        k_in, v_in = (s["k_in0"], s["k_in1"]), (s["v_in0"], s["v_in1"])
        block = ctx.enter_context(nc.Block())

        @block.sync
        def _(sp):
            for b, u in blocks(sp):
                for made in ("pairs", "more_pairs", "lin"):
                    need(sp, s[made], 2 * b - 2)
                sp.dma_start(kext[:, u].rearrange("p h i -> p (h i)"),
                             k.kext_rows[bass.ds(b * P, P), :]).then_inc(k_in[u], 16)
                need(sp, s["used"], 2 * b - 2)
                sp.dma_start(v1[:, u].rearrange("p h i -> p (h i)"),
                             k.v1_rows[bass.ds(b * P, P), :]).then_inc(v_in[u], 16)

        def pairs(eng, u, half, d0, d1):
            a = kext[:, u, 4 * half:4 * half + 4]
            return eng.tensor_tensor(over(kk[:, half, 0, d0 * MD:], (PAIRS, 4), (MD, d1 - d0), (1, MD)),
                                     over(a, (48, 4), (0, d1 - d0), (1, MD)),
                                     over(a[:, 0, d0:], (48, 4), (1, d1 - d0), (1, MD)), ALU.mult)

        @block.vector
        def _(dve):
            dve.memset(zero, 0.0)
            dve.memset(k.mt, 0.0)
            dve.memset(kk[:, :, :, PAIRS - 1:], 1.0)
            dve.memset(sums, 0.0).then_inc(s["set"], 1)
            for b, u in blocks(dve):
                dve.wait_ge(k_in[u], 8 * (b - u) + 16)
                for half in (0, 1):
                    need(dve, s["used"], 2 * b + half - 1)
                    pairs(dve, u, half, 0, FIRST_D).then_inc(s["pairs"], 1)

        @block.gpsimd
        def _(pool):
            for b, u in blocks(pool):
                pool.wait_ge(k_in[u], 8 * (b - u) + 16)
                for half in (0, 1):
                    need(pool, s["used"], 2 * b + half - 1)
                    pairs(pool, u, half, FIRST_D, ND).then_inc(s["more_pairs"], 1)

        @block.tensor
        def _(pe):
            pe.wait_ge(s["set"], 1)
            for side in (0, 64):
                for bank in range(5):
                    n = 512 if bank < 4 else 4 * 65
                    pe.matmul(ps[side:side + 33, bank, 0:n], zero[:, 0:33], zero[:, 0:n], start=True, stop=False,
                              skip_group_check=True)
            for b, u in blocks(pe):
                pe.wait_ge(v_in[u], 8 * (b - u) + 16)
                for half in (0, 1):
                    pe.wait_ge(s["pairs"], 2 * b + half + 1)
                    pe.wait_ge(s["more_pairs"], 2 * b + half + 1)
                    pe.wait_ge(s["lin"], 2 * b + half + 1)
                    for j in range(4):
                        h = 4 * half + j
                        hp, side = h // 2, 64 * (h % 2)
                        pe.matmul(ps[side:side + 33, hp, :], v1[:, u, h, :], kk[:, half, j, 0:512],
                                  start=False, stop=False, skip_group_check=True)
                        mm = pe.matmul(ps[side:side + 33, 4, 65 * hp:65 * hp + 65], v1[:, u, h, :],
                                       kk[:, half, j, 512:PAIRS], start=False, stop=False,
                                       skip_group_check=True)
                    mm.then_inc(s["used"], 1)
            pe.wait_ge(s["copied"], 1)
            for t in range(20):
                mm = pe.transpose(ps[:, t // 4, (t % 4) * P:(t % 4 + 1) * P],
                                  sums[:, t // 5, (t % 5) * P:(t % 5 + 1) * P], k.ident)
            mm.then_inc(s["turned"], 1)

        @block.scalar
        def _(act):
            for b, u in blocks(act):
                act.wait_ge(k_in[u], 8 * (b - u) + 16)
                for half in (0, 1):
                    need(act, s["used"], 2 * b + half - 1)
                    act.copy(over(kk[:, half, 0, 544:], (PAIRS, 4), (1, MD)),
                             kext[:, u, 4 * half:4 * half + 4, 0:32]).then_inc(s["lin"], 1)
            act.wait_ge(s["used"], 2 * NB)
            for side in (0, 64):
                r = slice(side, side + 33)
                for hp in range(4):
                    act.mul(sums[r, hp, 0:32], ps[r, hp, 0:32], 0.5)
                    act.copy(sums[r, hp, 32:512], ps[r, hp, 32:512])
                    act.mul(sums[r, hp, 512:544], ps[r, 4, 65 * hp:65 * hp + 32], 0.5)
                    act.mul(sums[r, hp, 544:576], ps[r, 4, 65 * hp + 32:65 * hp + 64], MSCALE ** 2)
                    last = act.mul(sums[r, hp, 576:577], ps[r, 4, 65 * hp + 64:65 * hp + 65], MSCALE ** 4)
            last.then_inc(s["copied"], 1)
            act.wait_ge(s["turned"], 1)
            for bank in range(5):
                for side in (0, 1):
                    src = split(ps[:, bank, :], (4, P))[:, :, 64 * side:64 * side + 33]
                    dst = k.mt[:, 4 * bank:4 * bank + 4, side, :]
                    act.copy(dst[:, :, 32 * side:32 * side + 32], src[:, :, 1:33])
                    act.copy(dst[:, :, 64 + 32 * side:96 + 32 * side], src[:, :, 0:1].to_broadcast([P, 4, 32]))


def phase_starts(nc, k):
    w = Space(k.arena, k.WORK0, k.COLS0)
    ones, one_b = w.f32(P), w.bf16(P)
    tot, count, tiles, ends, first = w.f32(NB), w.f32(NB, dt=I32), w.f32(NB), w.f32(NB), w.f32(NB)
    whole = w.f32(NB, dt=I32)
    end_col, after = w.f32(2), w.bf16(CH * STEPS)
    half = CH * STEPS // 2
    ps = k.ps
    with ExitStack() as ctx:
        s = sems(nc, k, "starts", "set sums turned col after blocks d")
        block = ctx.enter_context(nc.Block())

        @block.tensor
        def _(pe):
            pe.wait_ge(s["set"], 1)
            pe.matmul(ps[:, 1, 0:NB], ones, k.start, start=True, stop=True)
            pe.matmul(ps[:, 2, 0:NB], k.cst[:, C_AFTER:C_AFTER + P], k.start, start=True,
                      stop=True).then_inc(s["sums"], 1)
            pe.wait_ge(s["d"], 5)
            pe.transpose(ps[0:NB, 3, 0:P], ends, k.ident).then_inc(s["turned"], 1)
            pe.wait_ge(s["after"], 1)
            for c in range(2):
                mm = pe.matmul(ps[0:1, 4 + c, 0:half], one_b[0:NB, 0:1], after[0:NB, c * half:(c + 1) * half],
                               start=True, stop=True)
            mm.then_inc(s["blocks"], 1)

        @block.vector
        def _(dve):
            done = 0

            def then(ins):
                nonlocal done
                done += 1
                ins.then_inc(s["d"], 1)
                dve.wait_ge(s["d"], done)

            dve.memset(one_b, 1.0)
            dve.memset(ones, 1.0).then_inc(s["set"], 1)
            dve.wait_ge(s["sums"], 1)
            then(dve.tensor_scalar(tot, ps[:, 1, 0:NB], float(P - 1), None, ALU.add))
            then(dve.tensor_copy(count, tot))
            then(dve.tensor_scalar(whole, count, 7, None, ALU.arith_shift_right))
            then(dve.tensor_copy(tiles, whole))
            then(dve.tensor_tensor_scan(ends, ones[:, 0:NB], tiles, 0.0, ALU.mult, ALU.add))
            then(dve.tensor_tensor(first, ends, tiles, ALU.subtract))
            then(dve.scalar_tensor_tensor(k.start, first, float(P), ps[:, 2, 0:NB], ALU.mult, ALU.add))
            dve.wait_ge(s["turned"], 1)
            dve.tensor_copy(end_col[0:NB, 0:1], ps[0:NB, 3, 0:1]).then_inc(s["col"], 1)
            dve.wait_ge(s["col"], 1)
            dve.tensor_scalar(after[0:NB, :], k.cst[0:NB, C_TILE:C_END], end_col[0:NB, 0:1], None,
                              ALU.is_ge).then_inc(s["after"], 1)
            dve.wait_ge(s["blocks"], 1)
            for c in range(2):
                dve.tensor_scalar(k.blocks[0:1, c * half:(c + 1) * half], ps[0:1, 4 + c, 0:half], float(NB - 1),
                                  None, ALU.min)


def phase_mix_scatter(nc, k):
    w = Space(k.arena, k.WORK0, k.MT0)
    wp = w.f32(4, D)
    qT = w.bf16(2, 4, P)
    a_sb = w.f32(2, 2, 4 * P)
    qq = w.f32(2, 5, 4 * P)
    xb, y, yT, xo = w.f32(2, D), w.f32(4, P), w.f32(4, P), w.f32(2, D)
    rn, rn_32 = w.f32(MH), w.f32(MH, 32)
    row_s, row_lo = w.f32(2, 8 * P), w.bf16(2, 8 * P)
    low_T, low, high = w.f32(2, 8, P), w.bf16(2, 8, P), w.bf16(2, 8, NB)
    table = w.f32(2, 8, NB)
    junk_e, junk_g = w.f32(8, P), w.f32(8, NB)
    before, rank, slot = w.f32(2, 8), w.f32(2, 8), w.f32(4, 8, dt=I32)
    rec, minus_p = w.f32(4, 8, REC), w.f32(2)[:, 0:1]
    ps = k.ps
    LAST = 2 * NB - 1
    with ExitStack() as ctx:
        s = sems(nc, k, "mix", "weights passed q_in0 q_in1 x_in0 x_in1 a_ps a4_ps b_ps a_sb a4_sb qq y y_sb den recip "
                 "rn_32 rows yT proj xo out0 out1")
        q_in, x_in, out = (s["q_in0"], s["q_in1"]), (s["x_in0"], s["x_in1"]), (s["out0"], s["out1"])
        e = sems(nc, k, "edges", "passed set rows0 rows1 attr0 attr1 attr2 attr3 hot high fields count table looked "
                 "summed ranked ranks slots apart low_T stored0 stored1 stored2 stored3")
        rows = (e["rows0"], e["rows1"])
        attr = (e["attr0"], e["attr1"], e["attr2"], e["attr3"])
        stored = (e["stored0"], e["stored1"], e["stored2"], e["stored3"])
        block = ctx.enter_context(nc.Block())

        @block.sync
        def _(sp):
            sp.dma_start(wp[0:64], k.proj_w).then_inc(s["weights"], 16)
            sp.wait_ge(e["set"], 1)
            sp.wait_ge(k.rows_stored, 32)
            for b, u in blocks(sp):
                for half in (0, 1):
                    n = 2 * b + half
                    need(sp, e["ranks"], n - 1)
                    need(sp, e["low_T"], n - 1)
                    sp.dma_start(row_s[:, half, :], k.row_s[bass.ds(n * 8 * P, 8 * P)].partition_broadcast(P)
                                 ).then_inc(rows[half], 16)
                    sp.dma_start(row_lo[:, half, :], k.row_lo[bass.ds(n * 8 * P, 8 * P)].partition_broadcast(P)
                                 ).then_inc(rows[half], 16)
                    need(sp, stored[2 * u + half], 64 * (b - u))
                    sp.dma_start(rec[:, 2 * u + half, :, 0:R_ONE], k.attr[:, bass.ds(n * 8, 8), :]
                                 ).then_inc(attr[2 * u + half], 16)
                    need(sp, s["qq"], 5 * n - 5)
                    sp.dma_start(qT[0:97, half],
                                 k.qT_rows[bass.ds(b * 97, 97), 512 * half:512 * half + 512].rearrange(
                                     "p (h n) -> p h n", h=4)).then_inc(q_in[half], 16)
                need(sp, s["xo"], b - 1)
                sp.dma_start(xb[:, u, :], k.x[bass.ds(b * P, P), :]).then_inc(x_in[u], 16)

        @block.gpsimd
        def _(pool):
            def store(b, u):
                pool.wait_ge(s["xo"], b + 1)
                pool.dma_start(k.xm_rows[bass.ds(b * P, P), :], xo[:, u, :]).then_inc(out[u], 16)

            pool.wait_ge(k.blanks_stored, 16 * (SLOTS // (BLANK * P)))
            for b, u in blocks(pool):
                for half in (0, 1):
                    v = 2 * u + half
                    pool.wait_ge(attr[v], 8 * (b - u) + 16)
                    pool.wait_ge(e["fields"], 2 * b + half + 1)
                    pool.wait_ge(e["slots"], 2 * b + half + 1)
                    pool.sem_inc(e["passed"])
                    for j in range(8):
                        pool.indirect_dma_start(out=k.records, out_offset=bass.IndirectOffsetOnAxis(
                            ap=slot[:, v, j:j + 1], axis=0), in_=rec[:, v, j, :], in_offset=None
                        ).then_inc(stored[v], 16)
                if not at_start(b, 2):
                    store(b - 2, u)
            store(NB - 2, 1)
            store(NB - 1, 0)
            for u in (0, 1):
                n = (NB + 1 - u) // 2
                pool.wait_ge(out[u], 16 * n)
                pool.wait_ge(stored[2 * u], 128 * n)
                pool.wait_ge(stored[2 * u + 1], 128 * n)

        @block.tensor
        def _(pe):
            def sum_head(b, half, j):
                n = 2 * b + half
                if j == 0:
                    pe.wait_ge(s["qq"], 5 * n + 5)
                    if half == 0:
                        need(pe, s["y_sb"], b)
                hp, side = (4 * half + j) // 2, j % 2
                for g in range(5):
                    r = slice(0, P) if g < 4 else slice(0, 65)
                    mm = pe.matmul(ps[:, 4, hp * P:(hp + 1) * P], k.mt[r, 5 * hp + g, side, :],
                                   qq[r, half, g, j * P:(j + 1) * P], start=(g == 0 and side == 0),
                                   stop=(g == 4 and side == 1))
                if j == 3:
                    mm.then_inc(s["y"], 1)

            def denominators(b):
                pe.wait_ge(s["y_sb"], b + 1)
                need(pe, s["xo"], b)
                for hp in range(4):
                    mm = pe.matmul(ps[:, 5, 2 * hp:2 * hp + 2], y[64:128, hp, :], over(k.ident[64:128, 64:], (32, 2)),
                                   start=True, stop=True)
                mm.then_inc(s["den"], 1)

            def reciprocals(b):
                pe.wait_ge(s["rn_32"], b + 1)
                pe.sem_inc(s["passed"])
                for hp in range(4):
                    mm = pe.transpose(ps[0:64, 5, hp * P:(hp + 1) * P],
                                      rn_32[:, 2 * hp:2 * hp + 2].rearrange("p h i -> p (h i)"), k.ident)
                mm.then_inc(s["rows"], 1)

            def project(b):
                pe.wait_ge(s["yT"], b + 1)
                for hp in range(4):
                    pe.matmul(ps[:, 5, 0:D], yT[0:64, hp, :], wp[0:64, hp, :], start=(hp == 0), stop=False)
                pe.matmul(ps[:, 5, 0:D], k.ones_b[0:3, :], k.bias3[0:3, 1280:], start=False,
                          stop=True).then_inc(s["proj"], 1)

            def count(n, u, part):
                for j in range(8):
                    c0, m = (j + 1, 7 - j) if part == 0 else (0, j + 1)
                    if m:
                        mm = pe.matmul(ps[:, 6, c0 * NB:(c0 + m) * NB], low[:, u, j, :],
                                       over(high[:, u, j, :], (0, m), (1, NB)), start=False, stop=False,
                                       skip_group_check=True)
                return mm

            def count_own(n, u):
                pe.wait_ge(e["hot"], n + 1)
                count(n, u, 0).then_inc(e["count"], 1)

            def look_up(n, u):
                pe.wait_ge(e["table"], n + 1)
                count(n, u, 1)
                pe.wait_ge(e["low_T"], n + 1)
                need(pe, e["summed"], n)
                for j in range(8):
                    mm = pe.matmul(ps[:, 7, j * NB:(j + 1) * NB], low_T[:, u, j, :], table[:, u, j, :],
                                   start=True, stop=True)
                mm.then_inc(e["looked"], 1)

            pe.matmul(ps[:, 6, 0:8 * NB], k.ident, over(k.start, (0, 8), (1, NB)), start=True, stop=False,
                      skip_group_check=True)
            def first_factors(b, half):
                n = 2 * b + half
                q = qT[0:97, half].rearrange("p h n -> p (h n)")
                pe.wait_ge(q_in[half], 16 * (b + 1))
                need(pe, s["a_sb"], n)
                pe.matmul(ps[:, 0, :], k.sel_b[0:97, 0, :], q, start=True, stop=True).then_inc(s["a_ps"], 1)
                need(pe, s["a4_sb"], n)
                pe.matmul(ps[0:65, 1, :], k.sel_b[0:97, 5, 0:65], q, start=True,
                          stop=True).then_inc(s["a4_ps"], 1)

            pe.wait_ge(s["weights"], 16)
            first_factors(0, 0)
            for b, _ in blocks(pe):
                first = at_start(b, 1)
                for half in (0, 1):
                    n = 2 * b + half
                    q = qT[0:97, half].rearrange("p h n -> p (h n)")
                    for g in range(5):
                        m = 5 * half + g
                        need(pe, s["qq"], 10 * b + m - 1)
                        if g < 4:
                            pe.matmul(ps[:, 2 + m % 2, :], k.sel_b[0:97, 1 + g, :], q, start=True,
                                      stop=True).then_inc(s["b_ps"], 1)
                        else:
                            pe.matmul(ps[0:65, 2 + m % 2, :], k.sel_b[0:97, 6, 0:65], q, start=True,
                                      stop=True).then_inc(s["b_ps"], 1)
                        if g >= 1:
                            if half == 1:
                                sum_head(b, 0, g - 1)
                            elif not first:
                                sum_head(b - 1, 1, g - 1)
                        if g in (0, 2) and not (first and n == 0):
                            (count_own, look_up)[g // 2](n - 1, 1 - half)
                        if g == 3 and not (isinstance(b, int) and n == LAST):
                            first_factors(b + half, 1 - half)
                        if half == 0 and g == 0 and not at_start(b, 2):
                            project(b - 2)
                        if half == 1 and not first and g in (1, 3):
                            (denominators, reciprocals)[g // 2](b - 1)
            for j in range(4):
                sum_head(NB - 1, 1, j)
            count_own(LAST, 1)
            project(NB - 2)
            denominators(NB - 1)
            reciprocals(NB - 1)
            project(NB - 1)
            look_up(LAST, 1)

        @block.scalar
        def _(act):
            def tables(n, u):
                act.wait_ge(e["count"], n + 1)
                need(act, e["looked"], n - 1)
                act.copy(table[:, u], split(ps[:, 6, 0:8 * NB], (8, NB))).then_inc(e["table"], 1)

            def first_factors(n, half):
                act.wait_ge(s["a_ps"], n + 1)
                need(act, s["qq"], 5 * n - 5)
                act.copy(a_sb[:, half, 0], ps[:, 0, :]).then_inc(s["a_sb"], 1)
                act.wait_ge(s["a4_ps"], n + 1)
                act.copy(a_sb[0:65, half, 1], ps[0:65, 1, :]).then_inc(s["a4_sb"], 1)

            def keep_sums(b):
                act.wait_ge(s["y"], 2 * b + 2)
                need(act, s["yT"], b)
                act.copy(y, split(ps[:, 4, :], (4, P))).then_inc(s["y_sb"], 1)

            def columns(b, u):
                n = 2 * b + u
                act.wait_ge(rows[u], 32 * (b + 1))
                need(act, e["looked"], n - 1)
                lo = low_T[:, u].rearrange("p j e -> p (j e)")
                act.activation(lo, row_lo[:, u, :], ACT.Abs, bias=minus_p).then_inc(e["apart"], 1)
                act.wait_ge(e["apart"], n + 1)
                act.activation(lo, lo, ACT.Relu, bias=1.0, scale=-1.0).then_inc(e["low_T"], 1)

            act.wait_ge(e["set"], 1)
            first_factors(0, 0)
            for b, u in blocks(act):
                for half in (0, 1):
                    n = 2 * b + half
                    if not at_start(n, 1):
                        tables(n - 1, 1 - half)
                    if not (isinstance(b, int) and n == LAST):
                        first_factors(n + 1, 1 - half)
                    if half == 0 and not at_start(b, 1):
                        keep_sums(b - 1)
                    columns(b, half)
                    v = 2 * u + half
                    need(act, stored[v], 64 * (b - u))
                    act.copy(rec[:, v, :, R_T:R_LO + 1].rearrange("p e f -> p f e"),
                             k.cols[:, 0:3, bass.ds(n * 8, 8)]).then_inc(e["fields"], 1)
            keep_sums(NB - 1)
            tables(LAST, 1)

        @block.vector
        def _(dve):
            def invert(b):
                dve.wait_ge(s["den"], b + 1)
                dve.reciprocal(rn, ps[:, 5, 0:MH]).then_inc(s["recip"], 1)
                dve.wait_ge(s["recip"], b + 1)
                need(dve, s["rows"], b)
                dve.tensor_copy(rn_32, split(rn, (MH, 1)).to_broadcast([P, MH, 32])).then_inc(s["rn_32"], 1)

            def normalise(b):
                dve.wait_ge(s["rows"], b + 1)
                need(dve, s["proj"], b)
                dve.tensor_tensor(yT[0:64], split(ps[0:64, 5, :], (4, P)), y[0:64], ALU.mult).then_inc(s["yT"], 1)

            def add(b, u):
                dve.wait_ge(s["proj"], b + 1)
                dve.wait_ge(x_in[u], 8 * (b - u) + 16)
                if not at_start(b, 2):
                    dve.wait_ge(out[u], 8 * (b - u))
                dve.tensor_tensor(xo[:, u, :], ps[:, 5, 0:D], xb[:, u, :], ALU.add).then_inc(s["xo"], 1)

            def one_hot(b, u, part):
                n = 2 * b + u
                if part == 0:
                    dve.wait_ge(rows[u], 32 * (b + 1))
                if part == 1:
                    need(dve, e["looked"], n - 1)
                    need(dve, e["slots"], n - 1)
                    one_hot_high(k, dve, high[:, u], n)
                    one_hot_low(k, dve, low[:, u], n).then_inc(e["hot"], 1)
                if part >= 2:
                    for j in range(4 * part - 8, 4 * part - 4):
                        last = dve.scalar_tensor_tensor(junk_e[:, j, :], row_s[:, u, j * P:(j + 1) * P],
                                                        k.cols[:, 1, bass.ds(n * 8 + j, 1)],
                                                        k.cst[:, C_BEFORE:C_BEFORE + P], ALU.is_equal, ALU.mult,
                                                        accum_out=before[:, u, j:j + 1])
                if part == 3:
                    last.then_inc(e["ranks"], 1)

            def slots(n, u, v, b):
                dve.wait_ge(e["looked"], n + 1)
                dve.tensor_tensor(junk_g, split(ps[:, 7, 0:8 * NB], (8, NB)), high[:, u], ALU.mult
                                  ).then_inc(e["summed"], 1)
                dve.wait_ge(e["summed"], n + 1)
                dve.tensor_reduce(rank[:, u, :], junk_g, AX, ALU.add).then_inc(e["ranked"], 1)
                dve.wait_ge(e["ranked"], n + 1)
                need(dve, stored[v], 64 * (b - v // 2))
                dve.tensor_tensor(slot[:, v, :], before[:, u, :], rank[:, u, :], ALU.add).then_inc(e["slots"], 1)

            dve.tensor_scalar(minus_p, k.cst[:, C_P:C_P + 1], -1.0, None, ALU.mult)
            dve.memset(rec, 0.0).then_inc(e["high"], 1)
            dve.wait_ge(e["high"], 1)
            dve.memset(rec[:, :, :, R_ONE:R_ONE + 1], 1.0).then_inc(e["set"], 1)
            for b, u in blocks(dve):
                start = at_start(b, 1)
                for half in (0, 1):
                    n = 2 * b + half
                    dve.wait_ge(s["a_sb"], n + 1)
                    dve.wait_ge(s["a4_sb"], n + 1)
                    need(dve, s["y"], n - 1)
                    for g in range(5):
                        m = 5 * half + g
                        r = slice(0, P) if g < 4 else slice(0, 65)
                        dve.wait_ge(s["b_ps"], 10 * b + m + 1)
                        dve.tensor_tensor(qq[r, half, g], ps[r, 2 + m % 2, :], a_sb[r, half, int(g == 4)],
                                          ALU.mult).then_inc(s["qq"], 1)
                        if g in (2, 4) and half == 1 and not start:
                            (invert, normalise)[g // 2 - 1](b - 1)
                        if g == 1 and half == 0 and not at_start(b, 2):
                            add(b - 2, u)
                        if g < 4:
                            one_hot(b, half, g)
                        elif half == 1:
                            slots(n - 1, 0, 2 * u, b)
                        elif not start:
                            slots(n - 1, 1, 3 - 2 * u, b - 1)
            add(NB - 2, 1)
            invert(NB - 1)
            normalise(NB - 1)
            slots(LAST, 1, 1, NB - 1)
            add(NB - 1, 0)


def records_of(k, g):
    return k.records.rearrange("(c g e) f -> g e c f", c=CH, g=STEPS)[bass.ds(g, 1)].rearrange(
        "o e c f -> (o e) c f")


def blocks_of(nc, k, g, engine):
    return nc.values_load_multi_w_load_instructions(
        k.blocks[0:1, bass.ds(g * CH, CH)], engines=[engine], min_val=0, max_val=NB - 1,
        skip_runtime_bounds_check_because="phase_starts keeps them at most NB - 1")[1]


def phase_compat(nc, k):
    w = Space(k.arena, k.WORK0, k.BIG1)
    rec, kg = w.f32(4, CH, REC), w.f32(4, CH, P)
    t_int = w.f32(4, CH, dt=I32)
    hot, hot_T = w.bf16(2, CH, P), w.bf16(2, CH, P)
    rec_T = w.f32(2, 2, P)
    ks, prod = w.f32(2, 4, P), w.f32(2, 4, P)
    score, node = w.f32(4, CH, GH), w.f32(4, CH, GH)
    wr = w.f32(4, 2 * P)
    ps = k.ps
    with ExitStack() as ctx:
        s = sems(nc, k, "compat", "passed weights r_in0 r_in1 r_in2 r_in3 t k_in0 k_in1 k_in2 k_in3 hot hot_ps hot_T "
                 "rec_ps rec_T qk ks prod score node turned stored")
        r_in = (s["r_in0"], s["r_in1"], s["r_in2"], s["r_in3"])
        k_in = (s["k_in0"], s["k_in1"], s["k_in2"], s["k_in3"])
        block = ctx.enter_context(nc.Block())

        @block.sync
        def _(sp):
            sp.dma_start(wr, k.rpe_w).then_inc(s["weights"], 16)
            for g, v in fours(sp, STEPS):
                need(sp, s["rec_ps"], g - 3)
                need(sp, s["hot"], g - 3)
                need(sp, s["node"], g - 3)
                sp.dma_start(rec[:, v], records_of(k, g)).then_inc(r_in[v], 16)

        @block.gpsimd
        def _(pool):
            for g, v in fours(pool, STEPS):
                pool.wait_ge(s["t"], g + 1)
                need(pool, s["ks"], 2 * g - 6)
                pool.sem_inc(s["passed"])
                for c in range(CH):
                    pool.indirect_dma_start(out=kg[:, v, c, :], out_offset=None, in_=k.k_rows,
                                            in_offset=bass.IndirectOffsetOnAxis(ap=t_int[:, v, c:c + 1], axis=0)
                                            ).then_inc(k_in[v], 16)

        @block.tensor
        def _(pe):
            def products(g, v):
                u = v % 2
                blk = blocks_of(nc, k, g, ENG.PE)
                pe.wait_ge(s["rec_T"], g + 1)
                pe.wait_ge(s["hot_T"], g + 1)
                for half in (0, 1):
                    need(pe, s["prod"], 2 * g + half - 1)
                    for j in range(4):
                        c = 4 * half + j
                        bank, at = 2 + 2 * half + j // 2, (j % 2) * 2 * P
                        pe.matmul(ps[:, bank, at:at + 2 * P], rec_T[:, u, half, :], wr[:, j, :], start=True,
                                  stop=False, skip_group_check=True)
                        for part in range(3):
                            q = k.qtab[:, bass.ds(blk[c], 1), part, :].rearrange("p o d -> p (o d)")
                            mm = pe.matmul(ps[:, bank, at:at + P], hot_T[:, u, c, :], q, start=False,
                                           stop=(part == 2), skip_group_check=True)
                    mm.then_inc(s["qk"], 1)

            def turn(g, v):
                pe.wait_ge(s["score"], 2 * g + 2)
                pe.wait_ge(s["node"], g + 1)
                need(pe, s["stored"], g)
                pe.transpose(ps[:, 6, 0:P], score[:, v].rearrange("p c h -> p (c h)"), k.ident)
                pe.transpose(ps[:, 6, P:2 * P], node[:, v].rearrange("p c h -> p (c h)"),
                             k.ident).then_inc(s["turned"], 1)

            pe.wait_ge(s["weights"], 16)
            for g, v in fours(pe, STEPS):
                pe.wait_ge(r_in[v], 4 * (g - v) + 16)
                need(pe, s["rec_T"], g)
                for half in (0, 1):
                    mm = pe.transpose(ps[:, 1, half * P:(half + 1) * P],
                                      rec[:, v, 4 * half:4 * half + 4].rearrange("p c f -> p (c f)"), k.ident)
                mm.then_inc(s["rec_ps"], 1)
                pe.wait_ge(s["hot"], g + 1)
                need(pe, s["hot_T"], g)
                for c in range(CH):
                    mm = pe.transpose(k.ps_b[:, 0, c * P:(c + 1) * P], hot[:, v % 2, c, :], k.ident_b)
                mm.then_inc(s["hot_ps"], 1)
                if not at_start(g, 1):
                    products(g - 1, (v - 1) % 4)
                if not at_start(g, 3):
                    turn(g - 3, (v - 3) % 4)
            products(STEPS - 1, 3)
            for g in (STEPS - 3, STEPS - 2, STEPS - 1):
                turn(g, g % 4)

        @block.scalar
        def _(act):
            def store(g):
                act.wait_ge(s["turned"], g + 1)
                act.copy(k.scores[:, bass.ds(g * P, P)], ps[:, 6, 0:P])
                act.copy(k.owner[:, bass.ds(g * P, P)], ps[:, 6, P:2 * P]).then_inc(s["stored"], 1)

            for g, v in fours(act, STEPS):
                act.wait_ge(s["rec_ps"], g + 1)
                need(act, s["qk"], 2 * g - 2)
                act.copy(rec_T[:, v % 2], split(ps[:, 1, 0:2 * P], (2, P))).then_inc(s["rec_T"], 1)
                act.wait_ge(s["hot_ps"], g + 1)
                act.copy(hot_T[:, v % 2], split(k.ps_b[:, 0, :], (CH, P))).then_inc(s["hot_T"], 1)
                act.wait_ge(r_in[v], 4 * (g - v) + 16)
                need(act, s["turned"], g - 3)
                act.copy(node[:, v], over(rec[:, v, 0, R_S:], (REC, CH), (0, GH))).then_inc(s["node"], 1)
                if not at_start(g, 3):
                    store(g - 3)
            for g in (STEPS - 3, STEPS - 2, STEPS - 1):
                store(g)

        @block.vector
        def _(dve):
            def scores(g, v):
                dve.wait_ge(k_in[v], 32 * (g - v) + 128)
                for half in (0, 1):
                    qk = ps[:, 2 + 2 * half:4 + 2 * half, :].rearrange("p b (j w) -> p b j w", j=2)
                    n = 2 * g + half
                    sum_, product = (t[:, half].rearrange("p (b j) w -> p b j w", b=2) for t in (ks, prod))
                    dve.wait_ge(s["qk"], n + 1)
                    need(dve, s["prod"], n - 1)
                    dve.tensor_tensor(sum_, qk[:, :, :, P:2 * P],
                                      kg[:, v, 4 * half:4 * half + 4, :].rearrange("p (b j) w -> p b j w", b=2),
                                      ALU.add).then_inc(s["ks"], 1)
                    dve.wait_ge(s["ks"], n + 1)
                    need(dve, s["score"], n - 1)
                    dve.tensor_tensor(product, qk[:, :, :, 0:P], sum_, ALU.mult).then_inc(s["prod"], 1)
                need(dve, s["turned"], g - 2)
                for half in (0, 1):
                    dve.wait_ge(s["prod"], 2 * g + half + 1)
                    dve.tensor_reduce(score[:, v, 4 * half:4 * half + 4].rearrange("p c h -> p (c h)"),
                                      prod[:, half].rearrange("p c (h d) -> p (c h) d", d=GD), AX,
                                      ALU.add).then_inc(s["score"], 1)

            for g, v in fours(dve, STEPS):
                dve.wait_ge(r_in[v], 4 * (g - v) + 16)
                need(dve, k_in[v], 32 * (g - v))
                dve.tensor_copy(t_int[:, v, :], over(rec[:, v, 0, R_T:], (REC, CH))).then_inc(s["t"], 1)
                need(dve, s["hot_ps"], g - 1)
                for c in range(CH):
                    last = dve.tensor_scalar(hot[:, v % 2, c, :], k.iota_b, rec[:, v, c, R_LO:R_LO + 1], None,
                                             ALU.is_equal)
                last.then_inc(s["hot"], 1)
                if not at_start(g, 2):
                    scores(g - 2, (v - 2) % 4)
            scores(STEPS - 2, 2)
            scores(STEPS - 1, 3)


def message_rows(nc, k):
    w = Space(k.arena, 0, k.WORK0)
    rec, vg, t_int = w.f32(4, CH, REC), w.f32(4, CH, D), w.f32(4, CH, dt=I32)
    return rec, vg, t_int, sems(nc, k, "fetch", "r_in0 r_in1 r_in2 r_in3 t v_in0 v_in1 v_in2 v_in3")


def phase_seg_max(nc, k):
    L = STEPS * P
    H, T = L // 2, L - 32 * P
    w = Space(k.arena, k.WORK0, k.FL0)
    ends, row, carry, col = w.f32(4), w.f32(4, CH, GH), w.f32(6, CH, GH), w.f32(2)
    breaks = k.breaks
    ps = k.ps
    k.msg_rec, k.msg_v, k.msg_t, k.fetch = message_rows(nc, k)
    rec, vg, t_int, f = k.msg_rec, k.msg_v, k.msg_t, k.fetch
    with ExitStack() as ctx:
        s = sems(nc, k, "segmax", "d ends turned carry back last_third upper_half subtracted")
        block = ctx.enter_context(nc.Block())

        @block.sync
        def _(sp):
            for g in range(4):
                sp.dma_start(rec[:, g], records_of(k, g)).then_inc(f[f"r_in{g}"], 16)

        @block.gpsimd
        def _(pool):
            pool.tensor_tensor(breaks[:, T:L], k.owner[:, T:L], k.owner[:, T - 1:L - 1], ALU.subtract
                               ).then_inc(s["last_third"], 1)
            for g in range(4):
                pool.wait_ge(f["t"], g + 1)
                for c in range(CH):
                    pool.indirect_dma_start(out=vg[:, g, c, :], out_offset=None, in_=k.v_rows,
                                            in_offset=bass.IndirectOffsetOnAxis(ap=t_int[:, g, c:c + 1], axis=0)
                                            ).then_inc(f[f"v_in{g}"], 16)
            pool.wait_ge(s["upper_half"], 1)
            pool.tensor_tensor(k.scores[:, H:], k.scores[:, H:], k.owner[:, H:], ALU.subtract
                               ).then_inc(s["subtracted"], 1)
            pool.wait_ge(s["subtracted"], 1)

        @block.tensor
        def _(pe):
            pe.wait_ge(s["ends"], 1)
            for n in range(4):
                mm = pe.transpose(ps[0:1, 0, n * P:(n + 1) * P], ends[:, n:n + 1], k.ident)
            mm.then_inc(s["turned"], 1)
            pe.wait_ge(s["carry"], 1)
            for n in range(2):
                mm = pe.matmul(ps[:, 1, n:n + 1], carry[0:1, n].rearrange("p c h -> p (c h)"),
                               k.ident[0:1, 0:1], start=True, stop=True)
            mm.then_inc(s["back"], 1)

        @block.vector
        def _(dve):
            done = 0

            def then(ins):
                nonlocal done
                done += 1
                ins.then_inc(s["d"], 1)
                dve.wait_ge(s["d"], done)

            back = lambda ap: over(ap[:, L - 1:L], (-1, L))
            for g in range(4):
                dve.wait_ge(f[f"r_in{g}"], 16)
                dve.tensor_copy(t_int[:, g, :], over(rec[:, g, 0, R_T:], (REC, CH))).then_inc(f["t"], 1)
            dve.memset(breaks[:, 0:1], 0.0)
            then(dve.memset(breaks[:, L:L + 2], 0.0))
            then(dve.tensor_tensor(breaks[:, 1:T], k.owner[:, 1:T], k.owner[:, 0:T - 1], ALU.not_equal))
            dve.wait_ge(s["last_third"], 1)
            then(dve.tensor_scalar(breaks[:, 1:L], breaks[:, 1:L], 0.0, NEG, ALU.not_equal, ALU.mult))
            dve.tensor_copy(ends[:, 0:1], k.owner[:, 0:1])
            then(dve.tensor_copy(ends[:, 1:2], k.owner[:, L - 1:L]))
            then(dve.tensor_tensor_scan(k.owner, breaks[:, 0:L], k.scores, NEG, ALU.add, ALU.max))
            then(dve.tensor_copy(ends[:, 2:3], k.owner[:, L - 1:L]))
            then(dve.tensor_tensor_scan(back(k.owner), back(breaks[:, 1:L + 1]), back(k.scores), NEG, ALU.add,
                                        ALU.max))
            dve.tensor_copy(ends[:, 3:4], k.owner[:, 0:1]).then_inc(s["ends"], 1)
            dve.wait_ge(s["turned"], 1)
            then(dve.tensor_copy(row[0:1], split(ps[0:1, 0, :], (4, CH, GH))))
            first, last, fwd, bwd = (row[0:1, n] for n in range(4))
            from_left, from_right, apart, many, both = (carry[0:1, n] for n in range(5))
            then(dve.memset(carry[0:1], NEG))
            dve.tensor_tensor(apart[:, 1:CH], first[:, 1:CH], last[:, 0:CH - 1], ALU.not_equal)
            then(dve.tensor_tensor(many, first, last, ALU.not_equal))
            dve.tensor_scalar(apart[:, 1:CH], apart[:, 1:CH], NEG, None, ALU.mult)
            then(dve.tensor_scalar(many, many, NEG, None, ALU.mult))
            for c in range(1, CH):
                then(dve.tensor_tensor(both[:, c], from_left[:, c - 1], many[:, c - 1], ALU.add))
                then(dve.tensor_tensor(both[:, c], both[:, c], fwd[:, c - 1], ALU.max))
                then(dve.tensor_tensor(from_left[:, c], both[:, c], apart[:, c], ALU.add))
            for c in range(CH - 2, -1, -1):
                then(dve.tensor_tensor(both[:, c], from_right[:, c + 1], many[:, c + 1], ALU.add))
                then(dve.tensor_tensor(both[:, c], both[:, c], bwd[:, c + 1], ALU.max))
                then(dve.tensor_tensor(from_right[:, c], both[:, c], apart[:, c + 1], ALU.add))
            dve.nop().then_inc(s["carry"], 1)
            dve.wait_ge(s["back"], 1)
            then(dve.tensor_copy(col, ps[:, 1, 0:2]))
            then(dve.tensor_tensor_scan(k.owner, breaks[:, 0:L], k.scores, col[:, 0:1], ALU.add, ALU.max))
            span = lambda ap, a, b: over(ap[:, b - 1:b], (-1, b - a))
            dve.tensor_tensor_scan(span(k.owner, H, L), span(breaks, H + 1, L + 1), span(k.owner, H, L),
                                   col[:, 1:2], ALU.add, ALU.max).then_inc(s["upper_half"], 1)
            dve.wait_ge(s["upper_half"], 1)
            then(dve.tensor_tensor_scan(span(k.owner, 0, H), span(breaks, 1, H + 1), span(k.owner, 0, H),
                                        k.owner[:, H:H + 1], ALU.add, ALU.max))
            then(dve.tensor_tensor(k.scores[:, 0:H], k.scores[:, 0:H], k.owner[:, 0:H], ALU.subtract))


def phase_messages(nc, k):
    w = Space(k.arena, k.WORK0, k.BIG1)
    rec, vg, t_int, f = k.msg_rec, k.msg_v, k.msg_t, k.fetch
    HB = NB // 2
    ex, msg, hot = w.f32(2, P), w.f32(2, CH, D + GH), w.f32(4, CH, P)
    ps = k.ps
    with ExitStack() as ctx:
        s = sems(nc, k, "msg", "passed cleared ex ex_ps weight hot msg sums acc")
        r_in = (f["r_in0"], f["r_in1"], f["r_in2"], f["r_in3"])
        v_in = (f["v_in0"], f["v_in1"], f["v_in2"], f["v_in3"])
        block = ctx.enter_context(nc.Block())

        @block.sync
        def _(sp):
            for g, v in fours(sp, STEPS):
                if at_start(g, 4):
                    continue
                sp.wait_ge(s["hot"], g - 3)
                sp.dma_start(rec[:, v], records_of(k, g)).then_inc(r_in[v], 16)

        @block.gpsimd
        def _(pool):
            pool.memset(k.acc[:, HB:], 0.0).then_inc(s["cleared"], 1)
            for g, v in fours(pool, STEPS):
                if at_start(g, 4):
                    continue
                pool.wait_ge(f["t"], g + 1)
                pool.wait_ge(s["msg"], 8 * g - 24)
                pool.sem_inc(s["passed"])
                for c in range(CH):
                    pool.indirect_dma_start(out=vg[:, v, c, :], out_offset=None, in_=k.v_rows,
                                            in_offset=bass.IndirectOffsetOnAxis(ap=t_int[:, v, c:c + 1], axis=0)
                                            ).then_inc(v_in[v], 16)

        @block.scalar
        def _(act):
            def weigh(g, v):
                act.wait_ge(s["ex_ps"], g + 1)
                need(act, s["sums"], 8 * g - 8)
                act.copy(msg[:, v % 2, :, D:], split(ps[:, v % 2, 0:P], (CH, GH))).then_inc(s["weight"], 1)

            for g, v in fours(act, STEPS):
                need(act, s["ex_ps"], g - 1)
                act.activation(ex[:, v % 2, :], k.scores[:, bass.ds(g * P, P)], ACT.Exp).then_inc(s["ex"], 1)
                if not at_start(g, 1):
                    weigh(g - 1, (v - 1) % 4)
            weigh(STEPS - 1, 3)

        @block.tensor
        def _(pe):
            def sums(g, v):
                pe.wait_ge(s["hot"], g + 1)
                for c in range(CH):
                    n = 8 * g + c
                    pe.wait_ge(s["msg"], n + 1)
                    need(pe, s["acc"], n - 3)
                    pe.matmul(ps[:, 2 + c % 4, 0:D + GH], hot[:, v, c, :], msg[:, v % 2, c, :], start=True,
                              stop=True).then_inc(s["sums"], 1)

            for g, v in fours(pe, STEPS):
                pe.wait_ge(s["ex"], g + 1)
                need(pe, s["weight"], g - 1)
                pe.transpose(ps[:, v % 2, 0:P], ex[:, v % 2, :], k.ident).then_inc(s["ex_ps"], 1)
                if not at_start(g, 2):
                    sums(g - 2, (v - 2) % 4)
            sums(STEPS - 2, 2)
            sums(STEPS - 1, 3)

        @block.vector
        def _(dve):
            def add(g, c, blk):
                n = 8 * g + c
                acc = k.acc[:, bass.ds(blk[c], 1), :].rearrange("p o w -> p (o w)")
                dve.wait_ge(s["sums"], n + 1)
                need(dve, s["acc"], n)
                dve.tensor_tensor(acc, ps[:, 2 + c % 4, 0:D + GH], acc, ALU.add).then_inc(s["acc"], 1)

            def messages(g, v, c):
                if c == 0:
                    dve.wait_ge(v_in[v], 32 * (g - v) + 128)
                    dve.wait_ge(s["weight"], g + 1)
                dve.tensor_tensor(split(msg[:, v % 2, c, 0:D], (GH, 16)), split(vg[:, v, c], (GH, 16)),
                                  over(msg[:, v % 2, c, D:], (1, GH), (0, 16)), ALU.mult).then_inc(s["msg"], 1)

            def both(g, v):
                blk = None if at_start(g, 1) else blocks_of(nc, k, g - 1, ENG.DVE)
                for c in range(CH):
                    if blk:
                        add(g - 1, c, blk)
                    if not (isinstance(g, int) and g == STEPS):
                        messages(g, v, c)

            dve.memset(k.acc[:, 0:HB], 0.0).then_inc(s["cleared"], 1)
            for g, v in fours(dve, STEPS):
                dve.wait_ge(r_in[v], 4 * (g - v) + 16)
                if not at_start(g, 4):
                    dve.wait_ge(v_in[v], 32 * (g - v))
                    dve.tensor_copy(t_int[:, v, :], over(rec[:, v, 0, R_T:], (REC, CH))).then_inc(f["t"], 1)
                dve.tensor_tensor(hot[:, v], over(k.iota_b, (0, CH), (1, P)),
                                  over(rec[:, v, 0, R_LO:], (REC, CH), (0, P)), ALU.is_equal).then_inc(s["hot"], 1)
                if at_start(g, 3) and g == 2:
                    dve.wait_ge(s["cleared"], 2)
                if not at_start(g, 2):
                    both(g - 2, (v - 2) % 4)
            for g in (STEPS - 2, STEPS - 1, STEPS):
                both(g, g % 4)


def phase_norm2(nc, k):
    w = Space(k.arena, k.WORK0, k.BIG2)
    CN, ROUNDS = CB * P, NB // CB
    wr, bias, ones = w.f32(2, NE), w.f32(NE), w.f32(CN // 2)
    xm, x1, xn, xT = w.f32(2, CB, D), w.f32(2, CB, D), w.f32(2, CB, D), w.f32(2, 2, CN)
    den, inv_den, g1 = w.f32(NB, GH), w.f32(NB, GH), w.f32(CB, D)
    stats, mean, stat = w.f32(2, CB, 6), w.f32(2, CB, 2), w.f32(2, 3, CB)
    ps = k.ps
    with ExitStack() as ctx:
        s = sems(nc, k, "norm2", "passed weights set x_in0 x_in1 den inv_den g1 x1 stats mean var root inv xn xT_ps xT "
                 "logit_ps logit out0 out1 t_out0 t_out1")
        x_in, out, t_out = (s["x_in0"], s["x_in1"]), (s["out0"], s["out1"]), (s["t_out0"], s["t_out1"])
        block = ctx.enter_context(nc.Block())
        rows = lambda ap, r: ap[bass.ds(r * CN, CN), :].rearrange("(n p) d -> p n d", p=P)

        @block.sync
        def _(sp):
            sp.dma_start(wr, k.route_w).then_inc(s["weights"], 16)
            sp.dma_start(bias[0:1, :], k.route_bias).then_inc(s["weights"], 16)
            for r, u in twos(sp, ROUNDS):
                need(sp, s["x1"], r - 1)
                sp.dma_start(xm[:, u], rows(k.xm_rows, r)).then_inc(x_in[u], 16)

        @block.gpsimd
        def _(pool):
            for r, u in twos(pool, ROUNDS):
                pool.wait_ge(s["x1"], r + 1)
                pool.dma_start(rows(k.x1_rows, r), x1[:, u]).then_inc(out[u], 16)
                pool.wait_ge(s["xT"], 4 * r + 4)
                pool.dma_start(k.x2T.rearrange("(c p) n -> p c n", p=P)[:, :, bass.ds(r * CN, CN)], xT[:, u]
                               ).then_inc(t_out[u], 16)
            for u in (0, 1):
                pool.wait_ge(out[u], 16 * ((ROUNDS + 1 - u) // 2))
                pool.wait_ge(t_out[u], 16 * ((ROUNDS + 1 - u) // 2))

        @block.tensor
        def _(pe):
            def logits(r, u):
                pe.wait_ge(s["xT"], 4 * r + 4)
                need(pe, s["logit"], r)
                for half in (0, 1):
                    n = slice(half * CN // 2, (half + 1) * CN // 2)
                    for c in range(2):
                        pe.matmul(ps[0:NE, 4 + half, 0:CN // 2], wr[:, c, :], xT[:, u, c, n], start=(c == 0),
                                  stop=False)
                    mm = pe.matmul(ps[0:NE, 4 + half, 0:CN // 2], bias[0:1, :], ones[0:1, :], start=False, stop=True)
                mm.then_inc(s["logit_ps"], 1)

            pe.wait_ge(s["weights"], 32)
            pe.wait_ge(s["set"], 1)
            for r, u in twos(pe, ROUNDS):
                for bank in range(4):
                    need(pe, s["xT"], 4 * r + bank - 3)
                    for nb in range(2 * bank, min(2 * bank + 2, CB)):
                        pe.wait_ge(s["xn"], CB * r + nb + 1)
                        for c in range(2):
                            at = (2 * c + nb % 2) * P
                            mm = pe.transpose(ps[:, bank, at:at + P], xn[:, u, nb, c * P:(c + 1) * P], k.ident)
                    mm.then_inc(s["xT_ps"], 1)
                if not at_start(r, 1):
                    logits(r - 1, 1 - u)
            logits(ROUNDS - 1, 0)

        @block.scalar
        def _(act):
            def root(r, u):
                act.wait_ge(s["var"], r + 1)
                act.activation(stat[:, u, 1], stat[:, u, 0], ACT.Sqrt).then_inc(s["root"], 1)

            def logits(r, u):
                act.wait_ge(s["logit_ps"], r + 1)
                act.copy(split(k.logit_T[0:NE, bass.ds(r * CN, CN)], (2, CN // 2)), ps[0:NE, 4:6, 0:CN // 2]
                         ).then_inc(s["logit"], 1)

            for r, u in twos(act, ROUNDS):
                root(r, u)
                need(act, s["logit_ps"], r - 1)
                need(act, t_out[u], 8 * (r - u))
                for bank in range(4):
                    m = min(2, CB - 2 * bank)
                    act.wait_ge(s["xT_ps"], 4 * r + bank + 1)
                    act.copy(xT[:, u, :, 2 * bank * P:(2 * bank + m) * P],
                             split(ps[:, bank, :], (2, 2 * P))[:, :, 0:m * P]).then_inc(s["xT"], 1)
                if not at_start(r, 1):
                    logits(r - 1, 1 - u)
            logits(ROUNDS - 1, 0)

        @block.vector
        def _(dve):
            def residual(r, u):
                acc = k.acc[:, bass.ds(r * CB, CB), 0:D].rearrange("p n (h d) -> p n h d", d=16)
                inv = inv_den[:, bass.ds(r * CB, CB), :].rearrange("p n (h o) -> p n h o", o=1)
                need(dve, s["x1"], r)
                dve.tensor_tensor(g1.rearrange("p n (h d) -> p n h d", d=16), acc, inv.to_broadcast([P, CB, GH, 16]),
                                  ALU.mult).then_inc(s["g1"], 1)
                dve.wait_ge(s["g1"], r + 1)
                dve.wait_ge(x_in[u], 8 * (r - u) + 16)
                need(dve, out[u], 8 * (r - u))
                dve.tensor_tensor(x1[:, u], g1, xm[:, u], ALU.add).then_inc(s["x1"], 1)
                dve.wait_ge(s["x1"], r + 1)
                for nb in range(CB):
                    last = dve.bn_stats(stats[:, u, nb], x1[:, u, nb])
                last.then_inc(s["stats"], 1)
                dve.wait_ge(s["stats"], r + 1)
                dve.sem_inc(s["passed"])
                for nb in range(CB):
                    last = dve.bn_aggr(mean[:, u, nb], stats[:, u, nb])
                last.then_inc(s["mean"], 1)
                dve.wait_ge(s["mean"], r + 1)
                dve.tensor_scalar(stat[:, u, 0], mean[:, u, :, 1], 1e-5, None, ALU.add).then_inc(s["var"], 1)

            def normalise(r, u):
                dve.wait_ge(s["root"], r + 1)
                dve.reciprocal(stat[:, u, 2], stat[:, u, 1]).then_inc(s["inv"], 1)
                dve.wait_ge(s["inv"], r + 1)
                need(dve, s["xT_ps"], 4 * r - 4)
                for nb in range(CB):
                    dve.tensor_scalar(xn[:, u, nb], x1[:, u, nb], mean[:, u, nb, 0:1], stat[:, u, 2, nb:nb + 1],
                                      ALU.subtract, ALU.mult).then_inc(s["xn"], 1)

            dve.memset(ones, 1.0).then_inc(s["set"], 1)
            dve.tensor_scalar(den, k.acc[:, :, D:], 1e-16, None, ALU.add).then_inc(s["den"], 1)
            dve.wait_ge(s["den"], 1)
            dve.reciprocal(inv_den, den).then_inc(s["inv_den"], 1)
            dve.wait_ge(s["inv_den"], 1)
            for r, u in twos(dve, ROUNDS):
                residual(r, u)
                if not at_start(r, 1):
                    normalise(r - 1, 1 - u)
            normalise(ROUNDS - 1, 0)


def phase_route(nc, k):
    w = Space(k.arena, k.WORK0, k.BIG2)
    top, ssum, sinv = w.f32(NB), w.f32(NB), w.f32(NB)
    low = w.f32(NB, NE)
    v = [w.f32(16) for _ in range(8)]
    ps = k.ps
    with ExitStack() as ctx:
        s = sems(nc, k, "route", "stored turned low ex d turn_w wT bn root bn_in")
        block = ctx.enter_context(nc.Block())

        @block.sync
        def _(sp):
            for n, src in enumerate(k.bn):
                sp.dma_start(k.bn_sb[:, n, :], src).then_inc(s["bn_in"], 16)
            sp.wait_ge(s["wT"], (NB + 3) // 4)
            sp.dma_start(k.gate_rows, k.logit_T[0:NE, :]).then_inc(s["stored"], 16)
            sp.wait_ge(s["stored"], 16)

        @block.tensor
        def _(pe):
            for b in range(NB):
                mm = pe.transpose(ps[:, 0, b * NE:(b + 1) * NE], k.logit_T[0:NE, b * P:(b + 1) * P],
                                  k.ident[0:NE, 0:NE])
            mm.then_inc(s["turned"], 1)
            pe.wait_ge(s["d"], 4)
            for b in range(NB):
                n = b // 4
                if n >= 2 and b % 4 == 0:
                    pe.wait_ge(s["wT"], n - 1)
                mm = pe.transpose(ps[0:NE, 1 + n % 2, (b % 4) * P:(b % 4 + 1) * P], k.gate[:, b, :], k.ident)
                if b % 4 == 3 or b == NB - 1:
                    mm.then_inc(s["turn_w"], 1)

        @block.scalar
        def _(act):
            act.wait_ge(s["low"], 1)
            act.activation(low, low, ACT.Exp).then_inc(s["ex"], 1)
            act.wait_ge(s["bn"], 2)
            act.activation(v[0], v[1], ACT.Sqrt)
            act.activation(v[2], v[3], ACT.Sqrt).then_inc(s["root"], 1)
            for n in range((NB + 3) // 4):
                m = min(4, NB - 4 * n) * P
                act.wait_ge(s["turn_w"], n + 1)
                act.copy(k.logit_T[0:NE, 4 * n * P:4 * n * P + m], ps[0:NE, 1 + n % 2, 0:m]).then_inc(s["wT"], 1)

        @block.vector
        def _(dve):
            done = 0

            def then(ins):
                nonlocal done
                done += 1
                ins.then_inc(s["d"], 1)
                dve.wait_ge(s["d"], done)

            logit = split(ps[:, 0, 0:NB * NE], (NB, NE))
            dve.wait_ge(s["turned"], 1)
            then(dve.tensor_reduce(top, logit, AX, ALU.max))
            dve.tensor_tensor(low, logit, over(top, (1, NB), (0, NE)), ALU.subtract).then_inc(s["low"], 1)
            dve.wait_ge(s["ex"], 1)
            then(dve.tensor_reduce(ssum, low, AX, ALU.add))
            then(dve.reciprocal(sinv, ssum))
            then(dve.tensor_tensor(k.gate, low, over(sinv, (1, NB), (0, NE)), ALU.mult))
            dve.wait_ge(s["bn_in"], 16 * 10)
            for layer in (0, 1):
                dve.tensor_scalar(v[1 + 2 * layer], k.bn_sb[:, 5 * layer + 4, :], 1e-3, None,
                                  ALU.add).then_inc(s["bn"], 1)
            dve.wait_ge(s["root"], 1)
            for layer in (0, 1):
                bias, gain, shift, mean, _var = (k.bn_sb[:, 5 * layer + n, :] for n in range(5))
                then(dve.reciprocal(v[4], v[2 * layer]))
                then(dve.tensor_tensor(k.scale[:, layer, :], gain, v[4], ALU.mult))
                then(dve.tensor_tensor(v[5], bias, mean, ALU.subtract))
                then(dve.tensor_tensor(v[6], v[5], k.scale[:, layer, :], ALU.mult))
                then(dve.tensor_tensor(k.shift[:, layer, :], v[6], shift, ALU.add))


def phase_experts(nc, k):
    CN = CB * P
    front = Space(k.unused, 0, k.unused.shape[1])
    y, x1, bo = front.f32(CB, D), front.f32(CB, D), front.f32(D)
    HALF = CN // 2
    ps = k.ps
    ROUNDS = NB // CB
    short_words, words = 6 * NE * 2 * D + 12 * CN, 5 * CN + 12 * D
    with ExitStack() as ctx:
        short = Space(ctx.enter_context(nc.sbuf_tensor("short_forms", [P, short_words], F32R)), 0, short_words)
        w_hi, w_lo = short.f32(3, NE, 2, D), short.f32(3, NE, 2, D)
        x_hi, x_lo, h_hi, h_lo = short.f32(2, CN), short.f32(2, CN), short.f32(2, 2, CN), short.f32(2, 2, CN)
        whole = Space(ctx.enter_context(nc.sbuf_tensor("expert_words", [P, words], F32)), 0, words)
        h, x_whole, gate_T, w_whole = whole.f32(2, CN), whole.f32(2, CN), whole.f32(CN), whole.f32(2, 3, 2, D)
        s = sems(nc, k, "experts", "w_in0 w_in1 gate x1_in x_in bias_in w_hi w_lo x_hi x_lo h_ps h h_hi h_lo seed_ps "
                 "seed y_ps y out")
        w_in = (s["w_in0"], s["w_in1"])
        block = ctx.enter_context(nc.Block())

        @block.sync
        def _(sp):
            def store(r):
                sp.wait_ge(s["y"], NE * CB * (r + 1))
                sp.dma_start(k.out[bass.ds(r * CN, CN), :].rearrange("(n p) d -> p n d", p=P), y).then_inc(s["out"], 16)

            def weights(e):
                need(sp, s["w_lo"], e - 1)
                for n, src in enumerate((k.w1, k.w2, k.w3)):
                    sp.dma_start(w_whole[:, e % 2, n], src[:, e]).then_inc(w_in[e % 2], 16)

            weights(0)
            for r in rounds(sp, ROUNDS):
                need(sp, s["x_lo"], 2 * r)
                sp.dma_start(x_whole, k.x2T.rearrange("(c p) n -> p c n", p=P)[:, :, bass.ds(r * CN, CN)]
                             ).then_inc(s["x_in"], 16)
                if at_start(r, 1):
                    weights(1)
                    sp.dma_start(bo[0:NE, :], k.out_bias).then_inc(s["bias_in"], 16)
                need(sp, s["seed_ps"], CB * r)
                sp.dma_start(gate_T[0:NE, :], k.gate_rows[:, bass.ds(r * CN, CN)]).then_inc(s["gate"], 16)
                need(sp, s["seed"], CB * r)
                sp.dma_start(x1, k.x1_rows[bass.ds(r * CN, CN), :].rearrange("(n p) d -> p n d", p=P)
                             ).then_inc(s["x1_in"], 16)
                if at_start(r, 1):
                    for e in range(2, NE):
                        weights(e)
                else:
                    store(r - 1)
            store(ROUNDS - 1)
            sp.wait_ge(s["out"], 16 * ROUNDS)

        @block.tensor
        def _(pe):
            def three_passes(out, hi, lo, moving_hi, moving_lo):
                passes = [(hi, moving_hi), (hi, moving_lo), (lo, moving_hi)]
                for c in (0, 1):
                    for n, (a, b) in enumerate(passes):
                        mm = pe.matmul(out, a(c), b(c), start=(c == 0 and n == 0),
                                       stop=(c == 1 and n == 2))
                return mm

            def hidden(r, e, layer):
                for ot in (0, 1):
                    m = 4 * e + 2 * layer + ot
                    need(pe, s["h"], 4 * NE * r + m - 1)
                    for half in (0, 1):
                        n = slice(half * HALF, (half + 1) * HALF)
                        unit = slice(ot * P, (ot + 1) * P)
                        hi, lo = (x_hi, x_lo) if layer == 0 else (h_hi[:, 0], h_lo[:, 0])
                        mm = three_passes(ps[:, 2 * (m % 2) + half, 0:HALF],
                                          lambda c: w_hi[:, layer, e, c, unit], lambda c: w_lo[:, layer, e, c, unit],
                                          lambda c: hi[:, c, n], lambda c: lo[:, c, n])
                    mm.then_inc(s["h_ps"], 1)

            def last(r, e):
                pe.wait_ge(s["h_lo"], 4 * NE * r + 4 * e + 4)
                for nb in range(CB):
                    need(pe, s["y"], CB * NE * r + CB * e + nb - 3)
                    n = slice(nb * P, (nb + 1) * P)
                    three_passes(ps[:, 4 + (CB * e + nb) % 4, 0:D],
                                 lambda c: h_hi[:, 1, c, n], lambda c: h_lo[:, 1, c, n],
                                 lambda c: w_hi[:, 2, e, c, :], lambda c: w_lo[:, 2, e, c, :]
                                 ).then_inc(s["y_ps"], 1)

            def seeds(r):
                need(pe, s["y"], NE * CB * r)
                if at_start(r, 1):
                    pe.wait_ge(s["bias_in"], 16)
                pe.wait_ge(s["gate"], 16 * (r + 1))
                for nb in range(CB):
                    need(pe, s["seed"], CB * r + nb - 3)
                    pe.matmul(ps[:, 4 + nb % 4, 0:D], gate_T[0:NE, nb * P:(nb + 1) * P], bo[0:NE, :],
                              start=True, stop=True).then_inc(s["seed_ps"], 1)
                pe.wait_ge(s["seed"], CB * r + CB)

            for r in rounds(pe, ROUNDS):
                first = isinstance(r, int)
                pe.wait_ge(s["x_lo"], 2 * r + 2)
                for e in range(NE):
                    if first:
                        pe.wait_ge(s["w_lo"], e + 1)
                    hidden(r, e, 0)
                    if e >= 1:
                        last(r, e - 1)
                    elif not first:
                        last(r - 1, NE - 1)
                    pe.wait_ge(s["h_lo"], 4 * NE * r + 4 * e + 2)
                    hidden(r, e, 1)
                    if e == 0:
                        seeds(r)
            last(ROUNDS - 1, NE - 1)

        @block.scalar
        def _(act):
            for r in rounds(act, ROUNDS):
                for e in range(NE):
                    for layer in (0, 1):
                        for ot in (0, 1):
                            m = 4 * e + 2 * layer + ot
                            act.wait_ge(s["h_ps"], 4 * NE * r + m + 1)
                            need(act, s["h_lo"], 4 * NE * r + m - 1)
                            act.activation(split(h[:, m % 2], (2, HALF)),
                                           ps[:, 2 * (m % 2):2 * (m % 2) + 2, 0:HALF], ACT.Relu,
                                           bias=k.shift[:, layer, 2 * e + ot:2 * e + ot + 1],
                                           scale=k.scale[:, layer, 2 * e + ot:2 * e + ot + 1]).then_inc(s["h"], 1)

        @block.vector
        def _(dve):
            def upper(out, value):
                return dve.tensor_copy(out, value)

            def lower(out, value, upper_part):
                return dve.tensor_tensor(out, value, upper_part.bitcast(F32), ALU.subtract)

            def weights(e):
                dve.wait_ge(w_in[e % 2], 48 * (e // 2 + 1))
                upper(w_hi[:, :, e], w_whole[:, e % 2]).then_inc(s["w_hi"], 1)
                dve.wait_ge(s["w_hi"], e + 1)
                lower(w_lo[:, :, e], w_whole[:, e % 2], w_hi[:, :, e]).then_inc(s["w_lo"], 1)

            def inputs(r, c):
                dve.wait_ge(s["x_in"], 16 * (r + 1))
                need(dve, s["h_ps"], 4 * NE * r - 2)
                upper(x_hi[:, c], x_whole[:, c]).then_inc(s["x_hi"], 1)
                dve.wait_ge(s["x_hi"], 2 * r + c + 1)
                lower(x_lo[:, c], x_whole[:, c], x_hi[:, c]).then_inc(s["x_lo"], 1)

            def parts(r, e, layer, ot):
                m = 4 * e + 2 * layer + ot
                dve.wait_ge(s["h"], 4 * NE * r + m + 1)
                upper(h_hi[:, layer, ot], h[:, m % 2]).then_inc(s["h_hi"], 1)
                dve.wait_ge(s["h_hi"], 4 * NE * r + m + 1)
                lower(h_lo[:, layer, ot], h[:, m % 2], h_hi[:, layer, ot]).then_inc(s["h_lo"], 1)

            def add(r, e, blocks):
                for nb in blocks:
                    n = CB * NE * r + CB * e + nb
                    dve.wait_ge(s["y_ps"], n + 1)
                    need(dve, s["y"], n - CB + 1)
                    gate = k.gate[:, bass.ds(r * CB + nb, 1), e:e + 1].rearrange("p a b -> p (a b)")
                    dve.scalar_tensor_tensor(y[:, nb, :], ps[:, 4 + (CB * e + nb) % 4, 0:D], gate, y[:, nb, :],
                                             ALU.mult, ALU.add).then_inc(s["y"], 1)

            def seeds(r):
                dve.wait_ge(s["x1_in"], 16 * (r + 1))
                need(dve, s["out"], 16 * r)
                for nb in range(CB):
                    dve.wait_ge(s["seed_ps"], CB * r + nb + 1)
                    dve.tensor_tensor(y[:, nb, :], ps[:, 4 + nb % 4, 0:D], x1[:, nb, :], ALU.add
                                      ).then_inc(s["seed"], 1)
                dve.wait_ge(s["seed"], CB * r + CB)

            weights(0)
            inputs(0, 0)
            inputs(0, 1)
            for r in inner_rounds(dve, ROUNDS):
                first = isinstance(r, int)
                for e in range(NE):
                    before = (r, e - 1) if e else None if at_start(r, 1) else (r - 1, NE - 1)
                    if at_start(r, 1) and e + 1 < NE:
                        weights(e + 1)
                    parts(r, e, 0, 0)
                    if before:
                        add(*before, [0])
                    parts(r, e, 0, 1)
                    more = e == NE - 1 and not (first and r == ROUNDS - 1)
                    if before:
                        add(*before, range(1, 4))
                    if more:
                        inputs(r + 1, 0)
                    if before:
                        add(*before, range(4, CB))
                    if more:
                        inputs(r + 1, 1)
                    parts(r, e, 1, 0)
                    parts(r, e, 1, 1)
                    if e == 0:
                        seeds(r)
            add(ROUNDS - 1, NE - 1, range(CB))


def free_semaphores(nc, k):
    nc.clear_and_free_semaphores(k.sems)
    nc.all_engine_barrier()
    k.sems = []


def build(nc, x, src_lin, src_col, dst_col, attr, consts, gnn_w, mix_w, node_bias, temperature, proj_w, proj_bias,
          rpe_w, route_w, route_bias, w1, w2, w3, out_bias, bn, out, upto=99, probes=None):
    k = Shared()
    k.x, k.src_lin, k.src_col, k.dst_col, k.attr = x, src_lin, src_col, dst_col, attr
    k.consts, k.gnn_w, k.mix_w, k.node_bias, k.temperature = consts, gnn_w, mix_w, node_bias, temperature
    k.proj_w, k.proj_bias, k.rpe_w, k.route_w, k.route_bias = proj_w, proj_bias, rpe_w, route_w, route_bias
    k.w1, k.w2, k.w3, k.out_bias, k.bn = w1, w2, w3, out_bias, bn
    k.out = out
    scratch = lambda n, shape, dt=F32: nc.dram_tensor(n, shape, dt).ap()
    k.row_s, k.row_lo = scratch("row_s", [EP]), scratch("row_lo", [EP], BF16)
    k.records = scratch("records", [SLOTS, REC])
    k.k_rows, k.v_rows = scratch("k_rows", [NP, P]), scratch("v_rows", [NP, D])
    k.kext_rows, k.v1_rows = scratch("kext_rows", [NP, MH * 48]), scratch("v1_rows", [NP, MH * 33])
    k.qT_rows = scratch("qT_rows", [NB * 97, MH * P], BF16)
    k.xm_rows, k.x1_rows, k.x2T = scratch("xm_rows", [NP, D]), scratch("x1_rows", [NP, D]), scratch("x2T", [D, NP])
    k.gate_rows = scratch("gate_rows", [NE, NP])
    with ExitStack() as ctx:
        q_words, breaks_words, score_words, acc_words = NB * 3 * P // 2, STEPS * P // 2 + 16, STEPS * P, NB * (D + GH)
        front = C_END + C_END % 2 + (9 * P + 5 * D + D + P) // 2 + NB + CH * STEPS + NB * NE + 14 * 16
        total = SBUF_WORDS - front
        constant_words = ctx.enter_context(nc.sbuf_tensor("constant_words", [P, front], F32))
        k.sems = []
        c = Space(constant_words, 0, front)
        k.cst = c.f32(C_END + C_END % 2)[:, 0:C_END]
        k.ident_b, k.iota_b, k.sel_b = c.bf16(P), c.bf16(P), c.bf16(7, P)
        k.bias3, k.ones_b = c.bf16(1280 + D), c.bf16(P)
        k.start, k.blocks = c.f32(NB), c.f32(CH * STEPS, dt=I32)
        k.unused = split(constant_words[:, C_ID + P:c.at], (c.at - C_ID - P,))
        k.gate, k.scale, k.shift, k.bn_sb = c.f32(NB, NE), c.f32(2, 16), c.f32(2, 16), c.f32(10, 16)
        k.ident = k.cst[:, C_ID:C_ID + P]
        k.WORK0 = q_words
        k.BIG2 = total - acc_words
        k.BIG1 = k.BIG2 - score_words
        k.FL0 = k.BIG1 - breaks_words
        k.COLS0 = total - 4 * ET
        k.MT0 = k.COLS0 - 40 * P
        psum = ctx.enter_context(nc.psum_tensor("banks", [P, 8, 512], F32))
        k.ps = psum[:, :, :]
        k.ps_b = psum[:, :, :].rearrange("p b w -> p (b w)").bitcast(BF16).rearrange("p (b w) -> p b w", b=8)
        phases = [phase_setup, phase_nodes, phase_kv_sums, phase_starts,
                  phase_mix_scatter, phase_compat, phase_seg_max, phase_messages, phase_norm2, phase_route]
        with nc.sbuf_tensor("arena", [P, total], F32) as arena:
            k.arena = arena
            at = lambda a, b: Space(arena, a, b)
            k.qtab = at(0, k.WORK0).bf16(NB, 3, P)
            k.cols = at(k.COLS0, total).f32(4, ET)
            k.mt = at(k.MT0, k.COLS0).f32(20, 2, P)
            k.breaks = at(k.FL0, k.BIG1).bf16(STEPS * P + 2)
            k.scores = at(k.BIG1, k.BIG2).f32(STEPS * P)
            k.owner = at(k.BIG2, total).f32(STEPS * P)
            k.acc = at(k.BIG2, total).f32(NB, D + GH)
            k.logit_T = at(0, k.WORK0).f32(NP)
            for n, phase in enumerate(phases[:upto]):
                phase(nc, k)
                if phase is phase_mix_scatter:
                    free_semaphores(nc, k)
        if upto > len(phases):
            phase_experts(nc, k)
        free_semaphores(nc, k)
        if probes:
            probes(nc, k)


def layout(inputs):
    a = {n: np.asarray(v) for n, v in inputs.items()}
    f = np.float32
    pad_rows = lambda v, n, fill=0: np.concatenate([v, np.full((n - v.shape[0],) + v.shape[1:], fill, v.dtype)])
    src = pad_rows(a["src"], EP, FAKE)
    dst = pad_rows(a["dst"], EP)
    attr = pad_rows(a["edge_attr_18"], EP)
    tiles = lambda v: np.ascontiguousarray(v.reshape(ET, P, *v.shape[1:]).swapaxes(0, 1))
    inner = lambda wt: np.ascontiguousarray(wt.reshape(2, P, -1).swapaxes(0, 1))
    experts = lambda wt: np.ascontiguousarray(wt.reshape(NE, 2, P, D).transpose(2, 0, 1, 3))
    units = lambda v: np.ascontiguousarray(v.reshape(NE, 2, P).transpose(2, 0, 1).reshape(P, 2 * NE))
    row = lambda v: np.ascontiguousarray(v.reshape(1, -1))
    one = np.concatenate([np.concatenate([a["L0_gnn_Wq_rpe"], a["L0_gnn_Wk_rpe"]], 1),
                          np.concatenate([row(a["L0_gnn_bq_rpe"]), row(a["L0_gnn_bk_rpe"])], 1),
                          np.zeros((REC - 19, 2 * P), f)])
    rpe = np.zeros((4, REC, 4, 2 * P), f)
    for j in range(4):
        rpe[j, :, j] = one
    r = {
        "x": pad_rows(a["x"], NP), "src_lin": src.reshape(P, ET), "src_col": tiles(src), "dst_col": tiles(dst),
        "attr": tiles(attr), "consts": constants(),
        "gnn_w": inner(a["L0_gnn_Wqkv"]), "mix_w": inner(a["L0_mix_Wqkv"].T),
        "node_bias": np.concatenate([row(a["L0_gnn_bqkv"]), row(a["L0_mix_bqkv"])], 1),
        "temperature": row(a["L0_mix_temperature"]),
        "proj_w": np.ascontiguousarray(a["L0_mix_Wproj"].T.reshape(4, 64, D).swapaxes(0, 1)),
        "proj_bias": row(a["L0_mix_bproj"]),
        "rpe_w": rpe.reshape(P, 4, 2 * P),
        "route_w": inner(a["L0_ffn_Wr"]), "route_bias": row(a["L0_ffn_br"]),
        "w1": experts(a["L0_ffn_W1"]), "w2": experts(a["L0_ffn_W2"]), "w3": experts(a["L0_ffn_Wo"]),
        "out_bias": a["L0_ffn_bo"],
    }
    for layer in ("1", "2"):
        for n in ("b", "g", "be", "m", "v"):
            r[f"bn_{n}{layer}"] = units(a[f"L0_ffn_{n}{layer}"])
    return {n: np.ascontiguousarray(v) for n, v in r.items()}


def kernel(**inputs):
    import concourse.bacc as bacc
    from concourse.bass_utils import run_bass_kernel_spmd

    arrays = layout(inputs)
    nc = bacc.Bacc("TRN2", target_bir_lowering=False, num_devices=1)
    args = {n: nc.dram_tensor(f"in_{n}", v.shape, mybir.dt.from_np(v.dtype), kind="ExternalInput").ap()
            for n, v in arrays.items()}
    out = nc.dram_tensor("out", [NP, D], F32, kind="ExternalOutput").ap()
    bn = [args.pop(n) for n in list(args) if n.startswith("bn_")]
    build(nc, **args, bn=bn, out=out)
    result = run_bass_kernel_spmd(nc, [{f"in_{n}": v for n, v in arrays.items()}], core_ids=[0])
    return result.results[0]["out"][:N]
```
